# Optimizing a Trainium2 kernel written in Bass

```python
import numpy as np
import jax
import jax.numpy as jnp

def _softmax(x, axis=-1):
    return jax.nn.softmax(x, axis=axis)

def _gelu(x):
    return jax.nn.gelu(x, approximate=True)

def _silu(x):
    return jax.nn.silu(x)

def _sigmoid(x):
    return jax.nn.sigmoid(x)

def _layernorm(x, axis=-1, eps=1e-05):
    m = jnp.mean(x, axis=axis, keepdims=True)
    v = jnp.var(x, axis=axis, keepdims=True)
    return (x - m) / jnp.sqrt(v + eps)

def _scatter_add(tgt, idx, src, axis=0):
    return tgt.at[idx].add(src)

def _segment_sum(src, seg, n):
    return jax.ops.segment_sum(src, seg, n)
kernel_name = 'mk_flamingo_gated_d4_seqx_r8_51a64d'

def setup_inputs(seed: int=0):
    np.random.seed(seed)
    _w = jnp.asarray

    def _rec_inputs():
        import jax
        import jax.numpy as jnp
        _rk = jax.random.key(seed)
        x = -0.0005207 + 1.001 * jax.random.normal(jax.random.fold_in(_rk, 1), (4, 256, 128), jnp.float32)
        _lenS = 256 - jax.random.randint(jax.random.fold_in(_rk, 7), (4,), 0, max(1, 256 // 4) + 1, jnp.int32)
        _lenS2 = 64 - jax.random.randint(jax.random.fold_in(_rk, 8), (4,), 0, max(1, 64 // 4) + 1, jnp.int32)
        _ctx_1024P = jax.random.normal(jax.random.fold_in(_rk, 11), (4, 16, 128), jnp.float32)
        _ctx_1024c = jax.random.dirichlet(jax.random.fold_in(_rk, 511), 0.3 * jnp.ones((16,), jnp.float32), (4, 64))
        _ctx_1024t = jnp.einsum('bsk,bkd->bsd', _ctx_1024c, _ctx_1024P)
        _ctx_1024t = _ctx_1024t * jax.lax.rsqrt(jnp.mean(jnp.square(_ctx_1024t)) + 1e-12) * 0.953939
        ctx_1024 = -1.39393e-06 + 0.999914 * (_ctx_1024t + 0.3 * jax.random.normal(jax.random.fold_in(_rk, 611), (4, 64, 128), jnp.float32))
        itok_BxS_0_1023 = jax.random.randint(jax.random.fold_in(_rk, 12), (4, 256), 0, 128, jnp.int32)
        itok_BxS2_0_2047 = jax.random.randint(jax.random.fold_in(_rk, 13), (4, 64), 0, 256, jnp.int32)
        _validS = jnp.arange(256)[None, :] < _lenS[:, None]
        _validS2 = jnp.arange(64)[None, :] < _lenS2[:, None]
        _causal = jnp.tril(jnp.ones((256, 256), dtype=bool))
        mask_1x1xSxS2_bf1 = jnp.ones((1, 1, 256, 64), dtype=bool)
        _g = jax.random.normal(jax.random.fold_in(_rk, 9001), (2, 4), jnp.float32)
        _g = jnp.sign(_g) * jnp.maximum(jnp.abs(_g), 1.0) + (_g == 0) * 1.0
        g_xattn = _g[0]
        g_ffn = _g[1]
        return (x, ctx_1024, itok_BxS_0_1023, itok_BxS2_0_2047, mask_1x1xSxS2_bf1, g_xattn, g_ffn)
    x, ctx_1024, itok_BxS_0_1023, itok_BxS2_0_2047, mask_1x1xSxS2_bf1, g_xattn, g_ffn = _rec_inputs()

    def _L0_xattn_setup():
        import jax, jax.numpy as jnp
        import numpy as np
        DIM = 128
        H = 16
        HD = DIM // H
        SCALE = HD ** (-0.5)
        LAMBDA_INIT = 0.1
        EPS = 1e-06

        def _split_heads(x, B, N):
            return x.reshape(B, N, H, HD).transpose(0, 2, 1, 3)
        key0 = jax.random.key(seed)
        ks = jax.random.split(key0, 12)
        B, Nq, Nk = (2, 128, 256)
        w = 0.02
        inp = {'query': jax.random.normal(ks[0], (B, Nq, DIM), jnp.float32), 'key': jax.random.normal(ks[1], (B, Nk, DIM), jnp.float32), 'value': jax.random.normal(ks[2], (B, Nk, DIM), jnp.float32), 'qpos': jax.random.randint(ks[3], (B, Nq), 0, Nq, jnp.int32), 'kpos': jax.random.randint(ks[4], (B, Nk), 0, Nk, jnp.int32), 'q1_w': jax.random.normal(ks[5], (DIM, DIM), jnp.float32) * w, 'q2_w': jax.random.normal(ks[6], (DIM, DIM), jnp.float32) * w, 'kv1_w': jax.random.normal(ks[7], (2 * DIM, DIM), jnp.float32) * w, 'kv2_w': jax.random.normal(ks[8], (2 * DIM, DIM), jnp.float32) * w, 'proj_w': jax.random.normal(ks[9], (DIM, DIM), jnp.float32) * w, 'proj_b': jnp.zeros((DIM,), jnp.float32), 'norm_w': jnp.ones((DIM,), jnp.float32), 'lambda_1': jnp.ones((1, H, 1, 1), jnp.float32), 'lambda_2': jnp.full((1, H, 1, 1), 1.0 - LAMBDA_INIT * (1.0 / 12.0), jnp.float32)}
        return inp
    _L0_xattn_all = _L0_xattn_setup()
    _L0_xattn_in = {k: v for k, v in _L0_xattn_all.items() if k in ('q1_w', 'q2_w', 'kv1_w', 'kv2_w', 'proj_w', 'proj_b', 'norm_w', 'lambda_1', 'lambda_2')}
    del _L0_xattn_all

    def _L0_ffn_setup():
        import jax, jax.numpy as jnp
        import numpy as np
        B, S, D, F, E, NS, K = (2, 128, 128, 512, 8, 8, 2)
        FS = F // NS
        key = jax.random.key(seed)
        ks = jax.random.split(key, 8)
        scale = 0.02
        return {'hidden_states': jax.random.normal(ks[0], (B, S, D), jnp.float32), 'gate_W': jax.random.normal(ks[1], (E, D), jnp.float32) * scale, 'w1_e': jax.random.normal(ks[2], (E, D, F), jnp.float32) * scale, 'w3_e': jax.random.normal(ks[3], (E, D, F), jnp.float32) * scale, 'w2_e': jax.random.normal(ks[4], (E, F, D), jnp.float32) * scale, 'w1_s': jax.random.normal(ks[5], (NS, D, FS), jnp.float32) * scale, 'w3_s': jax.random.normal(ks[6], (NS, D, FS), jnp.float32) * scale, 'w2_s': jax.random.normal(ks[7], (NS, FS, D), jnp.float32) * scale}
    _L0_ffn_all = _L0_ffn_setup()
    _L0_ffn_in = {k: v for k, v in _L0_ffn_all.items() if k in ('gate_W', 'w1_e', 'w3_e', 'w2_e', 'w1_s', 'w3_s', 'w2_s')}
    del _L0_ffn_all

    def _L1_xattn_setup():
        import jax, jax.numpy as jnp
        import numpy as np
        D_MODEL = 128
        SCALE = 1.0 / np.sqrt(D_MODEL).astype(np.float32)
        key = jax.random.key(seed)
        ks = jax.random.split(key, 7)
        B, S, D, DK = (4, 512, D_MODEL, 64)
        return {'query': jax.random.normal(ks[0], (B, S, D), dtype=jnp.float32), 'key': jax.random.normal(ks[1], (B, S, D), dtype=jnp.float32), 'value': jax.random.normal(ks[2], (B, S, D), dtype=jnp.float32), 'Wq': jax.random.normal(ks[3], (D, DK), dtype=jnp.float32) * (1.0 / np.sqrt(D).astype(np.float32)), 'bq': jax.random.normal(ks[4], (DK,), dtype=jnp.float32) * 0.01, 'Wo': jax.random.normal(ks[5], (DK, D), dtype=jnp.float32) * (1.0 / np.sqrt(DK).astype(np.float32)), 'bo': jax.random.normal(ks[6], (D,), dtype=jnp.float32) * 0.01}
    _L1_xattn_all = _L1_xattn_setup()
    _L1_xattn_in = {k: v for k, v in _L1_xattn_all.items() if k in ('Wq', 'bq', 'Wo', 'bo')}
    del _L1_xattn_all

    def _L1_ffn_setup():
        import jax, jax.numpy as jnp
        import numpy as np
        EPS = 1e-06
        LN_EPS = 1e-05

        def _absmean_core(W):
            gamma = jnp.mean(jnp.abs(W)) + EPS
            Ws = W / gamma
            Wq = jnp.sign(Ws) * jnp.minimum(jnp.round(jnp.abs(Ws)), 1.0)
            return (Wq, gamma)

        @jax.custom_vjp
        def absmean(W):
            return _absmean_core(W)[0]

        def _absmean_fwd(W):
            Wq, gamma = _absmean_core(W)
            return (Wq, gamma)

        def _absmean_bwd(gamma, g):
            return (g / gamma,)
        absmean.defvjp(_absmean_fwd, _absmean_bwd)

        def layernorm(x, w, b, eps=LN_EPS):
            mu = jnp.mean(x, axis=-1, keepdims=True)
            var = jnp.mean((x - mu) ** 2, axis=-1, keepdims=True)
            return (x - mu) * jax.lax.rsqrt(var + eps) * w + b
        key = jax.random.key(seed)
        k1, k2, k3 = jax.random.split(key, 3)
        d, h = (128, 512)
        B, T = (8, 256)
        return {'x': jax.random.normal(k1, (B, T, d), jnp.float32), 'W_fc': jax.random.normal(k2, (h, d), jnp.float32), 'ln_w': jnp.ones((h,), jnp.float32), 'ln_b': jnp.zeros((h,), jnp.float32), 'W_proj': jax.random.normal(k3, (d, h), jnp.float32)}
    _L1_ffn_all = _L1_ffn_setup()
    _L1_ffn_in = {k: v for k, v in _L1_ffn_all.items() if k in ('W_fc', 'ln_w', 'ln_b', 'W_proj')}
    del _L1_ffn_all

    def _L2_xattn_setup():
        import jax, jax.numpy as jnp
        import numpy as np
        B, SQ, SKV, D = (8, 256, 256, 128)
        key = jax.random.key(seed)
        ks = jax.random.split(key, 8)
        s = 1.0 / np.sqrt(D)
        return {'target': jax.random.normal(ks[0], (B, SQ, D), dtype=jnp.float32), 'non_target': jax.random.normal(ks[1], (B, SKV, D), dtype=jnp.float32), 'Wq': jax.random.uniform(ks[2], (D, D), jnp.float32, -s, s), 'bq': jax.random.uniform(ks[3], (D,), jnp.float32, -s, s), 'Wk': jax.random.uniform(ks[4], (D, D), jnp.float32, -s, s), 'bk': jax.random.uniform(ks[5], (D,), jnp.float32, -s, s), 'Wv': jax.random.uniform(ks[6], (D, D), jnp.float32, -s, s), 'bv': jax.random.uniform(ks[7], (D,), jnp.float32, -s, s)}
    _L2_xattn_all = _L2_xattn_setup()
    _L2_xattn_in = {k: v for k, v in _L2_xattn_all.items() if k in ('Wq', 'bq', 'Wk', 'bk', 'Wv', 'bv')}
    del _L2_xattn_all

    def _L2_ffn_setup():
        import jax, jax.numpy as jnp
        import numpy as np
        E = 8
        K = 2
        TEMP = 1.0
        D = 128
        H = 4 * D
        B, T = (2, 256)
        key = jax.random.key(seed)
        ks = jax.random.split(key, 5)
        x = jax.random.normal(ks[0], (B, T, D), jnp.float32)
        gate_w = jax.random.normal(ks[1], (D, E), jnp.float32) * 0.02
        gate_b = jnp.zeros((E,), jnp.float32)
        w1 = jax.random.normal(ks[2], (E, D, H), jnp.float32) * 0.02
        b1 = jnp.zeros((E, H), jnp.float32)
        w2 = jax.random.normal(ks[3], (E, H, D), jnp.float32) * 0.02
        b2 = jnp.zeros((E, D), jnp.float32)
        return {'x': x, 'gate_w': gate_w, 'gate_b': gate_b, 'w1': w1, 'b1': b1, 'w2': w2, 'b2': b2}
    _L2_ffn_all = _L2_ffn_setup()
    _L2_ffn_in = {k: v for k, v in _L2_ffn_all.items() if k in ('gate_w', 'gate_b', 'w1', 'b1', 'w2', 'b2')}
    del _L2_ffn_all

    def _L3_xattn_setup():
        import jax, jax.numpy as jnp
        import numpy as np
        D_MODEL = 128
        H = 16
        D_K = D_MODEL // H
        B, S = (2, 256)

        def _split_heads(x):
            b, s, _ = x.shape
            return x.reshape(b, s, H, D_K).transpose(0, 2, 1, 3)
        key = jax.random.key(seed)
        ks = jax.random.split(key, 11)
        sc = 1.0 / np.sqrt(D_MODEL)
        inp = {'q': jax.random.normal(ks[0], (B, S, D_MODEL), jnp.float32), 'k': jax.random.normal(ks[1], (B, S, D_MODEL), jnp.float32), 'v': jax.random.normal(ks[2], (B, S, D_MODEL), jnp.float32), 'mask': jnp.ones((1, 1, S, S), dtype=bool), 'wq_w': jax.random.normal(ks[3], (D_MODEL, D_MODEL), jnp.float32) * sc, 'wq_b': jnp.zeros((D_MODEL,), jnp.float32), 'wk_w': jax.random.normal(ks[4], (D_MODEL, D_MODEL), jnp.float32) * sc, 'wk_b': jnp.zeros((D_MODEL,), jnp.float32), 'wv_w': jax.random.normal(ks[5], (D_MODEL, D_MODEL), jnp.float32) * sc, 'wv_b': jnp.zeros((D_MODEL,), jnp.float32), 'wo_w': jax.random.normal(ks[6], (D_MODEL, D_MODEL), jnp.float32) * sc, 'wo_b': jnp.zeros((D_MODEL,), jnp.float32)}
        return inp
    _L3_xattn_all = _L3_xattn_setup()
    _L3_xattn_in = {k: v for k, v in _L3_xattn_all.items() if k in ('wq_w', 'wq_b', 'wk_w', 'wk_b', 'wv_w', 'wv_b', 'wo_w', 'wo_b')}
    del _L3_xattn_all

    def _L3_ffn_setup():
        import jax, jax.numpy as jnp
        import numpy as np
        B, S, H, NH, E, F = (4, 128, 128, 16, 8, 512)
        D = H // NH
        EPS = 1e-05

        def _layernorm(x, g, b):
            mu = jnp.mean(x, axis=-1, keepdims=True)
            var = jnp.var(x, axis=-1, keepdims=True)
            return (x - mu) * jax.lax.rsqrt(var + EPS) * g + b
        key = jax.random.key(seed)
        ks = jax.random.split(key, 16)
        s = 0.02
        return {'x': jax.random.normal(ks[0], (B, S, H), jnp.float32), 'ln1_g': jnp.ones((H,), jnp.float32), 'ln1_b': jnp.zeros((H,), jnp.float32), 'ln2_g': jnp.ones((H,), jnp.float32), 'ln2_b': jnp.zeros((H,), jnp.float32), 'wq': jax.random.normal(ks[1], (H, H), jnp.float32) * s, 'bq': jnp.zeros((H,), jnp.float32), 'wk': jax.random.normal(ks[2], (H, H), jnp.float32) * s, 'bk': jnp.zeros((H,), jnp.float32), 'wv': jax.random.normal(ks[3], (H, H), jnp.float32) * s, 'bv': jnp.zeros((H,), jnp.float32), 'wo': jax.random.normal(ks[4], (H, H), jnp.float32) * s, 'bo': jnp.zeros((H,), jnp.float32), 'gate_w': jax.random.normal(ks[5], (H, E), jnp.float32) * s, 'gate_b': jnp.zeros((E,), jnp.float32), 'w1': jax.random.normal(ks[6], (E, H, F), jnp.float32) * s, 'b1': jnp.zeros((E, F), jnp.float32), 'w2': jax.random.normal(ks[7], (E, F, H), jnp.float32) * s, 'b2': jnp.zeros((E, H), jnp.float32)}
    _L3_ffn_all = _L3_ffn_setup()
    _L3_ffn_in = {k: v for k, v in _L3_ffn_all.items() if k in ('ln1_g', 'ln1_b', 'ln2_g', 'ln2_b', 'wq', 'bq', 'wk', 'bk', 'wv', 'bv', 'wo', 'bo', 'gate_w', 'gate_b', 'w1', 'b1', 'w2', 'b2')}
    del _L3_ffn_all
    return {'x': x, 'ctx_1024': ctx_1024, 'itok_BxS_0_1023': itok_BxS_0_1023, 'itok_BxS2_0_2047': itok_BxS2_0_2047, 'mask_1x1xSxS2_bf1': mask_1x1xSxS2_bf1, 'g_xattn': g_xattn, 'g_ffn': g_ffn, 'L0_xattn_q1_w': _L0_xattn_in['q1_w'], 'L0_xattn_q2_w': _L0_xattn_in['q2_w'], 'L0_xattn_kv1_w': _L0_xattn_in['kv1_w'], 'L0_xattn_kv2_w': _L0_xattn_in['kv2_w'], 'L0_xattn_proj_w': _L0_xattn_in['proj_w'], 'L0_xattn_proj_b': _L0_xattn_in['proj_b'], 'L0_xattn_norm_w': _L0_xattn_in['norm_w'], 'L0_xattn_lambda_1': _L0_xattn_in['lambda_1'], 'L0_xattn_lambda_2': _L0_xattn_in['lambda_2'], 'L0_ffn_gate_W': _L0_ffn_in['gate_W'], 'L0_ffn_w1_e': _L0_ffn_in['w1_e'], 'L0_ffn_w3_e': _L0_ffn_in['w3_e'], 'L0_ffn_w2_e': _L0_ffn_in['w2_e'], 'L0_ffn_w1_s': _L0_ffn_in['w1_s'], 'L0_ffn_w3_s': _L0_ffn_in['w3_s'], 'L0_ffn_w2_s': _L0_ffn_in['w2_s'], 'L1_xattn_Wq': _L1_xattn_in['Wq'], 'L1_xattn_bq': _L1_xattn_in['bq'], 'L1_xattn_Wo': _L1_xattn_in['Wo'], 'L1_xattn_bo': _L1_xattn_in['bo'], 'L1_ffn_W_fc': _L1_ffn_in['W_fc'], 'L1_ffn_ln_w': _L1_ffn_in['ln_w'], 'L1_ffn_ln_b': _L1_ffn_in['ln_b'], 'L1_ffn_W_proj': _L1_ffn_in['W_proj'], 'L2_xattn_Wq': _L2_xattn_in['Wq'], 'L2_xattn_bq': _L2_xattn_in['bq'], 'L2_xattn_Wk': _L2_xattn_in['Wk'], 'L2_xattn_bk': _L2_xattn_in['bk'], 'L2_xattn_Wv': _L2_xattn_in['Wv'], 'L2_xattn_bv': _L2_xattn_in['bv'], 'L2_ffn_gate_w': _L2_ffn_in['gate_w'], 'L2_ffn_gate_b': _L2_ffn_in['gate_b'], 'L2_ffn_w1': _L2_ffn_in['w1'], 'L2_ffn_b1': _L2_ffn_in['b1'], 'L2_ffn_w2': _L2_ffn_in['w2'], 'L2_ffn_b2': _L2_ffn_in['b2'], 'L3_xattn_wq_w': _L3_xattn_in['wq_w'], 'L3_xattn_wq_b': _L3_xattn_in['wq_b'], 'L3_xattn_wk_w': _L3_xattn_in['wk_w'], 'L3_xattn_wk_b': _L3_xattn_in['wk_b'], 'L3_xattn_wv_w': _L3_xattn_in['wv_w'], 'L3_xattn_wv_b': _L3_xattn_in['wv_b'], 'L3_xattn_wo_w': _L3_xattn_in['wo_w'], 'L3_xattn_wo_b': _L3_xattn_in['wo_b'], 'L3_ffn_ln1_g': _L3_ffn_in['ln1_g'], 'L3_ffn_ln1_b': _L3_ffn_in['ln1_b'], 'L3_ffn_ln2_g': _L3_ffn_in['ln2_g'], 'L3_ffn_ln2_b': _L3_ffn_in['ln2_b'], 'L3_ffn_wq': _L3_ffn_in['wq'], 'L3_ffn_bq': _L3_ffn_in['bq'], 'L3_ffn_wk': _L3_ffn_in['wk'], 'L3_ffn_bk': _L3_ffn_in['bk'], 'L3_ffn_wv': _L3_ffn_in['wv'], 'L3_ffn_bv': _L3_ffn_in['bv'], 'L3_ffn_wo': _L3_ffn_in['wo'], 'L3_ffn_bo': _L3_ffn_in['bo'], 'L3_ffn_gate_w': _L3_ffn_in['gate_w'], 'L3_ffn_gate_b': _L3_ffn_in['gate_b'], 'L3_ffn_w1': _L3_ffn_in['w1'], 'L3_ffn_b1': _L3_ffn_in['b1'], 'L3_ffn_w2': _L3_ffn_in['w2'], 'L3_ffn_b2': _L3_ffn_in['b2']}

def reference(x, ctx_1024, itok_BxS_0_1023, itok_BxS2_0_2047, mask_1x1xSxS2_bf1, g_xattn, g_ffn, L0_xattn_q1_w, L0_xattn_q2_w, L0_xattn_kv1_w, L0_xattn_kv2_w, L0_xattn_proj_w, L0_xattn_proj_b, L0_xattn_norm_w, L0_xattn_lambda_1, L0_xattn_lambda_2, L0_ffn_gate_W, L0_ffn_w1_e, L0_ffn_w3_e, L0_ffn_w2_e, L0_ffn_w1_s, L0_ffn_w3_s, L0_ffn_w2_s, L1_xattn_Wq, L1_xattn_bq, L1_xattn_Wo, L1_xattn_bo, L1_ffn_W_fc, L1_ffn_ln_w, L1_ffn_ln_b, L1_ffn_W_proj, L2_xattn_Wq, L2_xattn_bq, L2_xattn_Wk, L2_xattn_bk, L2_xattn_Wv, L2_xattn_bv, L2_ffn_gate_w, L2_ffn_gate_b, L2_ffn_w1, L2_ffn_b1, L2_ffn_w2, L2_ffn_b2, L3_xattn_wq_w, L3_xattn_wq_b, L3_xattn_wk_w, L3_xattn_wk_b, L3_xattn_wv_w, L3_xattn_wv_b, L3_xattn_wo_w, L3_xattn_wo_b, L3_ffn_ln1_g, L3_ffn_ln1_b, L3_ffn_ln2_g, L3_ffn_ln2_b, L3_ffn_wq, L3_ffn_bq, L3_ffn_wk, L3_ffn_bk, L3_ffn_wv, L3_ffn_bv, L3_ffn_wo, L3_ffn_bo, L3_ffn_gate_w, L3_ffn_gate_b, L3_ffn_w1, L3_ffn_b1, L3_ffn_w2, L3_ffn_b2):
    import jax
    import jax.numpy as jnp

    def _L0_xattn_ref(query, key, value, qpos, kpos, q1_w, q2_w, kv1_w, kv2_w, proj_w, proj_b, norm_w, lambda_1, lambda_2):
        import jax, jax.numpy as jnp
        import numpy as np
        DIM = 128
        H = 16
        HD = DIM // H
        SCALE = HD ** (-0.5)
        LAMBDA_INIT = 0.1
        EPS = 1e-06

        def _split_heads(x, B, N):
            return x.reshape(B, N, H, HD).transpose(0, 2, 1, 3)
        B, Nq, C = query.shape
        Nk = key.shape[1]
        q1 = _split_heads(query @ q1_w.T, B, Nq)
        q2 = _split_heads(query @ q2_w.T, B, Nq)
        kv1 = (key @ kv1_w.T).reshape(B, Nk, 2, H, HD).transpose(2, 0, 3, 1, 4)
        k1, v1 = (kv1[0], kv1[1])
        kv2 = (key @ kv2_w.T).reshape(B, Nk, 2, H, HD).transpose(2, 0, 3, 1, 4)
        k2 = kv2[0]
        attn1 = jax.nn.softmax(jnp.einsum('bhqd,bhkd->bhqk', q1, k1) * SCALE, axis=-1)
        attn2 = jax.nn.softmax(jnp.einsum('bhqd,bhkd->bhqk', q2, k2) * SCALE, axis=-1)
        lambda_full = lambda_1 - lambda_2 + LAMBDA_INIT
        diff_attn = attn1 - lambda_full * attn2
        x = jnp.einsum('bhqk,bhkd->bhqd', diff_attn, v1)
        x = x.transpose(0, 2, 1, 3).reshape(B, Nq, C)
        xf = x.astype(jnp.float32)
        xf = xf * jax.lax.rsqrt(jnp.mean(xf * xf, axis=-1, keepdims=True) + EPS) * norm_w
        x = xf.astype(x.dtype)
        return x @ proj_w.T + proj_b

    def _L0_ffn_ref(hidden_states, gate_W, w1_e, w3_e, w2_e, w1_s, w3_s, w2_s):
        import jax, jax.numpy as jnp
        import numpy as np
        B, S, D, F, E, NS, K = (2, 128, 128, 512, 8, 8, 2)
        FS = F // NS
        b, s, d = hidden_states.shape
        e = gate_W.shape[0]
        flat = hidden_states.reshape(-1, d)
        T = flat.shape[0]
        logits = (flat @ gate_W.T).astype(jnp.float32)
        probs = jax.nn.softmax(logits, axis=-1)
        top_v, top_i = jax.lax.top_k(probs, K)
        gates = jnp.zeros((T, e), probs.dtype).at[jnp.arange(T)[:, None], top_i].set(top_v)
        g = jax.nn.silu(jnp.einsum('td,edf->etf', flat, w1_e))
        u = jnp.einsum('td,edf->etf', flat, w3_e)
        out_e = jnp.einsum('etf,efd->etd', g * u, w2_e)
        routed = jnp.einsum('te,etd->td', gates, out_e).reshape(b, s, d)
        gs = jax.nn.silu(jnp.einsum('bsd,ndf->nbsf', hidden_states, w1_s))
        us = jnp.einsum('bsd,ndf->nbsf', hidden_states, w3_s)
        shared = jnp.einsum('nbsf,nfd->bsd', gs * us, w2_s) / w1_s.shape[0]
        alpha = 0.5
        return alpha * shared + (1.0 - alpha) * routed

    def _L1_xattn_ref(query, key, value, Wq, bq, Wo, bo):
        import jax, jax.numpy as jnp
        import numpy as np
        D_MODEL = 128
        SCALE = 1.0 / np.sqrt(D_MODEL).astype(np.float32)
        q = query @ Wq + bq
        k = key @ Wq + bq
        v = value @ Wq + bq
        scores = jnp.einsum('bqd,bkd->bqk', q, k) * SCALE
        attn = jax.nn.softmax(scores, axis=-1)
        f = jnp.einsum('bqk,bkd->bqd', attn, v)
        return f @ Wo + bo

    def _L1_ffn_ref(x, W_fc, ln_w, ln_b, W_proj):
        import jax, jax.numpy as jnp
        import numpy as np
        EPS = 1e-06
        LN_EPS = 1e-05

        def _absmean_core(W):
            gamma = jnp.mean(jnp.abs(W)) + EPS
            Ws = W / gamma
            Wq = jnp.sign(Ws) * jnp.minimum(jnp.round(jnp.abs(Ws)), 1.0)
            return (Wq, gamma)

        @jax.custom_vjp
        def absmean(W):
            return _absmean_core(W)[0]

        def _absmean_fwd(W):
            Wq, gamma = _absmean_core(W)
            return (Wq, gamma)

        def _absmean_bwd(gamma, g):
            return (g / gamma,)
        absmean.defvjp(_absmean_fwd, _absmean_bwd)

        def layernorm(x, w, b, eps=LN_EPS):
            mu = jnp.mean(x, axis=-1, keepdims=True)
            var = jnp.mean((x - mu) ** 2, axis=-1, keepdims=True)
            return (x - mu) * jax.lax.rsqrt(var + eps) * w + b
        h = jnp.einsum('btd,hd->bth', x, absmean(W_fc))
        h = jax.nn.gelu(h, approximate=False)
        h = layernorm(h, ln_w, ln_b)
        return jnp.einsum('bth,dh->btd', h, absmean(W_proj))

    def _L2_xattn_ref(target, non_target, Wq, bq, Wk, bk, Wv, bv):
        import jax, jax.numpy as jnp
        import numpy as np
        B, SQ, SKV, D = (8, 256, 256, 128)
        q = jnp.einsum('bsd,ed->bse', target, Wq) + bq
        k = jnp.einsum('bsd,ed->bse', non_target, Wk) + bk
        v = jnp.einsum('bsd,ed->bse', non_target, Wv) + bv
        scores = jnp.einsum('bqd,bkd->bqk', q, k)
        weights = jax.nn.softmax(scores, axis=-1)
        return jnp.einsum('bqk,bkd->bqd', weights, v)

    def _L2_ffn_ref(x, gate_w, gate_b, w1, b1, w2, b2):
        import jax, jax.numpy as jnp
        import numpy as np
        E = 8
        K = 2
        TEMP = 1.0
        D = 128
        H = 4 * D
        B, T = (2, 256)
        b, t, d = x.shape
        xf = x.reshape(-1, d)
        logits = xf @ gate_w + gate_b
        gates = jax.nn.softmax(logits / TEMP, axis=-1)
        topk_gates, topk_idx = jax.lax.top_k(gates, K)
        topk_gates = topk_gates / (topk_gates.sum(-1, keepdims=True) + 1e-09)
        comb = (jax.nn.one_hot(topk_idx, E, dtype=xf.dtype) * topk_gates[..., None]).sum(axis=1)
        out = jnp.zeros_like(xf)
        for e in range(E):
            h = jax.nn.gelu(xf @ w1[e] + b1[e], approximate=False)
            out = out + comb[:, e:e + 1] * (h @ w2[e] + b2[e])
        return out.reshape(b, t, d)

    def _L3_xattn_ref(q, k, v, mask, wq_w, wq_b, wk_w, wk_b, wv_w, wv_b, wo_w, wo_b):
        import jax, jax.numpy as jnp
        import numpy as np
        D_MODEL = 128
        H = 16
        D_K = D_MODEL // H
        B, S = (2, 256)

        def _split_heads(x):
            b, s, _ = x.shape
            return x.reshape(b, s, H, D_K).transpose(0, 2, 1, 3)
        qh = _split_heads(q @ wq_w.T + wq_b)
        kh = _split_heads(k @ wk_w.T + wk_b)
        vh = _split_heads(v @ wv_w.T + wv_b)
        scores = jnp.einsum('bhqd,bhkd->bhqk', qh, kh) / jnp.sqrt(jnp.float32(D_K))
        scores = jnp.where(mask, scores, jnp.float32(-1000000000.0))
        attn = jax.nn.softmax(scores, axis=-1)
        out = jnp.einsum('bhqk,bhkd->bhqd', attn, vh)
        out = out.transpose(0, 2, 1, 3).reshape(q.shape[0], q.shape[1], D_MODEL)
        return out @ wo_w.T + wo_b

    def _L3_ffn_ref(x, ln1_g, ln1_b, ln2_g, ln2_b, wq, bq, wk, bk, wv, bv, wo, bo, gate_w, gate_b, w1, b1, w2, b2):
        import jax, jax.numpy as jnp
        import numpy as np
        B, S, H, NH, E, F = (4, 128, 128, 16, 8, 512)
        D = H // NH
        EPS = 1e-05

        def _layernorm(x, g, b):
            mu = jnp.mean(x, axis=-1, keepdims=True)
            var = jnp.var(x, axis=-1, keepdims=True)
            return (x - mu) * jax.lax.rsqrt(var + EPS) * g + b
        b, s, h = x.shape
        hn = _layernorm(x, ln1_g, ln1_b)
        q = (hn @ wq + bq).reshape(b, s, NH, D).transpose(0, 2, 1, 3)
        k = (hn @ wk + bk).reshape(b, s, NH, D).transpose(0, 2, 1, 3)
        v = (hn @ wv + bv).reshape(b, s, NH, D).transpose(0, 2, 1, 3)
        scores = jnp.einsum('bhqd,bhkd->bhqk', q, k) / jnp.sqrt(jnp.float32(D))
        attn = jax.nn.softmax(scores, axis=-1)
        o = jnp.einsum('bhqk,bhkd->bhqd', attn, v)
        o = o.transpose(0, 2, 1, 3).reshape(b, s, h)
        x = x + (o @ wo + bo)
        hn2 = _layernorm(x, ln2_g, ln2_b).reshape(-1, h)
        logits = hn2 @ gate_w + gate_b
        idx = jnp.argmax(logits, axis=-1)
        mid = jax.nn.relu(jnp.einsum('th,ehf->etf', hn2, w1) + b1[:, None, :])
        y = jnp.einsum('etf,efh->eth', mid, w2) + b2[:, None, :]
        moe = y[idx, jnp.arange(hn2.shape[0])]
        return x + moe.reshape(b, s, h)
    x = x + jnp.tanh(g_xattn[0]) * _L0_xattn_ref(_layernorm(x, axis=-1), ctx_1024, ctx_1024, itok_BxS_0_1023, itok_BxS2_0_2047, L0_xattn_q1_w, L0_xattn_q2_w, L0_xattn_kv1_w, L0_xattn_kv2_w, L0_xattn_proj_w, L0_xattn_proj_b, L0_xattn_norm_w, L0_xattn_lambda_1, L0_xattn_lambda_2)
    x = x + jnp.tanh(g_ffn[0]) * _L0_ffn_ref(_layernorm(x, axis=-1), L0_ffn_gate_W, L0_ffn_w1_e, L0_ffn_w3_e, L0_ffn_w2_e, L0_ffn_w1_s, L0_ffn_w3_s, L0_ffn_w2_s)
    x = x + jnp.tanh(g_xattn[1]) * _L1_xattn_ref(_layernorm(x, axis=-1), ctx_1024, ctx_1024, L1_xattn_Wq, L1_xattn_bq, L1_xattn_Wo, L1_xattn_bo)
    x = x + jnp.tanh(g_ffn[1]) * _L1_ffn_ref(_layernorm(x, axis=-1), L1_ffn_W_fc, L1_ffn_ln_w, L1_ffn_ln_b, L1_ffn_W_proj)
    x = x + jnp.tanh(g_xattn[2]) * _L2_xattn_ref(_layernorm(x, axis=-1), ctx_1024, L2_xattn_Wq, L2_xattn_bq, L2_xattn_Wk, L2_xattn_bk, L2_xattn_Wv, L2_xattn_bv)
    x = x + jnp.tanh(g_ffn[2]) * _L2_ffn_ref(_layernorm(x, axis=-1), L2_ffn_gate_w, L2_ffn_gate_b, L2_ffn_w1, L2_ffn_b1, L2_ffn_w2, L2_ffn_b2)
    x = x + jnp.tanh(g_xattn[3]) * _L3_xattn_ref(_layernorm(x, axis=-1), ctx_1024, ctx_1024, mask_1x1xSxS2_bf1, L3_xattn_wq_w, L3_xattn_wq_b, L3_xattn_wk_w, L3_xattn_wk_b, L3_xattn_wv_w, L3_xattn_wv_b, L3_xattn_wo_w, L3_xattn_wo_b)
    x = x + jnp.tanh(g_ffn[3]) * _L3_ffn_ref(_layernorm(x, axis=-1), L3_ffn_ln1_g, L3_ffn_ln1_b, L3_ffn_ln2_g, L3_ffn_ln2_b, L3_ffn_wq, L3_ffn_bq, L3_ffn_wk, L3_ffn_bk, L3_ffn_wv, L3_ffn_bv, L3_ffn_wo, L3_ffn_bo, L3_ffn_gate_w, L3_ffn_gate_b, L3_ffn_w1, L3_ffn_b1, L3_ffn_w2, L3_ffn_b2)
    return x

_drawn_inputs = setup_inputs


def setup_inputs(seed=0):
    import zlib

    import numpy as np

    out = dict(_drawn_inputs(seed))
    spreads = {'L0_xattn_proj_b': (0.0, 0.1),
     'L0_xattn_norm_w': (1.0, 0.2),
     'L0_xattn_lambda_1': (1.0, 0.2),
     'L0_xattn_lambda_2': (0.9916666746139526, 0.2),
     'L1_ffn_ln_w': (1.0, 0.2),
     'L1_ffn_ln_b': (0.0, 0.1),
     'L2_ffn_gate_b': (0.0, 0.8),
     'L2_ffn_b1': (0.0, 0.8),
     'L2_ffn_b2': (0.0, 0.8),
     'L3_xattn_wq_b': (0.0, 0.8),
     'L3_xattn_wk_b': (0.0, 0.8),
     'L3_xattn_wv_b': (0.0, 0.8),
     'L3_xattn_wo_b': (0.0, 0.8),
     'L3_ffn_ln1_g': (1.0, 0.6),
     'L3_ffn_ln1_b': (0.0, 0.8),
     'L3_ffn_ln2_g': (1.0, 0.6),
     'L3_ffn_ln2_b': (0.0, 0.8),
     'L3_ffn_bq': (0.0, 0.8),
     'L3_ffn_bk': (0.0, 0.8),
     'L3_ffn_bv': (0.0, 0.8),
     'L3_ffn_bo': (0.0, 0.8),
     'L3_ffn_gate_b': (0.0, 0.8),
     'L3_ffn_b1': (0.0, 0.8),
     'L3_ffn_b2': (0.0, 0.8)}
    factors = {'L0_xattn_q1_w': 8.0,
     'L0_xattn_q2_w': 8.0,
     'L0_xattn_kv2_w': 8.0,
     'L0_ffn_gate_W': 8.0,
     'L0_ffn_w1_e': 8.0,
     'L0_ffn_w3_e': 8.0,
     'L0_ffn_w2_e': 8.0,
     'L0_ffn_w1_s': 8.0,
     'L0_ffn_w3_s': 8.0,
     'L0_ffn_w2_s': 8.0,
     'L1_xattn_bq': 5.594,
     'L1_xattn_bo': 5.397,
     'L2_xattn_Wq': 3.114,
     'L2_xattn_bq': 8.0,
     'L2_xattn_Wk': 3.147,
     'L2_xattn_bk': 8.0,
     'L2_xattn_bv': 8.0,
     'L2_ffn_gate_w': 8.0,
     'L2_ffn_w1': 8.0,
     'L2_ffn_w2': 8.0,
     'L3_xattn_wq_w': 5.911,
     'L3_xattn_wk_w': 5.864,
     'L3_ffn_wq': 8.0,
     'L3_ffn_wk': 8.0,
     'L3_ffn_wv': 8.0,
     'L3_ffn_wo': 8.0,
     'L3_ffn_gate_w': 8.0,
     'L3_ffn_w1': 8.0,
     'L3_ffn_w2': 8.0}
    for name, (base, spread) in spreads.items():
        noise = np.random.default_rng([zlib.crc32(name.encode()), seed]).standard_normal(out[name].shape)
        drawn = base * np.exp(spread * noise) if base else spread * noise
        out[name] = jnp.asarray(drawn.astype(out[name].dtype))
    for name, factor in factors.items():
        out[name] = (out[name] * factor).astype(out[name].dtype)
    return out
```

```python
from contextlib import ExitStack

import numpy as np

import concourse.bass as bass
from concourse import mybir

ALU = mybir.AluOpType
ACT = mybir.ActivationFunctionType
AX = mybir.AxisListType
F32 = mybir.dt.float32
BF16 = mybir.dt.bfloat16
U32 = mybir.dt.uint32
U8 = mybir.dt.uint8

P = 128
B, S, SK = 4, 256, 64
T = B * S // P
TPB = S // P
N = B * S
HALF = N // 2
H, DH = 16, 8
VW = DH + 1
E = 8
FF = 512
FC = FF // P
UNIT = 1024
BANK = 512
LN_EPS = 1e-5
RMS_EPS = 1e-6
ABSMEAN_EPS = 1e-6
MASKED = -1e30

SQUARE = ["A0q1", "A0q2", "A0k1", "A0k2", "A0v", "A0o", "A3k", "A2k", "A3v", "A2v", "A3q", "A3o", "A2q",
          "F3q", "F3k", "F3v", "F3o"]
W_COLS = {n: (P * i, P) for i, n in enumerate(SQUARE)}
_at = P * len(SQUARE)
for _n, _w in (("A1o", P), ("A1q", 64), ("F0g", E), ("F2g", E), ("F3g", E)):
    W_COLS[_n] = (_at, _w)
    _at += _w
W_WIDTH = _at
COLS = {}
_at = 0
for _n, _w in (("A0norm", 1), ("A1bq", 1), ("A2bq", 1), ("A2bk", 1), ("A3bq", 1), ("A3bk", 1), ("F3bq", 1),
               ("F3bk", 1), ("F3g1", 1), ("F3b1", 1), ("F3g2", 1), ("F3b2", 1), ("F1w", FC), ("F1b", FC)):
    COLS[_n] = (_at, _w)
    _at += _w
COLS_WIDTH = _at
ROWS = {}
_at = 0
for _n, _w in (("A0bo", P), ("A1bo", P), ("A2bv", P), ("A3bv", P), ("A3bo", P), ("F3bv", P), ("F3bo", P),
               ("A1bv", 64), ("F2gb", E), ("F3gb", E), ("gx", 4), ("gf", 4), ("lam1", H), ("lam2", H)):
    ROWS[_n] = (_at, _w)
    _at += _w
ROWS_WIDTH = _at
SCALARS = 8 + 2 * H
C_ID, C_ONES, C_HEAD, C_IOTA = 0, P, 2 * P, 2 * P + H
C_WIDTH = 2 * P + H + E
POWERS = ["A0", "A0rms", "F0", "A1", "F1", "F1h", "A2", "F2", "A3", "F3in", "B3", "F3"]
TURNED = ["A0", "F0", "A1", "F1", "A2", "F2", "A3", "B3", "F3"]


def build(nc, x_in, ctx_in, w_in, cols_in, rows_in, const_in, mask_in, f1_in, moe0_in, moe2_in, moe3_in, down_bias_in, out):
    with ExitStack() as ctx:
        def sb(name, shape, dt=F32):
            return ctx.enter_context(nc.sbuf_tensor(name, shape, dt))

        x = sb("x", [P, T, P])
        z = sb("z", [P, T, P])
        xn = sb("xn", [P, T, P])
        xnT = sb("xnT", [P, N])
        ctxT = sb("ctxT", [P, B, 2, SK])
        w = sb("w", [P, W_WIDTH])
        cols = sb("cols", [P, COLS_WIDTH])
        rows = sb("rows", [1, ROWS_WIDTH])
        const = sb("const", [P, C_WIDTH])
        ident_bf = sb("ident_bf", [P, P], BF16)
        mask_raw = sb("mask_raw", [P, TPB, SK], U8)
        mask_add = sb("mask_add", [P, TPB, SK], BF16)
        f1w = sb("f1w", [P, 2, FF])
        f1q = sb("f1q", [P, 2, FF])
        f1t = sb("f1t", [P, 2, FF])
        down_bias = sb("down_bias", [E, 2, P])
        wring = sb("wring", [P, 3, 3 * FF])
        keyT = sb("keyT", [P, 5, B * SK])
        kblock = sb("kblock", [P, 16 * UNIT])
        v0 = sb("v0", [P, B, H // 2, 2 * VW])
        v3 = sb("v3", [P, B, H // 2, 2 * VW])
        vself = sb("vself", [P, T, H, VW])
        v2 = sb("v2", [P, B, P])
        v1 = sb("v1", [P, B, 64])
        qT = sb("qT", [P, 2, N])
        qslot = sb("qslot", [P, 4, P])
        prob = sb("prob", [P, 2, UNIT])
        probT = sb("probT", [P, 2, UNIT])
        heads = sb("heads", [P, 2, T, P])
        headsT = heads[:, 1, :, :].rearrange("p t c -> p (t c)")
        hid = sb("hid", [P, 2, FC, BANK])
        silu = sb("silu", [P, 2, BANK])
        acc = sb("acc", [P, T, P])
        stats = sb("stats", [P, T, 6])
        meanvar = sb("meanvar", [P, T, 2])
        var_eps = sb("var_eps", [P, T])
        rstd = sb("rstd", [P, T])
        minus_half = sb("minus_half", [P, T])
        rowmax = sb("rowmax", [P, 2, H])
        rsum = sb("rsum", [P, 2, H])
        scal = sb("scal", [P, SCALARS])
        tanh_g = sb("tanh_g", [P, 9])
        lam = sb("lam", [P, H])
        thr = sb("thr", [P, 6])
        logit = sb("logit", [P, T, E])
        gprob = sb("gprob", [P, T, E])
        top = sb("top", [P, T, 8])
        topi = sb("topi", [P, T, 8], U32)
        topf = sb("topf", [P, T, 8])
        pick = sb("pick", [P, 2, T, E])
        small = sb("small", [P, 4, T])
        gates = sb("gates", [P, T, E + 1])
        gatesT = probT[0:E, 0, :]
        bank = ctx.enter_context(nc.psum_tensor("bank", [P, 8, BANK], F32))

        ident = const[:, C_ID:C_ID + P]
        ones_row = const[0:1, C_ONES:C_ONES + P]
        ones_sq = const[:, C_ONES:C_ONES + P]
        head_of = const[:, C_HEAD:C_HEAD + H]
        iota = const[:, C_IOTA:C_IOTA + E]

        def W(name):
            o, n = W_COLS[name]
            return w[:, o:o + n]

        def col(name, i=0):
            o = COLS[name][0] + i
            return cols[:, o:o + 1]

        def row(name):
            o, n = ROWS[name]
            return rows[0:1, o:o + n]

        def banks(i, n=2):
            return bank[:, i:i + n, :].rearrange("p b c -> p (b c)")

        def spread(ap, shape, axis):
            return ap.unsqueeze(axis).broadcast_to(shape)

        made = {}

        def sig(name):
            if name not in made:
                made[name] = ctx.enter_context(nc.semaphore(name))
            return made[name]

        class Attn:
            def __init__(self, name, span, units, slots, maps, heads_per_unit, scale, ones_values):
                self.name, self.units, self.slots, self.maps = name, units, slots, maps
                self.span, self.rounds, self.tiles = span, B // span, span * TPB
                self.hpu, self.kpu = heads_per_unit, UNIT // heads_per_unit
                self.scale, self.values = scale, ones_values
                self.per_slot = units // slots

            def tile(self, j):
                return j * self.tiles // self.units

            def map(self, j):
                return j % self.maps

            def group(self, j):
                return j % (H // self.hpu)

            def key_at(self, r, j):
                if self.name == "A0":
                    return r * (self.span * UNIT) + self.map(j) * B * UNIT
                if self.name == "A3":
                    return r * (self.span * UNIT) + (2 * B + self.tile(j) // TPB) * UNIT
                return r * (4 * UNIT) + self.group(j) * UNIT

        A0 = Attn("A0", 1, 2 * TPB, 2 * TPB, 2, H, DH ** -0.5, v0)
        A3 = Attn("A3", 2, 2 * TPB, 2 * TPB, 1, H, DH ** -0.5, v3)
        B3 = Attn("B3", 1, 4 * TPB, TPB, 1, 4, DH ** -0.5, vself)

        class Moe:
            def __init__(self, name, experts, ring, func, gated):
                self.name, self.experts, self.ring, self.func, self.gated = name, experts, ring, func, gated
                self.rounds = experts // ring

        F0 = Moe("F0", E + 1, 3, ACT.Silu, True)
        F2 = Moe("F2", E, 2, ACT.Gelu, False)
        F3 = Moe("F3", E, 2, ACT.Relu, False)
        moe_dram = {"F0": moe0_in, "F2": moe2_in, "F3": moe3_in}

        block = ctx.enter_context(nc.Block())

        @block.sync
        def _(sp):
            sp.dma_start(const[:], const_in).then_inc(sig("const_landed"), 16)
            sp.dma_start(x[:], x_in).then_inc(sig("x_landed"), 16)
            sp.dma_start(f1w[:], f1_in).then_inc(sig("f1_landed"), 16)
            sp.dma_start(mask_raw[:], mask_in).then_inc(sig("mask_landed"), 16)
            sp.dma_start(down_bias[:], down_bias_in).then_inc(sig("down_bias_landed"), 16)

            def load_expert(m, e, slot):
                width = 3 * FF if m.gated else 2 * FF + FC
                sp.dma_start(wring[:, slot, 0:width], moe_dram[m.name][e]).then_inc(
                    sig(f"{m.name}_w{slot}_landed"), 16)

            def stream_experts(m, before):
                if before is not None:
                    sp.wait_ge(sig(f"{before.name}_down_ready"), 2 * before.experts)
                for r in range(m.ring):
                    load_expert(m, r, r)
                with sp.Fori(1, m.rounds) as i:
                    for r in range(m.ring):
                        sp.wait_ge(sig(f"{m.name}_down_ready"), (i - 1) * (2 * m.ring) + 2 * (r + 1))
                        load_expert(m, bass.ds(i * m.ring + r, 1), r)

            stream_experts(F0, None)
            stream_experts(F2, F0)
            stream_experts(F3, F2)
            sp.wait_ge(sig("x_final"), 1)
            sp.dma_start(out, x[:]).then_inc(sig("out_written"), 16)
            sp.wait_ge(sig("out_written"), 16)

        @block.gpsimd
        def _(pool):
            def power(name):
                pool.wait_ge(sig("var_ready"), POWERS.index(name) + 1)
                nc.gpsimd.tensor_tensor(rstd[:], var_eps[:], minus_half[:], ALU.pow).then_inc(sig("rstd_ready"), 1)

            def block_keys(name, dst, src, width):
                nc.gpsimd.tensor_tensor(
                    kblock[:, dst:dst + H * width].rearrange("p (h k) -> p h k", h=H),
                    spread(src, [P, H, width], 1), spread(head_of, [P, H, width], 2), ALU.mult,
                ).then_inc(sig(f"{name}_keys_spread"), 1)

            def fill_slots(a):
                def fill(b, s):
                    j = s * a.per_slot
                    at = b * (a.tiles * P) + a.tile(j) * P
                    nc.gpsimd.tensor_copy(qslot[:, s, :], qT[:, a.map(j), bass.ds(at, P)]).then_inc(
                        sig(f"{a.name}_slot_filled"), 1)

                pool.wait_ge(sig(f"{a.name}_q_copied"), 2 * a.maps)
                for s in range(a.slots):
                    fill(0, s)
                with pool.Fori(1, a.rounds) as b:
                    for s in range(a.slots):
                        pool.wait_ge(sig(f"{a.name}_scores_ready"), (b - 1) * a.units + (s + 1) * a.per_slot)
                        fill(b, s)

            nc.gpsimd.memset(minus_half[:], -0.5).then_inc(sig("minus_half_set"), 1)
            pool.wait_ge(sig("minus_half_set"), 1)
            power("A0")
            pool.wait_ge(sig("const_landed"), 16)
            pool.wait_ge(sig("keys_copied"), 2)
            for b in range(B):
                block_keys("A0m1", (B + b) * UNIT, keyT[:, 1, b * SK:(b + 1) * SK], SK)
            fill_slots(A0)
            pool.wait_ge(sig("keys_copied"), 5)
            for b in range(B):
                block_keys("A3", (2 * B + b) * UNIT, keyT[:, 2, b * SK:(b + 1) * SK], SK)
            power("A0rms")
            pool.wait_ge(sig("thresholds_ready"), 1)
            for i in range(2):
                nc.gpsimd.tensor_scalar(f1t[:, i, :], f1w[:, i, :], thr[:, 4 + i:5 + i], None, ALU.is_lt)
                nc.gpsimd.tensor_scalar(f1q[:, i, :], f1w[:, i, :], thr[:, 2 + i:3 + i], None, ALU.is_gt).then_inc(
                    sig("f1_compared"), 1)
            pool.wait_ge(sig("f1_compared"), 2)
            nc.gpsimd.tensor_tensor(f1q[:], f1q[:], f1t[:], ALU.subtract).then_inc(sig("f1_ternary"), 1)
            for name in ["F0", "A1", "F1", "F1h", "A2", "F2", "A3"]:
                power(name)
            fill_slots(A3)
            power("F3in")
            power("B3")
            pool.wait_ge(sig("B3_k_copied"), 2)
            for b in range(B):
                block_keys("B3", b * 4 * UNIT, qT[:, 1, b * S:(b + 1) * S], S)
                if b == 0:
                    pool.wait_ge(sig("B3_q_copied"), 2)
                    for s in range(B3.slots):
                        nc.gpsimd.tensor_copy(qslot[:, s, :], qT[:, 0, s * P:(s + 1) * P]).then_inc(
                            sig("B3_slot_filled"), 1)
            with pool.Fori(1, B) as b:
                for s in range(B3.slots):
                    pool.wait_ge(sig("B3_scores_ready"), (b - 1) * B3.units + (s + 1) * B3.per_slot)
                    nc.gpsimd.tensor_copy(qslot[:, s, :], qT[:, 0, bass.ds(b * S + s * P, P)]).then_inc(
                        sig("B3_slot_filled"), 1)
            power("F3")

        @block.scalar
        def _(act):
            act.dma_start(ctxT[:], ctx_in).then_inc(sig("ctx_landed"), 16)
            act.dma_start(w[:], w_in).then_inc(sig("w_landed"), 16)
            act.dma_start(rows[:], rows_in).then_inc(sig("rows_landed"), 16)
            act.dma_start(cols[:], cols_in).then_inc(sig("cols_landed"), 16)

            def copy(dst, src, bias=None, scale=None):
                if bias is None and scale is None:
                    return nc.scalar.copy(dst, src)
                return nc.scalar.activation(dst, src, ACT.Identity, bias=0.0 if bias is None else bias,
                                            scale=1.0 if scale is None else scale)

            def take_transposed(name, gain=None, bias=None):
                act.wait_ge(sig("turned"), 2 * TURNED.index(name) + 1)
                copy(xnT[:, 0:HALF], bank[:, 0, :], bias, gain).then_inc(sig("xnT_ready"), 1)

            def take_queries(name, m, first_bank, bias=None, what="q", rows_=P):
                for i in range(2):
                    act.wait_ge(sig(f"{name}_{what}_projected"), 2 * m + i + 1 if what == "q" else i + 1)
                    slot = 1 if what == "k" else m
                    copy(qT[0:rows_, slot, i * HALF:(i + 1) * HALF], bank[0:rows_, first_bank + i, :], bias).then_inc(
                        sig(f"{name}_{what}_copied"), 1)

            def attend(a):
                def exps(b, j):
                    act.wait_ge(sig(f"{a.name}_shifted"), b * a.units + (j + 1))
                    nc.scalar.activation(prob[:, j % 2, :], prob[:, j % 2, :], ACT.Exp, scale=a.scale).then_inc(
                        sig(f"{a.name}_exp_ready"), 1)

                def take(b, j):
                    act.wait_ge(sig(f"{a.name}_probs_turned"), b * a.units + (j + 1))
                    nc.scalar.copy(probT[:, j % 2, :], banks(4)).then_inc(sig(f"{a.name}_probT_ready"), 1)

                def round_(b, more):
                    for j in range(a.units):
                        take(b, j)
                        if more or j + 1 < a.units:
                            exps(b, j + 1)

                exps(0, 0)
                with act.Fori(0, a.rounds - 1) as b:
                    round_(b, True)
                round_(a.rounds - 1, False)

            def take_heads(name, scale=None):
                for i in range(2):
                    act.wait_ge(sig(f"{name}_heads_turned"), i + 1)
                    copy(headsT[:, i * HALF:(i + 1) * HALF], bank[:, i, :], None, scale).then_inc(
                        sig(f"{name}_headsT_ready"), 1)

            def single_head(name, m_rows, bias, scale):
                take_transposed(name)
                take_queries(name, 0, 2, bias[0:m_rows], rows_=m_rows)
                act.wait_ge(sig(f"{name}_shifted"), 1)
                nc.scalar.activation(prob[:, 0, 0:T * SK], prob[:, 0, 0:T * SK], ACT.Exp, scale=scale).then_inc(
                    sig(f"{name}_exp_ready"), 1)
                act.wait_ge(sig(f"{name}_probs_turned"), 1)
                nc.scalar.copy(probT[:, 0, 0:BANK], bank[:, 1, :]).then_inc(sig(f"{name}_probT_ready"), 1)

            def experts(m):
                if m.name != "F3":
                    act.wait_ge(sig(f"{m.name}_logits_shifted"), 1)
                    nc.scalar.activation(gprob[:], gprob[:], ACT.Exp).then_inc(sig(f"{m.name}_gate_exp_ready"), 1)

                def unit(i, r, half, f):
                    u = (r * 2 + half) * FC + f
                    act.wait_ge(sig(f"{m.name}_up_ready"), i * (m.ring * 2 * FC) + (u + 1))
                    if m.gated:
                        nc.scalar.activation(silu[:, f % 2, :], bank[:, f % 2, :], m.func).then_inc(
                            sig(f"{m.name}_act_ready"), 1)
                    else:
                        nc.scalar.activation(hid[:, half, f, :], bank[:, f % 2, :], m.func,
                                             bias=wring[:, r, 2 * FF + f:2 * FF + f + 1]).then_inc(
                            sig(f"{m.name}_act_ready"), 1)

                def round_(i, skip=0):
                    for u in range(skip, m.ring * 2 * FC):
                        unit(i, u // (2 * FC), u // FC % 2, u % FC)

                with act.Fori(0, m.rounds - 1) as i:
                    round_(i)
                unit(m.rounds - 1, 0, 0, 0)
                unit(m.rounds - 1, 0, 0, 1)
                if not m.gated:
                    act.wait_ge(sig(f"{m.name}_gates_turned"), 1)
                    nc.scalar.copy(gatesT, banks(6)[0:E, :]).then_inc(sig(f"{m.name}_gatesT_ready"), 1)
                round_(m.rounds - 1, 2)

            act.wait_ge(sig("cols_landed"), 16)
            for i, (bk, off, bias, r) in enumerate([(0, 0, None, P), (0, 256, None, P), (1, 0, "A3bk", P),
                                                    (1, 256, "A2bk", P), (2, 0, "A1bq", 64)]):
                act.wait_ge(sig("keys_projected"), (2, 2, 4, 4, 5)[i])
                copy(keyT[0:r, i, :], bank[0:r, bk, off:off + B * SK], None if bias is None else col(bias)[0:r]
                     ).then_inc(sig("keys_copied"), 1)
            act.wait_ge(sig("scalars_copied"), 1)
            nc.scalar.activation(tanh_g[:, 0:8], scal[:, 0:8], ACT.Tanh).then_inc(sig("gates_ready"), 1)

            take_transposed("A0")
            take_queries("A0", 0, 2)
            take_queries("A0", 1, 4)
            attend(A0)
            take_heads("A0", col("A0norm"))
            take_transposed("F0")
            experts(F0)
            single_head("A1", 64, col("A1bq"), float(np.float32(1.0) / np.sqrt(np.float32(P))))
            for i in range(2):
                act.wait_ge(sig("A1_heads_turned"), i + 1)
                nc.scalar.copy(headsT[:, i * 256:(i + 1) * 256], bank[:, i, 0:256]).then_inc(
                    sig("A1_headsT_ready"), 1)
            take_transposed("F1")
            for t in range(T):
                act.wait_ge(sig("F1_up_ready"), t + 1)
                nc.scalar.activation(hid[:, t // FC, t % FC, :], bank[:, 2 + t % 2, :], ACT.Gelu).then_inc(
                    sig("F1_act_ready"), 1)
            single_head("A2", P, col("A2bq"), 1.0)
            take_transposed("F2")
            experts(F2)
            take_transposed("A3")
            take_queries("A3", 0, 2, col("A3bq"))
            attend(A3)
            take_heads("A3")
            take_transposed("B3", col("F3g1"), col("F3b1"))
            take_queries("B3", 0, 4, col("F3bk"), what="k")
            take_queries("B3", 0, 2, col("F3bq"))
            attend(B3)
            take_heads("B3")
            take_transposed("F3", col("F3g2"), col("F3b2"))
            experts(F3)

        @block.vector
        def _(dve):
            fence = nc.vector.drain

            def normalise(name, src, dst):
                for t in range(T):
                    nc.vector.bn_stats(stats[:, t, :], src[:, t, :])
                fence()
                for t in range(T):
                    nc.vector.bn_aggr(meanvar[:, t, :], stats[:, t, :])
                fence()
                nc.vector.tensor_scalar_add(var_eps[:], meanvar[:, :, 1], LN_EPS).then_inc(sig("var_ready"), 1)
                dve.wait_ge(sig("rstd_ready"), POWERS.index(name) + 1)
                for t in range(T):
                    ins = nc.vector.tensor_scalar(dst[:, t, :], src[:, t, :], meanvar[:, t, 0:1], rstd[:, t:t + 1],
                                                  ALU.subtract, ALU.mult)
                    if t % FC == FC - 1 and name in TURNED:
                        ins.then_inc(sig("normed"), 1)

            def take_transposed(name, gain=None, bias=None):
                dve.wait_ge(sig("turned"), 2 * TURNED.index(name) + 2)
                if gain is None:
                    ins = nc.vector.tensor_copy(xnT[:, HALF:N], bank[:, 1, :])
                else:
                    ins = nc.vector.tensor_scalar(xnT[:, HALF:N], bank[:, 1, :], gain, bias, ALU.mult, ALU.add)
                ins.then_inc(sig("xnT_ready"), 1)

            def attend(a):
                nc.vector.sem_inc(sig(f"{a.name}_out_free"), 2)

                def shift(b, j):
                    sc = banks(2 * (j % 2)).rearrange("p (h k) -> p h k", h=a.hpu)
                    dve.wait_ge(sig(f"{a.name}_scores_ready"), b * a.units + (j + 1))
                    nc.vector.reduce_max(rowmax[:, j % 2, 0:a.hpu], sc, AX.X)
                    fence()
                    nc.vector.tensor_tensor(prob[:, j % 2, :].rearrange("p (h k) -> p h k", h=a.hpu), sc,
                                            spread(rowmax[:, j % 2, 0:a.hpu], [P, a.hpu, a.kpu], 2),
                                            ALU.subtract).then_inc(sig(f"{a.name}_shifted"), 1)

                def take(b, j):
                    o = bank[:, 6 + j % 2, 0:a.hpu * VW].rearrange("p (h c) -> p h c", h=a.hpu)
                    dve.wait_ge(sig(f"{a.name}_out_ready"), b * a.units + (j + 1))
                    nc.vector.reciprocal(rsum[:, j % 2, 0:a.hpu], o[:, :, DH])
                    fence()
                    width = a.hpu * DH
                    dst = heads[:, a.map(j), :, :].rearrange("p t c -> p (t c)")[
                        :, bass.ds(b * (a.tiles * P) + (a.tile(j) * P + a.group(j) % (P // width) * width), width)]
                    nc.vector.tensor_tensor(dst.rearrange("p (h c) -> p h c", h=a.hpu), o[:, :, 0:DH],
                                            spread(rsum[:, j % 2, 0:a.hpu], [P, a.hpu, DH], 2),
                                            ALU.mult).then_inc(sig(f"{a.name}_out_free"), 1)

                def round_(b, more):
                    for j in range(a.units):
                        if more or j + 2 < a.units:
                            shift(b, j + 2)
                        take(b, j)

                shift(0, 0)
                shift(0, 1)
                with dve.Fori(0, a.rounds - 1) as b:
                    round_(b, True)
                round_(a.rounds - 1, False)

            def add_gated(name, gate, src):
                flat = x[:].rearrange("p t c -> p (t c)")
                nc.vector.scalar_tensor_tensor(flat, src, gate, flat, ALU.mult, ALU.add)
                fence()

            def single_head(name, width, values_dup):
                take_transposed(name)
                sc = bank[:, 0, :].rearrange("p (t k) -> p t k", t=T)
                pr = prob[:, 0, 0:T * SK].rearrange("p (t k) -> p t k", t=T)
                dve.wait_ge(sig(f"{name}_scores_ready"), 1)
                nc.vector.reduce_max(rowmax[:, 0, 0:T], sc, AX.X)
                fence()
                nc.vector.tensor_tensor(pr, sc, spread(rowmax[:, 0, 0:T], [P, T, SK], 2), ALU.subtract).then_inc(
                    sig(f"{name}_shifted"), 1)
                dve.wait_ge(sig(f"{name}_exp_ready"), 1)
                nc.vector.reduce_sum(rsum[:, 0, 0:T], pr, AX.X)
                fence()
                nc.vector.reciprocal(rsum[:, 1, 0:T], rsum[:, 0, 0:T])
                fence()
                dve.wait_ge(sig(f"{name}_out_ready"), 1)
                dst = heads[:].rearrange("p m t c -> p (m t c)")[:, 0:T * width].rearrange("p (t c) -> p t c", t=T)
                for odd in range(2):
                    o = bank[:, 6 + odd, 0:T // 2 * width].rearrange("p (t c) -> p t c", t=T // 2)
                    ins = nc.vector.tensor_tensor(dst[:, odd::2, :], o,
                                                  spread(rsum[:, 1, odd:T:2], [P, T // 2, width], 2), ALU.mult)
                return ins

            def route(m):
                lg = bank[:, 6, 0:T * E].rearrange("p (t e) -> p t e", t=T)
                wide = [P, T, E]
                dve.wait_ge(sig(f"{m.name}_logits_ready"), 1)
                if m.name == "F3":
                    nc.vector.tensor_copy(gprob[:], lg)
                    fence()
                else:
                    nc.vector.reduce_max(small[:, 0, :], lg, AX.X)
                    fence()
                    nc.vector.tensor_tensor(gprob[:], lg, spread(small[:, 0, :], wide, 2), ALU.subtract).then_inc(
                        sig(f"{m.name}_logits_shifted"), 1)
                    dve.wait_ge(sig(f"{m.name}_gate_exp_ready"), 1)
                    nc.vector.reduce_sum(small[:, 1, :], gprob[:], AX.X)
                    fence()
                    nc.vector.reciprocal(small[:, 2, :], small[:, 1, :])
                    fence()
                    nc.vector.tensor_tensor(gprob[:], gprob[:], spread(small[:, 2, :], wide, 2), ALU.mult)
                    fence()
                for t in range(T):
                    nc.vector.max(top[:, t, :], gprob[:, t, :])
                fence()
                for t in range(T):
                    nc.vector.max_index(topi[:, t, :], top[:, t, :], gprob[:, t, :])
                fence()
                nc.vector.tensor_copy(topf[:], topi[:])
                fence()
                iotas = spread(iota, wide, 1)
                if m.name == "F3":
                    nc.vector.tensor_tensor(gates[:, :, 0:E], iotas, topf[:, :, 0:1].broadcast_to(wide), ALU.is_equal)
                    fence()
                    return
                for k in range(2):
                    nc.vector.tensor_tensor(pick[:, k, :, :], iotas, topf[:, :, k:k + 1].broadcast_to(wide), ALU.is_equal)
                fence()
                nc.vector.tensor_tensor(pick[:, 0, :, :], pick[:, 0, :, :], pick[:, 1, :, :], ALU.add)
                fence()
                if m.name == "F2":
                    nc.vector.tensor_tensor(small[:, 0, :], top[:, :, 0], top[:, :, 1], ALU.add)
                    fence()
                    nc.vector.tensor_scalar_add(small[:, 1, :], small[:, 0, :], 1e-9)
                    fence()
                    nc.vector.reciprocal(small[:, 2, :], small[:, 1, :])
                    fence()
                    nc.vector.tensor_tensor(gprob[:], gprob[:], spread(small[:, 2, :], wide, 2), ALU.mult)
                    fence()
                nc.vector.tensor_tensor(gates[:, :, 0:E], gprob[:], pick[:, 0, :, :], ALU.mult)
                fence()

            def experts(m):
                route(m)
                if not m.gated:
                    nc.vector.sem_inc(sig(f"{m.name}_gates_set"), 1)
                nc.vector.memset(acc[:], 0.0)
                fence()
                nc.vector.sem_inc(sig(f"{m.name}_acc_free"), 2)

                def mult(i, g, f):
                    u = g * FC + f
                    dve.wait_ge(sig(f"{m.name}_act_ready"), i * (m.ring * 2 * FC) + (u + 1))
                    nc.vector.tensor_tensor(hid[:, g % 2, f, :], silu[:, f % 2, :], bank[:, 2 + f % 2, :],
                                            ALU.mult).then_inc(sig(f"{m.name}_hid_ready"), 1)

                def gather(i, g):
                    dve.wait_ge(sig(f"{m.name}_down_ready"), i * (2 * m.ring) + (g + 1))
                    for j in range(FC):
                        t = g % 2 * FC + j
                        ins = nc.vector.scalar_tensor_tensor(
                            acc[:, t, :], bank[:, 4 + g % 2, j * P:(j + 1) * P],
                            gates[:, t, bass.ds(i * m.ring + g // 2, 1)], acc[:, t, :], ALU.mult, ALU.add)
                    ins.then_inc(sig(f"{m.name}_acc_free"), 1)
                    fence()

                def round_(i, more):
                    for g in range(2 * m.ring):
                        if m.gated:
                            mult(i, g, 2)
                            mult(i, g, 3)
                            if more or g + 1 < 2 * m.ring:
                                mult(i, g + 1, 0)
                                mult(i, g + 1, 1)
                        gather(i, g)

                if m.gated:
                    mult(0, 0, 0)
                    mult(0, 0, 1)
                with dve.Fori(0, m.rounds - 1) as i:
                    round_(i, True)
                if not m.gated:
                    dve.wait_ge(sig(f"{m.name}_gated_bias_ready"), 1)
                    flat = acc[:].rearrange("p t c -> p (t c)")
                    nc.vector.tensor_tensor(flat, flat, banks(6), ALU.add)
                    fence()
                round_(m.rounds - 1, False)

            dve.wait_ge(sig("x_landed"), 16)
            normalise("A0", x, xn)
            nc.vector.memset(gates[:, :, E], 1.0 / E)
            nc.vector.memset(v0[:], 0.0)
            nc.vector.memset(v3[:], 0.0)
            nc.vector.memset(vself[:, :, :, DH], 1.0)
            fence()
            for v in (v0, v3):
                for i in range(2):
                    nc.vector.memset(v[64 * i:64 * i + 64, :, :, i * VW + DH], 1.0)
            for v, bk, k in ((v0, 3, 1), (v3, 4, 2)):
                dve.wait_ge(sig("values_projected"), k)
                for i in range(2):
                    for b in range(B):
                        src = bank[64 * i:64 * i + 64, bk, b * P:(b + 1) * P].rearrange("p (h c) -> p h c", h=H)
                        nc.vector.tensor_copy(v[64 * i:64 * i + 64, b, :, i * VW:i * VW + DH], src[:, i::2, :])
            dve.wait_ge(sig("values_projected"), 4)
            nc.vector.tensor_copy(v2[:].rearrange("p b c -> p (b c)"), bank[:, 5, :])
            nc.vector.tensor_copy(v1[:].rearrange("p b c -> p (b c)"), bank[:, 6, 0:B * 64])
            fence()
            dve.wait_ge(sig("scalars_spread"), 1)
            nc.vector.tensor_copy(scal[:], bank[:, 7, 0:SCALARS]).then_inc(sig("scalars_copied"), 1)
            dve.wait_ge(sig("scalars_copied"), 1)
            nc.vector.tensor_tensor(lam[:], scal[:, 8:8 + H], scal[:, 8 + H:8 + 2 * H], ALU.subtract)
            fence()
            nc.vector.tensor_scalar_add(lam[:], lam[:], 0.1).then_inc(sig("values_placed"), 1)
            take_transposed("A0")
            dve.wait_ge(sig("keys_copied"), 1)
            for b in range(B):
                nc.vector.tensor_tensor(
                    kblock[:, b * UNIT:(b + 1) * UNIT].rearrange("p (h k) -> p h k", h=H),
                    spread(keyT[:, 0, b * SK:(b + 1) * SK], [P, H, SK], 1), spread(head_of, [P, H, SK], 2),
                    ALU.mult).then_inc(sig("A0m0_keys_spread"), 1)
            dve.wait_ge(sig("mask_landed"), 16)
            nc.vector.tensor_scalar(mask_add[:], mask_raw[:], 1.0, -MASKED, ALU.subtract, ALU.mult)
            nc.vector.tensor_copy(ident_bf[:], ident).then_inc(sig("mask_ready"), 1)
            attend(A0)
            fence()
            h0 = heads[:, 0, :, :].rearrange("p t c -> p (t c)")
            h1 = heads[:, 1, :, :].rearrange("p t c -> p (t c)")
            by_head = "p (t h) c -> p t h c"
            for t in range(T):
                a = heads[:, 1, t, :].rearrange("p (h c) -> p h c", h=H)
                nc.vector.tensor_tensor(a, a, spread(lam[:], [P, H, DH], 2), ALU.mult)
            fence()
            nc.vector.tensor_tensor(h0, h0, h1, ALU.subtract)
            fence()
            nc.vector.tensor_tensor(h1, h0, h0, ALU.mult)
            fence()
            nc.vector.reduce_sum(small[:, 0, :], heads[:, 1, :, :], AX.X)
            fence()
            nc.vector.tensor_scalar(var_eps[:], small[:, 0, :], 1.0 / P, RMS_EPS, ALU.mult, ALU.add).then_inc(
                sig("var_ready"), 1)
            dve.wait_ge(sig("rstd_ready"), POWERS.index("A0rms") + 1)
            nc.vector.tensor_tensor(heads[:, 0, :, :], heads[:, 0, :, :], spread(rstd[:], [P, T, P], 2),
                                    ALU.mult).then_inc(sig("A0_heads_done"), 1)
            dve.wait_ge(sig("f1_landed"), 16)
            nc.vector.tensor_reduce(thr[:, 0:2], f1w[:], AX.X, ALU.add, apply_absolute_value=True).then_inc(
                sig("magnitudes_ready"), 1)
            dve.wait_ge(sig("A0_projected"), 2)
            dve.wait_ge(sig("gates_ready"), 1)
            nc.vector.tensor_scalar_mul(tanh_g[:, 8:9], tanh_g[:, 4:5], 0.5)
            add_gated("A0", tanh_g[:, 0:1], banks(2))
            dve.wait_ge(sig("magnitudes_summed"), 1)
            nc.vector.tensor_scalar(thr[:, 0:2], bank[:, 7, 0:2], 1.0 / (FF * P), ABSMEAN_EPS, ALU.mult, ALU.add)
            fence()
            nc.vector.tensor_scalar_mul(thr[:, 2:4], thr[:, 0:2], 0.5)
            nc.vector.tensor_scalar_mul(thr[:, 4:6], thr[:, 0:2], -0.5).then_inc(sig("thresholds_ready"), 1)

            normalise("F0", x, xn)
            take_transposed("F0")
            experts(F0)
            add_gated("F0", tanh_g[:, 8:9], acc[:].rearrange("p t c -> p (t c)"))
            normalise("A1", x, xn)
            single_head("A1", 64, v1).then_inc(sig("A1_heads_done"), 1)
            dve.wait_ge(sig("A1_projected"), 2)
            for odd in range(2):
                xs = x[:, odd::2, :]
                nc.vector.scalar_tensor_tensor(xs, bank[:, 2 + odd, :].rearrange("p (t c) -> p t c", t=T // 2),
                                               tanh_g[:, 1:2], xs, ALU.mult, ALU.add)
            fence()
            normalise("F1", x, xn)
            take_transposed("F1")
            for t in range(T):
                dve.wait_ge(sig("F1_act_ready"), t + 1)
                nc.vector.bn_stats(stats[:, t, :], hid[:, t // FC, t % FC, :])
            fence()
            for t in range(T):
                nc.vector.bn_aggr(meanvar[:, t, :], stats[:, t, :])
            fence()
            nc.vector.tensor_scalar_add(var_eps[:], meanvar[:, :, 1], LN_EPS).then_inc(sig("var_ready"), 1)
            dve.wait_ge(sig("rstd_ready"), POWERS.index("F1h") + 1)

            def hidden_norm(t):
                h = hid[:, t // FC, t % FC, :]
                nc.vector.tensor_scalar(h, h, meanvar[:, t, 0:1], rstd[:, t:t + 1], ALU.subtract,
                                        ALU.mult).then_inc(sig("F1_hid_normed"), 1)

            hidden_norm(0)
            for t in range(T):
                if t + 1 < T:
                    hidden_norm(t + 1)
                dve.wait_ge(sig("F1_hid_turned"), t + 1)
                for f in range(FC):
                    ins = nc.vector.tensor_scalar(prob[:, t % 2, f * P:(f + 1) * P], bank[:, t % 2, f * P:(f + 1) * P],
                                                  col("F1w", f), col("F1b", f), ALU.mult, ALU.add)
                ins.then_inc(sig("F1_hidT_ready"), 1)
            dve.wait_ge(sig("F1_down_ready"), T)
            add_gated("F1", tanh_g[:, 5:6], banks(4))
            normalise("A2", x, xn)
            single_head("A2", P, v2)
            fence()
            add_gated("A2", tanh_g[:, 2:3], heads[:, 0, :, :].rearrange("p t c -> p (t c)"))
            normalise("F2", x, xn)
            take_transposed("F2")
            experts(F2)
            add_gated("F2", tanh_g[:, 6:7], acc[:].rearrange("p t c -> p (t c)"))
            normalise("A3", x, xn)
            take_transposed("A3")
            attend(A3)
            nc.vector.drain().then_inc(sig("A3_heads_done"), 1)
            dve.wait_ge(sig("A3_projected"), 2)
            add_gated("A3", tanh_g[:, 3:4], banks(2))
            zf = z[:].rearrange("p t c -> p (t c)")
            normalise("F3in", x, z)
            fence()
            normalise("B3", z, xn)
            take_transposed("B3", col("F3g1"), col("F3b1"))
            dve.wait_ge(sig("B3_v_projected"), 1)
            for i in range(2):
                nc.vector.tensor_copy(
                    vself[:, FC * i:FC * i + FC, :, 0:DH],
                    bank[:, 6 + i, :].rearrange("p (t h c) -> p t h c", t=FC, h=H)).then_inc(sig("B3_v_placed"), 1)
            attend(B3)
            nc.vector.drain().then_inc(sig("B3_heads_done"), 1)
            dve.wait_ge(sig("B3_projected"), 2)
            nc.vector.tensor_tensor(zf, zf, banks(2), ALU.add)
            fence()
            normalise("F3", z, xn)
            take_transposed("F3", col("F3g2"), col("F3b2"))
            experts(F3)
            nc.vector.tensor_tensor(zf, zf, acc[:].rearrange("p t c -> p (t c)"), ALU.add)
            fence()
            add_gated("F3", tanh_g[:, 7:8], zf)
            nc.vector.drain().then_inc(sig("x_final"), 1)

        @block.tensor
        def _(pe):
            mm = nc.tensor.matmul

            def turn(name):
                for t in range(T):
                    if t % FC == 0:
                        pe.wait_ge(sig("normed"), 2 * TURNED.index(name) + t // FC + 1)
                    ins = nc.tensor.transpose(bank[:, t // FC, (t % FC) * P:(t % FC + 1) * P], xn[:, t, :], ident)
                    if t % FC == FC - 1:
                        ins.then_inc(sig("turned"), 1)

            def project_T(name, weight, first_bank, what="q", rows_=P):
                for i in range(2):
                    mm(bank[0:rows_, first_bank + i, :], W(weight), xnT[:, i * HALF:(i + 1) * HALF], start=True,
                       stop=True).then_inc(sig(f"{name}_{what}_projected"), 1)

            def attend(a, keys, values):
                def scores(b, j):
                    late, j = divmod(j, a.units)
                    s = j // a.per_slot
                    if j % a.per_slot == 0:
                        pe.wait_ge(sig(f"{a.name}_slot_filled"), b * a.slots + (late * a.slots + s + 1))
                    for c in range(2):
                        at = a.key_at(b, j) + (a.key_at(late, j) - a.key_at(0, j) + c * BANK)
                        dst = bank[:, 2 * (j % 2) + c, :]
                        ins = mm(dst, qslot[:, s, :], kblock[:, bass.ds(at, BANK)], start=True, stop=a is not A3)
                        if a is A3:
                            ins = mm(dst.rearrange("p (h k) -> p h k", k=SK), ident_bf[:],
                                     spread(mask_add[:, a.tile(j) % TPB, :], [P, BANK // SK, SK], 1), start=False, stop=True)
                    ins.then_inc(sig(f"{a.name}_scores_ready"), 1)

                def turn_probs(b, j):
                    pe.wait_ge(sig(f"{a.name}_exp_ready"), b * a.units + (j + 1))
                    for c in range(UNIT // P):
                        ins = nc.tensor.transpose(bank[:, 4 + c // FC, (c % FC) * P:(c % FC + 1) * P],
                                                  prob[:, j % 2, c * P:(c + 1) * P], ident)
                    ins.then_inc(sig(f"{a.name}_probs_turned"), 1)

                def weigh(b, j):
                    pe.wait_ge(sig(f"{a.name}_probT_ready"), b * a.units + (j + 1))
                    pe.wait_ge(sig(f"{a.name}_out_free"), b * a.units + (j + 1))
                    if a is B3:
                        per = S // P
                        for h in range(a.hpu):
                            for k in range(per):
                                o = (h + a.group(j) * a.hpu) * VW
                                v = vself[:].rearrange("p t h c -> p (t h c)")[
                                    :, bass.ds(b * (per * H * VW) + (k * H * VW + o), VW)]
                                c = h * per + k
                                ins = mm(bank[:, 6 + j % 2, h * VW:(h + 1) * VW], probT[:, j % 2, c * P:(c + 1) * P], v,
                                         start=k == 0, stop=k == per - 1)
                    else:
                        flat = a.values[:].rearrange("p b h c -> p (b h c)")
                        for c in range(H // 2):
                            at = (a.tile(j) // TPB * (H // 2) + c) * 2 * VW
                            v = flat[:, bass.ds(b * (a.span * H * VW) + at, 2 * VW)]
                            ins = mm(bank[:, 6 + j % 2, c * 2 * VW:(c + 1) * 2 * VW], probT[:, j % 2, c * P:(c + 1) * P], v,
                                     start=True, stop=True)
                    ins.then_inc(sig(f"{a.name}_out_ready"), 1)

                def round_(b, more):
                    for j in range(a.units):
                        weigh(b, j)
                        if more or j + 1 < a.units:
                            turn_probs(b, j + 1)
                        if more or j + 3 < a.units:
                            scores(b, j + 3)

                keys()
                scores(0, 0)
                scores(0, 1)
                values()
                turn_probs(0, 0)
                scores(0, 2)
                with pe.Fori(0, a.rounds - 1) as b:
                    round_(b, True)
                round_(a.rounds - 1, False)

            def out_project(name, weight, bias):
                pe.wait_ge(sig(f"{name}_heads_done"), 1)
                for t in range(T):
                    ins = nc.tensor.transpose(bank[:, t // FC, (t % FC) * P:(t % FC + 1) * P], heads[:, 0, t, :], ident)
                    if t % FC == FC - 1:
                        ins.then_inc(sig(f"{name}_heads_turned"), 1)
                for i in range(2):
                    dst = bank[:, 2 + i, :]
                    mm(dst.rearrange("p (t c) -> p t c", t=FC), ones_row, spread(row(bias), [1, FC, P], 1),
                       start=True, stop=False)
                    pe.wait_ge(sig(f"{name}_headsT_ready"), i + 1)
                    for j in range(FC):
                        t = i * FC + j
                        ins = mm(dst[:, j * P:(j + 1) * P], headsT[:, t * P:(t + 1) * P], W(weight), start=False,
                                 stop=j == FC - 1)
                    ins.then_inc(sig(f"{name}_projected"), 1)

            def single_head(name, weight, key, width, values, rows_):
                turn(name)
                pe.wait_ge(sig("xnT_ready"), 2 * TURNED.index(name) + 2)
                project_T(name, weight, 2, rows_=rows_)
                for t in range(T):
                    if t % FC == 0:
                        pe.wait_ge(sig(f"{name}_q_copied"), t // FC + 1)
                    b = t // TPB
                    ins = mm(bank[:, 0, t * SK:(t + 1) * SK], qT[0:rows_, 0, t * P:(t + 1) * P],
                             keyT[0:rows_, key, b * SK:(b + 1) * SK], start=True, stop=True)
                ins.then_inc(sig(f"{name}_scores_ready"), 1)
                pe.wait_ge(sig(f"{name}_exp_ready"), 1)
                for c in range(T // 2):
                    ins = nc.tensor.transpose(bank[:, 1, c * P:(c + 1) * P], prob[:, 0, c * P:(c + 1) * P], ident)
                ins.then_inc(sig(f"{name}_probs_turned"), 1)
                pe.wait_ge(sig(f"{name}_probT_ready"), 1)
                for t in range(T):
                    lo = SK * (t % 2)
                    at = t // 2 * width
                    ins = mm(bank[:, 6 + t % 2, at:at + width], probT[lo:lo + SK, 0, (t // 2) * P:(t // 2 + 1) * P],
                             values[lo:lo + SK, t // TPB, :], start=True, stop=True)
                ins.then_inc(sig(f"{name}_out_ready"), 1)

            def experts(m, gate, gate_bias):
                for t in range(T):
                    dst = bank[:, 6, t * E:(t + 1) * E]
                    if gate_bias is not None:
                        mm(dst, ones_row, row(gate_bias), start=True, stop=False)
                    ins = mm(dst, xnT[:, t * P:(t + 1) * P], W(gate), start=gate_bias is None, stop=True)
                ins.then_inc(sig(f"{m.name}_logits_ready"), 1)
                groups = 2 * m.ring
                freed = "hid_ready" if m.gated else "act_ready"

                def up(i, g, f, free=True, later=0):
                    slot = g // 2
                    if f == 0 and g % 2 == 0:
                        pe.wait_ge(sig(f"{m.name}_w{slot}_landed"), (i + later) * 16 + 16)
                    if free:
                        pe.wait_ge(sig(f"{m.name}_{freed}"), (i + later) * (groups * FC) + (g * FC + f - 1))
                    rhs = xnT[:, (g % 2) * HALF:(g % 2 + 1) * HALF]
                    if m.gated:
                        mm(bank[:, 2 + f % 2, :], wring[:, slot, FF + f * P:FF + (f + 1) * P], rhs, start=True, stop=True)
                    mm(bank[:, f % 2, :], wring[:, slot, f * P:(f + 1) * P], rhs, start=True, stop=True).then_inc(
                        sig(f"{m.name}_up_ready"), 1)

                def down(i, g):
                    slot, base = g // 2, (2 if m.gated else 1) * FF
                    pe.wait_ge(sig(f"{m.name}_{freed}"), i * (groups * FC) + (g + 1) * FC)
                    pe.wait_ge(sig(f"{m.name}_acc_free"), i * groups + (g + 1))
                    for j in range(FC):
                        for f in range(FC):
                            ins = mm(bank[:, 4 + g % 2, j * P:(j + 1) * P], hid[:, g % 2, f, j * P:(j + 1) * P],
                                     wring[:, slot, base + f * P:base + (f + 1) * P], start=f == 0, stop=f == FC - 1)
                    ins.then_inc(sig(f"{m.name}_down_ready"), 1)

                def round_(i, more):
                    for g in range(groups):
                        up(i, g, 2)
                        up(i, g, 3)
                        if g + 1 < groups:
                            up(i, g + 1, 0)
                            up(i, g + 1, 1)
                        elif more:
                            up(i, 0, 0, later=1)
                            up(i, 0, 1, later=1)
                        down(i, g)

                up(0, 0, 0, free=False)
                up(0, 0, 1, free=False)
                with pe.Fori(0, m.rounds - 1) as i:
                    round_(i, True)
                if not m.gated:
                    pe.wait_ge(sig(f"{m.name}_gates_set"), 1)
                    for t in range(T):
                        ins = mm(bank[0:E, 6 + t // FC, (t % FC) * P:(t % FC + 1) * P], gates[:, t, 0:E], ident,
                                 start=True, stop=True)
                    ins.then_inc(sig(f"{m.name}_gates_turned"), 1)
                    pe.wait_ge(sig(f"{m.name}_gatesT_ready"), 1)
                    pe.wait_ge(sig("down_bias_landed"), 16)
                    for t in range(T):
                        ins = mm(bank[:, 6 + t // FC, (t % FC) * P:(t % FC + 1) * P], gatesT[:, t * P:(t + 1) * P],
                                 down_bias[:, ("F2", "F3").index(m.name), :], start=True, stop=True)
                    ins.then_inc(sig(f"{m.name}_gated_bias_ready"), 1)
                round_(m.rounds - 1, False)

            pe.wait_ge(sig("const_landed"), 16)
            pe.wait_ge(sig("ctx_landed"), 16)
            pe.wait_ge(sig("w_landed"), 16)
            pe.wait_ge(sig("rows_landed"), 16)
            ctx_keys = ctxT[:, :, 0, :]
            for name, bk, off, r in (("A0k1", 0, 0, P), ("A0k2", 0, 256, P), ("A3k", 1, 0, P), ("A2k", 1, 256, P),
                                     ("A1q", 2, 0, 64)):
                mm(bank[0:r, bk, off:off + B * SK].rearrange("p (b k) -> p b k", b=B), W(name), ctx_keys,
                   start=True, stop=True).then_inc(sig("keys_projected"), 1)
            for name, bk, bias, width in (("A0v", 3, None, P), ("A3v", 4, "A3bv", P), ("A2v", 5, "A2bv", P),
                                          ("A1q", 6, "A1bv", 64)):
                if bias is not None:
                    mm(bank[:, bk, 0:B * width].rearrange("p (b c) -> p b c", b=B), ones_row,
                       spread(row(bias), [1, B, width], 1), start=True, stop=False)
                for b in range(B):
                    ins = mm(bank[:, bk, b * width:(b + 1) * width], ctxT[:, b, :, :].rearrange("p r k -> p (r k)"),
                             W(name), start=bias is None, stop=bias is None or b == B - 1)
                ins.then_inc(sig("values_projected"), 1)
            at = ROWS["gx"][0]
            mm(bank[:, 7, 0:SCALARS], ones_row, rows[0:1, at:at + SCALARS], start=True, stop=True).then_inc(
                sig("scalars_spread"), 1)

            pe.wait_ge(sig("keys_copied"), 5)
            turn("A0")
            pe.wait_ge(sig("xnT_ready"), 2 * TURNED.index("A0") + 2)
            pe.wait_ge(sig("values_placed"), 1)
            project_T("A0", "A0q1", 2)
            project_T("A0", "A0q2", 4)

            def a0_keys():
                pe.wait_ge(sig("A0m0_keys_spread"), B)
                pe.wait_ge(sig("A0m1_keys_spread"), B)

            attend(A0, a0_keys, lambda: None)
            out_project("A0", "A0o", "A0bo")
            pe.wait_ge(sig("magnitudes_ready"), 1)
            mm(bank[:, 7, 0:2], ones_sq, thr[:, 0:2], start=True, stop=True).then_inc(sig("magnitudes_summed"), 1)
            turn("F0")
            pe.wait_ge(sig("xnT_ready"), 2 * TURNED.index("F0") + 2)
            experts(F0, "F0g", None)
            single_head("A1", "A1q", 4, 64, v1, 64)
            pe.wait_ge(sig("A1_heads_done"), 1)
            flat = heads[:, 0, :, :].rearrange("p t c -> p (t c)")
            for c in range(T // 2):
                ins = nc.tensor.transpose(bank[:, c // 2, (c % 2) * P:(c % 2 + 1) * P], flat[:, c * P:(c + 1) * P],
                                          ident)
                if c % 2:
                    ins.then_inc(sig("A1_heads_turned"), 1)
            for odd in range(2):
                dst = bank[:, 2 + odd, :]
                mm(dst.rearrange("p (t c) -> p t c", t=FC), ones_row, spread(row("A1bo"), [1, FC, P], 1),
                   start=True, stop=False)
                pe.wait_ge(sig("A1_headsT_ready"), 2)
                lo, o = 64 * odd, W_COLS["A1o"][0]
                for c in range(T // 2):
                    ins = mm(dst[:, c * P:(c + 1) * P], headsT[lo:lo + 64, c * P:(c + 1) * P],
                             w[lo:lo + 64, o:o + P], start=False, stop=c == T // 2 - 1)
                ins.then_inc(sig("A1_projected"), 1)
            turn("F1")
            pe.wait_ge(sig("f1_ternary"), 1)
            pe.wait_ge(sig("xnT_ready"), 2 * TURNED.index("F1") + 2)
            for t in range(T):
                if t >= 2:
                    pe.wait_ge(sig("F1_act_ready"), t - 1)
                mm(bank[:, 2 + t % 2, :], xnT[:, t * P:(t + 1) * P], f1q[:, 0, :], start=True, stop=True).then_inc(
                    sig("F1_up_ready"), 1)

            def turn_hidden(t):
                pe.wait_ge(sig("F1_hid_normed"), t + 1)
                for f in range(FC):
                    ins = nc.tensor.transpose(bank[:, t % 2, f * P:(f + 1) * P],
                                              hid[:, t // FC, t % FC, f * P:(f + 1) * P], ident)
                ins.then_inc(sig("F1_hid_turned"), 1)

            turn_hidden(0)
            for t in range(T):
                if t + 1 < T:
                    turn_hidden(t + 1)
                pe.wait_ge(sig("F1_hidT_ready"), t + 1)
                for f in range(FC):
                    ins = mm(bank[:, 4 + t // FC, (t % FC) * P:(t % FC + 1) * P], prob[:, t % 2, f * P:(f + 1) * P],
                             f1q[:, 1, f * P:(f + 1) * P], start=f == 0, stop=f == FC - 1)
                ins.then_inc(sig("F1_down_ready"), 1)
            single_head("A2", "A2q", 3, P, v2, P)
            turn("F2")
            pe.wait_ge(sig("xnT_ready"), 2 * TURNED.index("F2") + 2)
            experts(F2, "F2g", "F2gb")
            turn("A3")
            pe.wait_ge(sig("xnT_ready"), 2 * TURNED.index("A3") + 2)
            project_T("A3", "A3q", 2)
            pe.wait_ge(sig("mask_ready"), 1)
            attend(A3, lambda: pe.wait_ge(sig("A3_keys_spread"), B), lambda: None)
            out_project("A3", "A3o", "A3bo")
            turn("B3")
            pe.wait_ge(sig("xnT_ready"), 2 * TURNED.index("B3") + 2)
            project_T("B3", "F3k", 4, what="k")
            project_T("B3", "F3q", 2)
            for i in range(2):
                dst = bank[:, 6 + i, :]
                mm(dst.rearrange("p (t c) -> p t c", t=FC), ones_row, spread(row("F3bv"), [1, FC, P], 1),
                   start=True, stop=False)
                for j in range(FC):
                    t = i * FC + j
                    ins = mm(dst[:, j * P:(j + 1) * P], xnT[:, t * P:(t + 1) * P], W("F3v"), start=False,
                             stop=j == FC - 1)
            ins.then_inc(sig("B3_v_projected"), 1)
            attend(B3, lambda: pe.wait_ge(sig("B3_keys_spread"), B), lambda: pe.wait_ge(sig("B3_v_placed"), 2))
            out_project("B3", "F3o", "F3bo")
            turn("F3")
            pe.wait_ge(sig("xnT_ready"), 2 * TURNED.index("F3") + 2)
            experts(F3, "F3g", "F3gb")


def kernel(**inputs):
    import concourse.bacc as bacc
    from concourse.bass_utils import run_bass_kernel_spmd

    a = {k: np.asarray(v) for k, v in inputs.items()}
    f32 = np.float32

    square = {"A0q1": a["L0_xattn_q1_w"].T, "A0q2": a["L0_xattn_q2_w"].T, "A0k1": a["L0_xattn_kv1_w"][:P].T,
              "A0k2": a["L0_xattn_kv2_w"][:P].T, "A0v": a["L0_xattn_kv1_w"][P:].T, "A0o": a["L0_xattn_proj_w"].T,
              "A3k": a["L3_xattn_wk_w"].T, "A2k": a["L2_xattn_Wk"].T, "A3v": a["L3_xattn_wv_w"].T,
              "A2v": a["L2_xattn_Wv"].T, "A3q": a["L3_xattn_wq_w"].T, "A3o": a["L3_xattn_wo_w"].T,
              "A2q": a["L2_xattn_Wq"].T, "F3q": a["L3_ffn_wq"], "F3k": a["L3_ffn_wk"], "F3v": a["L3_ffn_wv"],
              "F3o": a["L3_ffn_wo"], "A1o": np.concatenate([a["L1_xattn_Wo"]] * 2, 0), "A1q": a["L1_xattn_Wq"],
              "F0g": a["L0_ffn_gate_W"].T, "F2g": a["L2_ffn_gate_w"], "F3g": a["L3_ffn_gate_w"]}
    w_pack = np.zeros((P, W_WIDTH), f32)
    for n, (o, c) in W_COLS.items():
        w_pack[:, o:o + c] = square[n]
    columns = {"A0norm": a["L0_xattn_norm_w"], "A2bq": a["L2_xattn_bq"], "A2bk": a["L2_xattn_bk"],
               "A3bq": a["L3_xattn_wq_b"], "A3bk": a["L3_xattn_wk_b"], "F3bq": a["L3_ffn_bq"], "F3bk": a["L3_ffn_bk"],
               "F3g1": a["L3_ffn_ln1_g"], "F3b1": a["L3_ffn_ln1_b"], "F3g2": a["L3_ffn_ln2_g"],
               "F3b2": a["L3_ffn_ln2_b"], "F1w": a["L1_ffn_ln_w"], "F1b": a["L1_ffn_ln_b"],
               "A1bq": np.concatenate([a["L1_xattn_bq"]] * 2)}
    cols_pack = np.zeros((P, COLS_WIDTH), f32)
    for n, (o, c) in COLS.items():
        cols_pack[:, o:o + c] = columns[n].reshape(c, P).T
    in_rows = {"A0bo": a["L0_xattn_proj_b"], "A1bo": a["L1_xattn_bo"], "A2bv": a["L2_xattn_bv"],
               "A3bv": a["L3_xattn_wv_b"], "A3bo": a["L3_xattn_wo_b"], "F3bv": a["L3_ffn_bv"], "F3bo": a["L3_ffn_bo"],
               "A1bv": a["L1_xattn_bq"], "F2gb": a["L2_ffn_gate_b"], "F3gb": a["L3_ffn_gate_b"], "gx": a["g_xattn"],
               "gf": a["g_ffn"], "lam1": a["L0_xattn_lambda_1"].reshape(-1), "lam2": a["L0_xattn_lambda_2"].reshape(-1)}
    rows_pack = np.zeros((1, ROWS_WIDTH), f32)
    for n, (o, c) in ROWS.items():
        rows_pack[0, o:o + c] = in_rows[n]

    def down_layout(m):
        return m.reshape(-1, FC, P, P).transpose(0, 2, 1, 3).reshape(-1, P, FF)

    shared = [a[f"L0_ffn_{n}_s"].transpose(1, 0, 2).reshape(1, P, FF) for n in ("w1", "w3")]
    moe0 = np.concatenate([
        np.concatenate([a["L0_ffn_w1_e"], a["L0_ffn_w3_e"], down_layout(a["L0_ffn_w2_e"])], 2),
        np.concatenate(shared + [down_layout(a["L0_ffn_w2_s"].reshape(1, FF, P))], 2)], 0)
    moe2, moe3 = (np.concatenate([a[f"{n}_w1"], down_layout(a[f"{n}_w2"]),
                                  a[f"{n}_b1"].reshape(E, FC, P).transpose(0, 2, 1)], 2) for n in ("L2_ffn", "L3_ffn"))
    f1 = np.stack([a["L1_ffn_W_fc"].T, a["L1_ffn_W_proj"].T.reshape(FC, P, P).transpose(1, 0, 2).reshape(P, FF)], 1)

    const = np.zeros((P, C_WIDTH), f32)
    const[:, C_ID:C_ID + P] = np.eye(P, dtype=f32)
    const[:, C_ONES:C_ONES + P] = 1.0
    const[:, C_HEAD:C_HEAD + H] = np.repeat(np.eye(H, dtype=f32), DH, 0)
    const[:, C_IOTA:C_IOTA + E] = np.arange(E, dtype=f32)

    ctx_t = a["ctx_1024"].transpose(2, 0, 1)
    arrays = {
        "x": a["x"].reshape(T, P, P).transpose(1, 0, 2),
        "ctx": np.stack([ctx_t, ctx_t], 2),
        "w": w_pack, "cols": cols_pack, "rows": rows_pack, "const": const,
        "mask": a["mask_1x1xSxS2_bf1"].reshape(TPB, P, SK).transpose(1, 0, 2).view(np.uint8),
        "f1": f1, "moe0": moe0, "moe2": moe2, "moe3": moe3,
        "down_bias": np.stack([a["L2_ffn_b2"], a["L3_ffn_b2"]], 1),
    }
    nc = bacc.Bacc("TRN2", target_bir_lowering=False, num_devices=1)
    feed, args = {}, []
    for name, arr in arrays.items():
        arr = np.ascontiguousarray(arr)
        feed[f"in_{name}"] = arr
        args.append(nc.dram_tensor(f"in_{name}", arr.shape, mybir.dt.from_np(arr.dtype), kind="ExternalInput").ap())
    args.append(nc.dram_tensor("out", (P, T, P), F32, kind="ExternalOutput").ap())
    build(nc, *args)
    r = run_bass_kernel_spmd(nc, [feed], core_ids=[0])
    return r.results[0]["out"].transpose(1, 0, 2).reshape(B, S, P)
```

```python
from contextlib import ExitStack

import numpy as np

import concourse.bass as bass
from concourse import mybir

ALU = mybir.AluOpType
ACT = mybir.ActivationFunctionType
AX = mybir.AxisListType
F32 = mybir.dt.float32
F32R = mybir.dt.float32r
BF16 = mybir.dt.bfloat16
U32 = mybir.dt.uint32
U8 = mybir.dt.uint8

P = 128
B, S, SK = 4, 256, 64
T = B * S // P
TPB = S // P
N = B * S
HALF = N // 2
H, DH = 16, 8
VW = DH + 1
E = 8
FF = 512
FC = FF // P
UNIT = 1024
BANK = 512
RING = 2
ROUND = 2 * RING
LN_EPS = 1e-5
RMS_EPS = 1e-6
ABSMEAN_EPS = 1e-6
MASKED = -1e30

SQUARE = ["A0q1", "A0q2", "A0k1", "A0k2", "A0v", "A0o", "A3k", "A2k", "A3v", "A2v", "A3q", "A3o", "A2q",
          "F3q", "F3k", "F3v", "F3o"]
W_COLS = {n: (P * i, P) for i, n in enumerate(SQUARE)}
_at = P * len(SQUARE)
for _n, _w in (("A1o", P), ("A1q", 64), ("F0g", E), ("F2g", E), ("F3g", E)):
    W_COLS[_n] = (_at, _w)
    _at += _w
W_WIDTH = _at
COLS = {}
_at = 0
for _n, _w in (("A0norm", 1), ("A1bq", 1), ("A2bq", 1), ("A2bk", 1), ("A3bq", 1), ("A3bk", 1), ("F3bq", 1),
               ("F3bk", 1), ("F3g1", 1), ("F3b1", 1), ("F3g2", 1), ("F3b2", 1), ("F1w", FC), ("F1b", FC)):
    COLS[_n] = (_at, _w)
    _at += _w
COLS_WIDTH = _at
ROWS = {}
_at = 0
for _n, _w in (("A0bo", P), ("A1bo", P), ("A2bv", P), ("A3bv", P), ("A3bo", P), ("F3bv", P), ("F3bo", P),
               ("A1bv", 64), ("F2gb", E), ("F3gb", E), ("gx", 4), ("gf", 4), ("lam1", H), ("lam2", H)):
    ROWS[_n] = (_at, _w)
    _at += _w
ROWS_WIDTH = _at
SCALARS = 8 + 2 * H
C_ID, C_ONES, C_HEAD, C_IOTA = 0, P, 2 * P, 2 * P + H
C_WIDTH = 2 * P + H + E
POWERS = ["A0", "A0rms", "F0", "A1", "F1", "F1h", "A2", "F2", "A3", "F3in", "B3", "F3"]
TURNED = ["A0", "F0", "A1", "F1", "A2", "F2", "A3", "B3", "F3"]


def build(nc, x_in, ctx_in, w_in, cols_in, rows_in, const_in, mask_in, f1_in, moe0_in, moe2_in, moe3_in, down_bias_in, out):
    with ExitStack() as ctx:
        def sb(name, shape, dt=F32):
            return ctx.enter_context(nc.sbuf_tensor(name, shape, dt))

        x = sb("x", [P, T, P])
        z = sb("z", [P, T, P])
        f1t = z[:].rearrange("p t c -> p (t c)").rearrange("p (i f) -> p i f", i=2)
        xn = sb("xn", [P, T, P])
        xnT = sb("xnT", [P, N])
        ctxT = sb("ctxT", [P, B, 2, SK])
        w = sb("w", [P, W_WIDTH])
        cols = sb("cols", [P, COLS_WIDTH])
        rows = sb("rows", [1, ROWS_WIDTH])
        const = sb("const", [P, C_WIDTH])
        ident_bf = sb("ident_bf", [P, P], BF16)
        mask_raw = sb("mask_raw", [P, TPB, SK], U8)
        mask_add = sb("mask_add", [P, TPB, SK], BF16)
        f1w = sb("f1w", [P, 2, FF])
        f1q = sb("f1q", [P, 2, FF])
        down_bias = sb("down_bias", [E, 2, P])
        wraw = sb("wraw", [P, RING, 2 * FF])
        whi = sb("whi", [P, RING, 2 * FF], F32R)
        wlo = sb("wlo", [P, RING, 2 * FF], F32R)
        wdown = sb("wdown", [P, RING, FF])
        up_bias = sb("up_bias", [P, RING, FC])
        xhi = sb("xhi", [P, N], F32R)
        xlo = sb("xlo", [P, N], F32R)
        keyT = sb("keyT", [P, 5, B * SK])
        kblock = sb("kblock", [P, 8 * UNIT])
        f1hid = kblock[:, 4 * UNIT:8 * UNIT].rearrange("p (t f) -> p t f", t=T)
        v0 = sb("v0", [P, B, H // 2, 2 * VW])
        v3 = sb("v3", [P, B, H // 2, 2 * VW])
        vself = sb("vself", [P, T, H, VW])
        v2 = sb("v2", [P, B, P])
        v1 = sb("v1", [P, B, 64])
        qT = sb("qT", [P, 2, N])
        qslot = sb("qslot", [P, 4, P])
        prob = sb("prob", [P, 2, UNIT])
        probT = sb("probT", [P, 2, UNIT])
        heads = sb("heads", [P, 2, T, P])
        headsT = heads[:, 1, :, :].rearrange("p t c -> p (t c)")
        hid = kblock[:, 4 * UNIT:8 * UNIT].rearrange("p (g f k) -> p g f k", g=2, f=FC)
        silu = heads[:, 0, :, :].rearrange("p t c -> p (t c)").rearrange("p (f k) -> p f k", f=2)
        acc = prob[:, 0, :].rearrange("p (t c) -> p t c", t=T)
        stats = sb("stats", [P, T, 6])
        meanvar = sb("meanvar", [P, T, 2])
        var_eps = sb("var_eps", [P, T])
        rstd = sb("rstd", [P, T])
        minus_half = sb("minus_half", [P, T])
        rowmax = sb("rowmax", [P, 2, H])
        rsum = sb("rsum", [P, 2, H])
        scal = sb("scal", [P, SCALARS])
        tanh_g = sb("tanh_g", [P, 9])
        lam = sb("lam", [P, H])
        thr = sb("thr", [P, 6])
        logit = sb("logit", [P, T, E])
        gprob = sb("gprob", [P, T, E])
        top = sb("top", [P, T, 8])
        topi = sb("topi", [P, T, 8], U32)
        topf = sb("topf", [P, T, 8])
        pick = sb("pick", [P, 2, T, E])
        small = sb("small", [P, 4, T])
        gates = sb("gates", [P, T, E + 1])
        gatesT = probT[0:E, 0, :]
        bank = ctx.enter_context(nc.psum_tensor("bank", [P, 8, BANK], F32))

        ident = const[:, C_ID:C_ID + P]
        ones_row = const[0:1, C_ONES:C_ONES + P]
        ones_sq = const[:, C_ONES:C_ONES + P]
        head_of = const[:, C_HEAD:C_HEAD + H]
        iota = const[:, C_IOTA:C_IOTA + E]

        def W(name):
            o, n = W_COLS[name]
            return w[:, o:o + n]

        def col(name, i=0):
            o = COLS[name][0] + i
            return cols[:, o:o + 1]

        def row(name):
            o, n = ROWS[name]
            return rows[0:1, o:o + n]

        def banks(i, n=2):
            return bank[:, i:i + n, :].rearrange("p b c -> p (b c)")

        def spread(ap, shape, axis):
            return ap.unsqueeze(axis).broadcast_to(shape)

        made = {}

        def sig(name):
            if name not in made:
                made[name] = ctx.enter_context(nc.semaphore(name))
            return made[name]

        class Attn:
            def __init__(self, name, span, units, slots, maps, heads_per_unit, scale, ones_values):
                self.name, self.units, self.slots, self.maps = name, units, slots, maps
                self.span, self.rounds, self.tiles = span, B // span, span * TPB
                self.hpu, self.kpu = heads_per_unit, UNIT // heads_per_unit
                self.scale, self.values = scale, ones_values
                self.per_slot = units // slots

            def tile(self, j):
                return j * self.tiles // self.units

            def map(self, j):
                return j % self.maps

            def group(self, j):
                return j % (H // self.hpu)

            def key_at(self, r, j):
                if self.name == "A0":
                    return r * (self.span * UNIT) + self.map(j) * B * UNIT
                if self.name == "A3":
                    return r * (self.span * UNIT) + self.tile(j) // TPB * UNIT
                return (r & 1) * (4 * UNIT) + self.group(j) * UNIT

        A0 = Attn("A0", 1, 2 * TPB, 2 * TPB, 2, H, DH ** -0.5, v0)
        A3 = Attn("A3", 2, 2 * TPB, 2 * TPB, 1, H, DH ** -0.5, v3)
        B3 = Attn("B3", 1, 4 * TPB, TPB, 1, 4, DH ** -0.5, vself)

        class Moe:
            def __init__(self, name, experts, func, gated, before):
                self.name, self.experts, self.func, self.gated, self.before = name, experts, func, gated, before
                self.width = 2 * FF if gated else FF
                self.raw = self.width + (0 if gated else FC)
                self.banks = 2 if gated else FC
                self.rounds = (experts - 1) // RING
                self.tail = 2 * (experts - self.rounds * RING)

        F0 = Moe("F0", E + 1, ACT.Silu, True, None)
        F2 = Moe("F2", E, ACT.Gelu, False, F0)
        F3 = Moe("F3", E, ACT.Relu, False, F2)
        def spread_group(g, engine):
            shape = [P, B3.hpu, S]
            return engine.tensor_tensor(
                kblock[:, g * UNIT:(g + 1) * UNIT].rearrange("p (h k) -> p h k", h=B3.hpu),
                spread(qT[:, 1, 0:S], shape, 1), spread(head_of[:, g * B3.hpu:(g + 1) * B3.hpu], shape, 2), ALU.mult)

        moe_dram = {"F0": moe0_in, "F2": moe2_in, "F3": moe3_in}

        block = ctx.enter_context(nc.Block())

        @block.sync
        def _(sp):
            sp.dma_start(const[:], const_in).then_inc(sig("const_landed"), 16)
            sp.dma_start(x[:], x_in).then_inc(sig("x_landed"), 16)
            sp.dma_start(f1w[:], f1_in).then_inc(sig("f1_landed"), 16)
            sp.dma_start(mask_raw[:], mask_in).then_inc(sig("mask_landed"), 16)
            sp.dma_start(down_bias[:], down_bias_in).then_inc(sig("down_bias_landed"), 16)

            def load_expert(m, e, slot):
                sp.dma_start(wraw[:, slot, 0:m.raw], moe_dram[m.name][e, :, 0:m.raw]).then_inc(
                    sig(f"{m.name}_w{slot}_landed"), 16)

            def load_down(m, e, slot):
                sp.dma_start(wdown[:, slot, :], moe_dram[m.name][e, :, m.raw:m.raw + FF]).then_inc(
                    sig(f"{m.name}_down{slot}_landed"), 16)

            def stream_experts(m):
                if m.before is not None:
                    sp.wait_ge(sig(f"{m.before.name}_split"), m.before.experts)
                for r in range(RING):
                    load_expert(m, r, r)
                if m.before is not None:
                    sp.wait_ge(sig(f"{m.before.name}_down_ready"), 2 * m.before.experts)
                for r in range(RING):
                    load_down(m, r, r)
                with sp.Fori(1, m.rounds) as i:
                    for r in range(RING):
                        sp.wait_ge(sig(f"{m.name}_split"), (i - 1) * RING + (r + 1))
                        load_expert(m, bass.ds(i * RING + r, 1), r)
                        sp.wait_ge(sig(f"{m.name}_down_ready"), (i - 1) * ROUND + 2 * (r + 1))
                        load_down(m, bass.ds(i * RING + r, 1), r)
                for r in range(m.tail // 2):
                    sp.wait_ge(sig(f"{m.name}_split"), (m.rounds - 1) * RING + r + 1)
                    load_expert(m, m.rounds * RING + r, r)
                    sp.wait_ge(sig(f"{m.name}_down_ready"), (m.rounds - 1) * ROUND + 2 * (r + 1))
                    load_down(m, m.rounds * RING + r, r)

            stream_experts(F0)
            stream_experts(F2)
            stream_experts(F3)
            for h in range(2):
                tiles = slice(FC * h, FC * (h + 1))
                sp.wait_ge(sig("x_final"), h + 1)
                sp.dma_start(out[:, tiles, :], x[:, tiles, :]).then_inc(sig("out_written"), 16)
            sp.wait_ge(sig("out_written"), 32)

        @block.gpsimd
        def _(pool):
            def power(name):
                for h in range(2):
                    half = slice(FC * h, FC * (h + 1))
                    pool.wait_ge(sig("var_ready"), 2 * POWERS.index(name) + h + 1)
                    nc.gpsimd.tensor_tensor(rstd[:, half], var_eps[:, half], minus_half[:, half], ALU.pow).then_inc(
                        sig("rstd_ready"), 1)

            def block_keys(name, dst, src, width):
                nc.gpsimd.tensor_tensor(
                    kblock[:, bass.ds(dst, H * width)].rearrange("p (h k) -> p h k", h=H),
                    spread(src, [P, H, width], 1), spread(head_of, [P, H, width], 2), ALU.mult,
                ).then_inc(sig(f"{name}_keys_spread"), 1)

            def fill_slots(a, between):
                def fill(b, s):
                    j = s * a.per_slot
                    at = b * (a.tiles * P) + a.tile(j) * P
                    nc.gpsimd.tensor_copy(qslot[:, s, :], qT[:, a.map(j), bass.ds(at, P)]).then_inc(
                        sig(f"{a.name}_slot_filled"), 1)

                pool.wait_ge(sig(f"{a.name}_q_copied"), 2 * a.maps)
                for s in range(a.slots):
                    fill(0, s)
                between()
                with pool.Fori(1, a.rounds) as b:
                    for s in range(a.slots):
                        pool.wait_ge(sig(f"{a.name}_scores_ready"), (b - 1) * a.units + (s + 1) * a.per_slot)
                        fill(b, s)

            def split_expert(m, i, r):
                raw, hi = wraw[:, r, 0:m.width], whi[:, r, 0:m.width]
                pool.wait_ge(sig(f"{m.name}_w{r}_landed"), i * 16 + 16)
                ones = const[:, C_ONES:C_ONES + 1].broadcast_to([P, m.width])
                nc.gpsimd.tensor_tensor(hi, raw, ones, ALU.mult).then_inc(sig(f"{m.name}_hi"), 1)
                if not m.gated:
                    nc.gpsimd.tensor_copy(up_bias[:, r, :], wraw[:, r, m.width:m.width + FC])
                pool.wait_ge(sig(f"{m.name}_hi"), i * RING + (r + 1))
                nc.gpsimd.tensor_tensor(wlo[:, r, 0:m.width], raw, hi.bitcast(F32), ALU.subtract).then_inc(
                    sig(f"{m.name}_split"), 1)

            def split_first(m):
                if m.before is not None:
                    pool.wait_ge(sig(f"{m.before.name}_act_ready"), 2 * FC * m.before.experts)
                for r in range(RING):
                    split_expert(m, 0, r)

            def split_rest(m):
                with pool.Fori(1, m.rounds) as i:
                    for r in range(RING):
                        pool.wait_ge(sig(f"{m.name}_act_ready"), (i - 1) * (ROUND * FC) + 2 * FC * (r + 1))
                        split_expert(m, i, r)
                for r in range(m.tail // 2):
                    pool.wait_ge(sig(f"{m.name}_act_ready"), (m.rounds - 1) * (ROUND * FC) + 2 * FC * (r + 1))
                    split_expert(m, m.rounds, r)

            nc.gpsimd.memset(minus_half[:], -0.5).then_inc(sig("minus_half_set"), 1)
            pool.wait_ge(sig("minus_half_set"), 1)
            power("A0")
            pool.wait_ge(sig("const_landed"), 16)
            pool.wait_ge(sig("keys_copied"), 2)
            for b in range(B):
                block_keys("A0m1", (B + b) * UNIT, keyT[:, 1, b * SK:(b + 1) * SK], SK)
            fill_slots(A0, lambda: split_first(F0))
            power("A0rms")
            power("F0")
            pool.wait_ge(sig("thresholds_ready"), 1)
            for i in range(2):
                nc.gpsimd.tensor_scalar(f1t[:, i, :], f1w[:, i, :], thr[:, 4 + i:5 + i], None, ALU.is_lt)
                nc.gpsimd.tensor_scalar(f1q[:, i, :], f1w[:, i, :], thr[:, 2 + i:3 + i], None, ALU.is_gt).then_inc(
                    sig("f1_compared"), 1)
            pool.wait_ge(sig("f1_compared"), 2)
            nc.gpsimd.tensor_tensor(f1q[:], f1q[:], f1t, ALU.subtract).then_inc(sig("f1_ternary"), 1)
            split_rest(F0)
            power("A1")
            pool.wait_ge(sig("keys_copied"), 5)
            pool.wait_ge(sig("A0_scores_ready"), A0.units * A0.rounds)
            for b in range(B):
                block_keys("A3", b * UNIT, keyT[:, 2, b * SK:(b + 1) * SK], SK)
            split_first(F2)
            power("F1")
            power("F1h")
            power("A2")
            power("F2")
            split_rest(F2)
            power("A3")
            fill_slots(A3, lambda: split_first(F3))
            power("F3in")
            power("B3")
            pool.wait_ge(sig("B3_k_copied"), 1)
            for g in range(2, 4):
                spread_group(g, nc.gpsimd).then_inc(sig("B3_first_keys_pool"), 1)
            pool.wait_ge(sig("B3_q_copied"), 2)

            def fill(b, s):
                nc.gpsimd.tensor_copy(qslot[:, s, :], qT[:, 0, bass.ds(b * S + s * P, P)]).then_inc(
                    sig("B3_slot_filled"), 1)

            fill(0, 0)
            fill(0, 1)
            block_keys("B3", H * S, qT[:, 1, S:2 * S], S)
            pool.wait_ge(sig("B3_k_copied"), 2)
            with pool.Fori(1, B - 1) as b:
                pool.wait_ge(sig("B3_scores_ready"), (b - 1) * B3.units + B3.per_slot)
                fill(b, 0)
                pool.wait_ge(sig("B3_scores_ready"), b * B3.units)
                fill(b, 1)
                block_keys("B3", ((b + 1) & 1) * (H * S), qT[:, 1, bass.ds((b + 1) * S, S)], S)
            pool.wait_ge(sig("B3_scores_ready"), (B - 2) * B3.units + B3.per_slot)
            fill(B - 1, 0)
            pool.wait_ge(sig("B3_scores_ready"), (B - 1) * B3.units)
            fill(B - 1, 1)
            power("F3")
            split_rest(F3)

        @block.scalar
        def _(act):
            act.dma_start(ctxT[:], ctx_in).then_inc(sig("ctx_landed"), 16)
            act.dma_start(w[:], w_in).then_inc(sig("w_landed"), 16)
            act.dma_start(rows[:], rows_in).then_inc(sig("rows_landed"), 16)
            act.dma_start(cols[:], cols_in).then_inc(sig("cols_landed"), 16)

            def copy(dst, src, bias=None, scale=None):
                if bias is None and scale is None:
                    return nc.scalar.copy(dst, src)
                return nc.scalar.activation(dst, src, ACT.Identity, bias=0.0 if bias is None else bias,
                                            scale=1.0 if scale is None else scale)

            def take_transposed(name, gain=None, bias=None):
                act.wait_ge(sig("turned"), 2 * TURNED.index(name) + 1)
                copy(xnT[:, 0:HALF], bank[:, 0, :], bias, gain).then_inc(sig("xnT0_ready"), 1)
                if name in ("F0", "F2", "F3"):
                    copy(xhi[:, 0:HALF], bank[:, 0, :], bias, gain).then_inc(sig("xhi_ready"), 1)

            def take_queries(name, m, first_bank, bias=None, what="q", rows_=P):
                for i in range(2):
                    act.wait_ge(sig(f"{name}_{what}_projected"), 2 * m + i + 1 if what == "q" else i + 1)
                    slot = 1 if what == "k" else m
                    copy(qT[0:rows_, slot, i * HALF:(i + 1) * HALF], bank[0:rows_, first_bank + i, :], bias).then_inc(
                        sig(f"{name}_{what}_copied"), 1)

            def attend(a):
                def exps(b, j):
                    act.wait_ge(sig(f"{a.name}_shifted"), b * a.units + (j + 1))
                    nc.scalar.activation(prob[:, j % 2, :], prob[:, j % 2, :], ACT.Exp, scale=a.scale).then_inc(
                        sig(f"{a.name}_exp_ready"), 1)

                def take(b, j):
                    act.wait_ge(sig(f"{a.name}_probs_turned"), b * a.units + (j + 1))
                    nc.scalar.copy(probT[:, j % 2, :], banks(4)).then_inc(sig(f"{a.name}_probT_ready"), 1)

                def round_(b, more):
                    for j in range(a.units):
                        take(b, j)
                        if more or j + 1 < a.units:
                            exps(b, j + 1)

                exps(0, 0)
                with act.Fori(0, a.rounds - 1) as b:
                    round_(b, True)
                round_(a.rounds - 1, False)

            def take_heads(name, scale=None):
                for i in range(2):
                    act.wait_ge(sig(f"{name}_heads_turned"), i + 1)
                    copy(headsT[:, i * HALF:(i + 1) * HALF], bank[:, i, :], None, scale).then_inc(
                        sig(f"{name}_headsT_ready"), 1)

            def single_head(name, m_rows, bias, scale):
                take_transposed(name)
                take_queries(name, 0, 2, bias[0:m_rows], rows_=m_rows)
                act.wait_ge(sig(f"{name}_shifted"), 1)
                nc.scalar.activation(prob[:, 0, 0:T * SK], prob[:, 0, 0:T * SK], ACT.Exp, scale=scale).then_inc(
                    sig(f"{name}_exp_ready"), 1)
                act.wait_ge(sig(f"{name}_probs_turned"), 1)
                nc.scalar.copy(probT[:, 0, 0:BANK], bank[:, 1, :]).then_inc(sig(f"{name}_probT_ready"), 1)

            def experts(m):
                if m.name != "F3":
                    act.wait_ge(sig(f"{m.name}_logits_shifted"), 1)
                    nc.scalar.activation(gprob[:], gprob[:], ACT.Exp).then_inc(sig(f"{m.name}_gate_exp_ready"), 1)

                def unit(i, u):
                    g, f = divmod(u, FC)
                    act.wait_ge(sig(f"{m.name}_up_ready"), i * (ROUND * FC) + (u + 1))
                    dst = silu[:, f % 2, :] if m.gated else hid[:, g % 2, f, :]
                    bias = {} if m.gated else {"bias": up_bias[:, g // 2 % RING, f:f + 1]}
                    nc.scalar.activation(dst, bank[:, f % m.banks, :], m.func, **bias).then_inc(
                        sig(f"{m.name}_act_ready"), 1)

                with act.Fori(0, m.rounds) as i:
                    for u in range(ROUND * FC):
                        unit(i, u)
                unit(m.rounds, 0)
                unit(m.rounds, 1)
                if not m.gated:
                    act.wait_ge(sig(f"{m.name}_gates_turned"), 1)
                    nc.scalar.copy(gatesT, banks(6)[0:E, :]).then_inc(sig(f"{m.name}_gatesT_ready"), 1)
                for u in range(2, m.tail * FC):
                    unit(m.rounds, u)

            act.wait_ge(sig("cols_landed"), 16)
            for i, (bk, off, bias, r) in enumerate([(0, 0, None, P), (0, 256, None, P), (1, 0, "A3bk", P),
                                                    (1, 256, "A2bk", P), (2, 0, "A1bq", 64)]):
                act.wait_ge(sig("keys_projected"), (2, 2, 4, 4, 5)[i])
                copy(keyT[0:r, i, :], bank[0:r, bk, off:off + B * SK], None if bias is None else col(bias)[0:r]
                     ).then_inc(sig("keys_copied"), 1)
            act.wait_ge(sig("scalars_copied"), 1)
            nc.scalar.activation(tanh_g[:, 0:8], scal[:, 0:8], ACT.Tanh).then_inc(sig("gates_ready"), 1)

            take_transposed("A0")
            take_queries("A0", 0, 2)
            take_queries("A0", 1, 4)
            attend(A0)
            take_heads("A0", col("A0norm"))
            take_transposed("F0")
            experts(F0)
            single_head("A1", 64, col("A1bq"), float(np.float32(1.0) / np.sqrt(np.float32(P))))
            for i in range(2):
                act.wait_ge(sig("A1_heads_turned"), i + 1)
                nc.scalar.copy(headsT[:, i * 256:(i + 1) * 256], bank[:, i, 0:256]).then_inc(
                    sig("A1_headsT_ready"), 1)
            take_transposed("F1")
            for t in range(T):
                act.wait_ge(sig("F1_up_ready"), t + 1)
                nc.scalar.activation(f1hid[:, t, :], bank[:, 2 + t % 2, :], ACT.Gelu).then_inc(
                    sig("F1_act_ready"), 1)
            for t in range(T):
                act.wait_ge(sig("F1_hid_turned"), t + 1)
                for f in range(FC):
                    at = slice(f * P, (f + 1) * P)
                    ins = copy(prob[:, t % 2, at], bank[:, t % 2, at], col("F1b", f), col("F1w", f))
                ins.then_inc(sig("F1_hidT_ready"), 1)
            single_head("A2", P, col("A2bq"), 1.0)
            take_transposed("F2")
            experts(F2)
            take_transposed("A3")
            take_queries("A3", 0, 2, col("A3bq"))
            attend(A3)
            take_heads("A3")
            take_transposed("B3", col("F3g1"), col("F3b1"))
            take_queries("B3", 0, 4, col("F3bk"), what="k")
            take_queries("B3", 0, 2, col("F3bq"))
            attend(B3)
            take_heads("B3")
            take_transposed("F3", col("F3g2"), col("F3b2"))
            experts(F3)

        @block.vector
        def _(dve):
            fence = nc.vector.drain

            def variances(h):
                tiles = slice(FC * h, FC * (h + 1))
                nc.vector.tensor_scalar_add(var_eps[:, tiles], meanvar[:, tiles, 1], LN_EPS).then_inc(sig("var_ready"), 1)

            def normalise(name, src, dst, update=lambda h: None):
                for h in range(2):
                    update(h)
                    for t in range(FC * h, FC * (h + 1)):
                        nc.vector.bn_stats(stats[:, t, :], src[:, t, :])
                    fence()
                    for t in range(FC * h, FC * (h + 1)):
                        nc.vector.bn_aggr(meanvar[:, t, :], stats[:, t, :])
                    fence()
                    variances(h)
                for h in range(2):
                    dve.wait_ge(sig("rstd_ready"), 2 * POWERS.index(name) + h + 1)
                    for t in range(FC * h, FC * (h + 1)):
                        ins = nc.vector.tensor_scalar(dst[:, t, :], src[:, t, :], meanvar[:, t, 0:1], rstd[:, t:t + 1],
                                                      ALU.subtract, ALU.mult)
                    if name in TURNED:
                        ins.then_inc(sig("normed"), 1)

            def take_transposed(name, gain=None, bias=None):
                dve.wait_ge(sig("turned"), 2 * TURNED.index(name) + 2)
                if gain is None:
                    ins = nc.vector.tensor_copy(xnT[:, HALF:N], bank[:, 1, :])
                else:
                    ins = nc.vector.tensor_scalar(xnT[:, HALF:N], bank[:, 1, :], gain, bias, ALU.mult, ALU.add)
                ins.then_inc(sig("xnT1_ready"), 1)
                if name in ("F0", "F2", "F3"):
                    dve.wait_ge(sig("xhi_ready"), ("F0", "F2", "F3").index(name) + 1)
                    nc.vector.tensor_tensor(xlo[:, 0:HALF], xnT[:, 0:HALF], xhi[:, 0:HALF].bitcast(F32),
                                            ALU.subtract).then_inc(sig("x_split"), 1)
                    fence()
                    nc.vector.tensor_copy(xhi[:, HALF:N], xnT[:, HALF:N])
                    fence()
                    nc.vector.tensor_tensor(xlo[:, HALF:N], xnT[:, HALF:N], xhi[:, HALF:N].bitcast(F32),
                                            ALU.subtract).then_inc(sig("x_split"), 1)

            def attend(a):
                nc.vector.sem_inc(sig(f"{a.name}_out_free"), 2)

                def shift(b, j):
                    sc = banks(2 * (j % 2)).rearrange("p (h k) -> p h k", h=a.hpu)
                    dve.wait_ge(sig(f"{a.name}_scores_ready"), b * a.units + (j + 1))
                    nc.vector.reduce_max(rowmax[:, j % 2, 0:a.hpu], sc, AX.X)
                    fence()
                    nc.vector.tensor_tensor(prob[:, j % 2, :].rearrange("p (h k) -> p h k", h=a.hpu), sc,
                                            spread(rowmax[:, j % 2, 0:a.hpu], [P, a.hpu, a.kpu], 2),
                                            ALU.subtract).then_inc(sig(f"{a.name}_shifted"), 1)

                def take(b, j):
                    o = bank[:, 6 + j % 2, 0:a.hpu * VW].rearrange("p (h c) -> p h c", h=a.hpu)
                    dve.wait_ge(sig(f"{a.name}_out_ready"), b * a.units + (j + 1))
                    nc.vector.reciprocal(rsum[:, j % 2, 0:a.hpu], o[:, :, DH])
                    fence()
                    if a.map(j) == 1:
                        nc.vector.tensor_tensor(rsum[:, 1, :], rsum[:, 1, :], lam[:], ALU.mult)
                        fence()
                    width = a.hpu * DH
                    dst = heads[:, a.map(j), :, :].rearrange("p t c -> p (t c)")[
                        :, bass.ds(b * (a.tiles * P) + (a.tile(j) * P + a.group(j) % (P // width) * width), width)]
                    nc.vector.tensor_tensor(dst.rearrange("p (h c) -> p h c", h=a.hpu), o[:, :, 0:DH],
                                            spread(rsum[:, j % 2, 0:a.hpu], [P, a.hpu, DH], 2),
                                            ALU.mult).then_inc(sig(f"{a.name}_out_free"), 1)
                    if a.map(j) == 1:
                        fence()
                        at = bass.ds(b * (a.tiles * P) + a.tile(j) * P, P)
                        first, second = (heads[:, m, :, :].rearrange("p t c -> p (t c)")[:, at] for m in range(2))
                        nc.vector.tensor_tensor(first, first, second, ALU.subtract)
                        fence()
                        nc.vector.bn_stats(stats[:].rearrange("p t s -> p (t s)")[
                            :, bass.ds(b * (a.tiles * 6) + a.tile(j) * 6, 6)], first)

                def round_(b, more):
                    for j in range(a.units):
                        if more or j + 2 < a.units:
                            shift(b, j + 2)
                        take(b, j)

                shift(0, 0)
                shift(0, 1)
                with dve.Fori(0, a.rounds - 1) as b:
                    round_(b, True)
                round_(a.rounds - 1, False)

            def flat(a, h=None):
                a = a.rearrange("p t c -> p (t c)")
                return a if h is None else a[:, h * HALF:(h + 1) * HALF]

            def add_gated(gate, src, h, dst=x):
                nc.vector.scalar_tensor_tensor(flat(dst[:], h), src, gate, flat(dst[:], h), ALU.mult, ALU.add)
                fence()

            def single_head(name, width, values_dup):
                take_transposed(name)
                sc = bank[:, 0, :].rearrange("p (t k) -> p t k", t=T)
                pr = prob[:, 0, 0:T * SK].rearrange("p (t k) -> p t k", t=T)
                dve.wait_ge(sig(f"{name}_scores_ready"), 1)
                nc.vector.reduce_max(rowmax[:, 0, 0:T], sc, AX.X)
                fence()
                nc.vector.tensor_tensor(pr, sc, spread(rowmax[:, 0, 0:T], [P, T, SK], 2), ALU.subtract).then_inc(
                    sig(f"{name}_shifted"), 1)
                dve.wait_ge(sig(f"{name}_exp_ready"), 1)
                nc.vector.reduce_sum(rsum[:, 0, 0:T], pr, AX.X)
                fence()
                nc.vector.reciprocal(rsum[:, 1, 0:T], rsum[:, 0, 0:T])
                fence()
                dve.wait_ge(sig(f"{name}_out_ready"), 1)

            def single_output(h, width):
                dst = heads[:].rearrange("p m t c -> p (m t c)")[:, 0:T * width].rearrange("p (t c) -> p t c", t=T)
                for odd in range(2):
                    o = bank[:, 6 + odd, h * 2 * width:(h + 1) * 2 * width].rearrange("p (t c) -> p t c", t=2)
                    tiles = slice(FC * h + odd, FC * (h + 1), 2)
                    ins = nc.vector.tensor_tensor(dst[:, tiles, :], o, spread(rsum[:, 1, tiles], [P, 2, width], 2), ALU.mult)
                return ins

            def route(m):
                lg = bank[:, 6, 0:T * E].rearrange("p (t e) -> p t e", t=T)
                wide = [P, T, E]
                dve.wait_ge(sig(f"{m.name}_logits_ready"), 1)
                if m.name == "F3":
                    nc.vector.tensor_copy(gprob[:], lg)
                    fence()
                else:
                    nc.vector.reduce_max(small[:, 0, :], lg, AX.X)
                    fence()
                    nc.vector.tensor_tensor(gprob[:], lg, spread(small[:, 0, :], wide, 2), ALU.subtract).then_inc(
                        sig(f"{m.name}_logits_shifted"), 1)
                    dve.wait_ge(sig(f"{m.name}_gate_exp_ready"), 1)
                    nc.vector.reduce_sum(small[:, 1, :], gprob[:], AX.X)
                    fence()
                    nc.vector.reciprocal(small[:, 2, :], small[:, 1, :])
                    fence()
                    nc.vector.tensor_tensor(gprob[:], gprob[:], spread(small[:, 2, :], wide, 2), ALU.mult)
                    fence()
                for t in range(T):
                    nc.vector.max(top[:, t, :], gprob[:, t, :])
                fence()
                for t in range(T):
                    nc.vector.max_index(topi[:, t, :], top[:, t, :], gprob[:, t, :])
                fence()
                nc.vector.tensor_copy(topf[:], topi[:])
                fence()
                iotas = spread(iota, wide, 1)
                if m.name == "F3":
                    nc.vector.tensor_tensor(gates[:, :, 0:E], iotas, topf[:, :, 0:1].broadcast_to(wide), ALU.is_equal)
                    fence()
                    return
                for k in range(2):
                    nc.vector.tensor_tensor(pick[:, k, :, :], iotas, topf[:, :, k:k + 1].broadcast_to(wide), ALU.is_equal)
                fence()
                nc.vector.tensor_tensor(pick[:, 0, :, :], pick[:, 0, :, :], pick[:, 1, :, :], ALU.add)
                fence()
                if m.name == "F2":
                    nc.vector.tensor_tensor(small[:, 0, :], top[:, :, 0], top[:, :, 1], ALU.add)
                    fence()
                    nc.vector.tensor_scalar_add(small[:, 1, :], small[:, 0, :], 1e-9)
                    fence()
                    nc.vector.reciprocal(small[:, 2, :], small[:, 1, :])
                    fence()
                    nc.vector.tensor_tensor(gprob[:], gprob[:], spread(small[:, 2, :], wide, 2), ALU.mult)
                    fence()
                nc.vector.tensor_tensor(gates[:, :, 0:E], gprob[:], pick[:, 0, :, :], ALU.mult)
                fence()

            def experts(m, between=lambda: None):
                nc.vector.memset(acc, 0.0)
                route(m)
                if not m.gated:
                    nc.vector.sem_inc(sig(f"{m.name}_gates_set"), 1)
                between()
                nc.vector.sem_inc(sig(f"{m.name}_acc_free"), 2)

                def mult(i, u):
                    g, f = divmod(u, FC)
                    dve.wait_ge(sig(f"{m.name}_act_ready"), i * (ROUND * FC) + (u + 1))
                    nc.vector.tensor_tensor(hid[:, g % 2, f, :], silu[:, f % 2, :], bank[:, 2 + f % 2, :],
                                            ALU.mult).then_inc(sig(f"{m.name}_mult_ready"), 1)

                def gather(i, g):
                    dve.wait_ge(sig(f"{m.name}_down_ready"), i * ROUND + (g + 1))
                    for j in range(FC):
                        t = g % 2 * FC + j
                        ins = nc.vector.scalar_tensor_tensor(
                            acc[:, t, :], bank[:, 4 + g % 2, j * P:(j + 1) * P],
                            gates[:, t, bass.ds(i * RING + g // 2, 1)], acc[:, t, :], ALU.mult, ALU.add)
                    ins.then_inc(sig(f"{m.name}_acc_free"), 1)
                    fence()

                def round_(i, groups, more, last=True):
                    for g in range(groups):
                        if m.gated:
                            for u in range(g * FC + 2, g * FC + 2 + FC):
                                if u < (groups + more) * FC:
                                    mult(i, u)
                        if last or g + 1 < groups:
                            gather(i, g)
                        if not last and g == 1 and not m.gated:
                            dve.wait_ge(sig(f"{m.name}_gated_bias_ready"), 1)
                            nc.vector.tensor_tensor(flat(acc), flat(acc), banks(6), ALU.add)
                            fence()

                if m.gated:
                    mult(0, 0)
                    mult(0, 1)
                with dve.Fori(0, m.rounds) as i:
                    round_(i, ROUND, 1)
                round_(m.rounds, m.tail, 0, last=False)

                def finish():
                    gather(m.rounds, m.tail - 1)

                return finish

            dve.wait_ge(sig("x_landed"), 16)
            normalise("A0", x, xn)
            nc.vector.memset(gates[:, :, E], 1.0 / E)
            nc.vector.memset(v0[:], 0.0)
            nc.vector.memset(v3[:], 0.0)
            nc.vector.memset(vself[:, :, :, DH], 1.0)
            fence()
            for v in (v0, v3):
                for i in range(2):
                    nc.vector.memset(v[64 * i:64 * i + 64, :, :, i * VW + DH], 1.0)
            for v, bk, k in ((v0, 3, 1), (v3, 4, 2)):
                dve.wait_ge(sig("values_projected"), k)
                for i in range(2):
                    for b in range(B):
                        src = bank[64 * i:64 * i + 64, bk, b * P:(b + 1) * P].rearrange("p (h c) -> p h c", h=H)
                        nc.vector.tensor_copy(v[64 * i:64 * i + 64, b, :, i * VW:i * VW + DH], src[:, i::2, :])
            dve.wait_ge(sig("values_projected"), 4)
            nc.vector.tensor_copy(v2[:].rearrange("p b c -> p (b c)"), bank[:, 5, :])
            nc.vector.tensor_copy(v1[:].rearrange("p b c -> p (b c)"), bank[:, 6, 0:B * 64])
            fence()
            dve.wait_ge(sig("scalars_spread"), 1)
            nc.vector.tensor_copy(scal[:], bank[:, 7, 0:SCALARS]).then_inc(sig("scalars_copied"), 1)
            dve.wait_ge(sig("scalars_copied"), 1)
            nc.vector.tensor_tensor(lam[:], scal[:, 8:8 + H], scal[:, 8 + H:8 + 2 * H], ALU.subtract)
            fence()
            nc.vector.tensor_scalar_add(lam[:], lam[:], 0.1).then_inc(sig("values_placed"), 1)
            take_transposed("A0")
            dve.wait_ge(sig("keys_copied"), 1)
            for b in range(B):
                nc.vector.tensor_tensor(
                    kblock[:, b * UNIT:(b + 1) * UNIT].rearrange("p (h k) -> p h k", h=H),
                    spread(keyT[:, 0, b * SK:(b + 1) * SK], [P, H, SK], 1), spread(head_of, [P, H, SK], 2),
                    ALU.mult).then_inc(sig("A0m0_keys_spread"), 1)
            dve.wait_ge(sig("mask_landed"), 16)
            nc.vector.tensor_scalar(mask_add[:], mask_raw[:], 1.0, -MASKED, ALU.subtract, ALU.mult)
            nc.vector.tensor_copy(ident_bf[:], ident).then_inc(sig("mask_ready"), 1)
            attend(A0)
            fence()
            for h in range(2):
                for t in range(FC * h, FC * (h + 1)):
                    nc.vector.bn_aggr(meanvar[:, t, :], stats[:, t, :])
                fence()
                tiles = slice(FC * h, FC * (h + 1))
                nc.vector.tensor_tensor(small[:, 0, tiles], meanvar[:, tiles, 0], meanvar[:, tiles, 0], ALU.mult)
                fence()
                nc.vector.scalar_tensor_tensor(var_eps[:, tiles], small[:, 0, tiles], RMS_EPS, meanvar[:, tiles, 1], ALU.add,
                                               ALU.add).then_inc(sig("var_ready"), 1)
            for h in range(2):
                tiles = slice(FC * h, FC * (h + 1))
                dve.wait_ge(sig("rstd_ready"), 2 * POWERS.index("A0rms") + h + 1)
                nc.vector.tensor_tensor(heads[:, 0, tiles, :], heads[:, 0, tiles, :], spread(rstd[:, tiles], [P, FC, P], 2),
                                        ALU.mult).then_inc(sig("A0_heads_done"), 1)
            dve.wait_ge(sig("f1_landed"), 16)
            nc.vector.tensor_reduce(thr[:, 0:2], f1w[:], AX.X, ALU.add, apply_absolute_value=True).then_inc(
                sig("magnitudes_ready"), 1)
            dve.wait_ge(sig("gates_ready"), 1)
            nc.vector.tensor_scalar_mul(tanh_g[:, 8:9], tanh_g[:, 4:5], 0.5)

            def attended(name, gate):
                def update(h):
                    dve.wait_ge(sig(f"{name}_projected"), h + 1)
                    add_gated(gate, bank[:, 2 + h, :], h)
                return update

            def mixed(finish, gate):
                def update(h):
                    if h == 1:
                        finish()
                    add_gated(gate, flat(acc, h), h)
                return update

            normalise("F0", x, xn, attended("A0", tanh_g[:, 0:1]))
            dve.wait_ge(sig("magnitudes_summed"), 1)
            nc.vector.tensor_scalar(thr[:, 0:2], bank[:, 7, 0:2], 1.0 / (FF * P), ABSMEAN_EPS, ALU.mult, ALU.add)
            fence()
            nc.vector.tensor_scalar_mul(thr[:, 2:4], thr[:, 0:2], 0.5)
            nc.vector.tensor_scalar_mul(thr[:, 4:6], thr[:, 0:2], -0.5).then_inc(sig("thresholds_ready"), 1)
            take_transposed("F0")
            finish = experts(F0)
            normalise("A1", x, xn, mixed(finish, tanh_g[:, 8:9]))
            single_head("A1", 64, v1)
            single_output(0, 64)
            single_output(1, 64).then_inc(sig("A1_heads_done"), 1)

            def a1_update(h):
                if h == 0:
                    dve.wait_ge(sig("A1_projected"), 2)
                for odd in range(2):
                    xs = x[:, FC * h + odd:FC * (h + 1):2, :]
                    src = bank[:, 2 + odd, h * 2 * P:(h + 1) * 2 * P].rearrange("p (t c) -> p t c", t=2)
                    nc.vector.scalar_tensor_tensor(xs, src, tanh_g[:, 1:2], xs, ALU.mult, ALU.add)
                fence()
            normalise("F1", x, xn, a1_update)
            take_transposed("F1")
            for h in range(2):
                for t in range(FC * h, FC * (h + 1)):
                    dve.wait_ge(sig("F1_act_ready"), t + 1)
                    nc.vector.bn_stats(stats[:, t, :], f1hid[:, t, :])
                fence()
                for t in range(FC * h, FC * (h + 1)):
                    nc.vector.bn_aggr(meanvar[:, t, :], stats[:, t, :])
                fence()
                variances(h)
            for t in range(T):
                if t % FC == 0:
                    dve.wait_ge(sig("rstd_ready"), 2 * POWERS.index("F1h") + t // FC + 1)
                hidden = f1hid[:, t, :]
                nc.vector.tensor_scalar(hidden, hidden, meanvar[:, t, 0:1], rstd[:, t:t + 1], ALU.subtract,
                                        ALU.mult).then_inc(sig("F1_hid_normed"), 1)

            def f1_update(h):
                dve.wait_ge(sig("F1_down_ready"), FC * (h + 1))
                add_gated(tanh_g[:, 5:6], bank[:, 4 + h, :], h)
            normalise("A2", x, xn, f1_update)
            single_head("A2", P, v2)

            def a2_update(h):
                single_output(h, P)
                fence()
                add_gated(tanh_g[:, 2:3], flat(heads[:, 0, :, :], h), h)
            normalise("F2", x, xn, a2_update)
            take_transposed("F2")
            finish = experts(F2)
            normalise("A3", x, xn, mixed(finish, tanh_g[:, 6:7]))
            take_transposed("A3")
            attend(A3)
            nc.vector.drain().then_inc(sig("A3_heads_done"), 2)
            normalise("F3in", x, z, attended("A3", tanh_g[:, 3:4]))
            fence()
            normalise("B3", z, xn)
            take_transposed("B3", col("F3g1"), col("F3b1"))
            dve.wait_ge(sig("B3_k_copied"), 1)
            for g in range(2):
                spread_group(g, nc.vector).then_inc(sig("B3_first_keys_dve"), 1)
            dve.wait_ge(sig("B3_v_projected"), 1)
            for i in range(2):
                nc.vector.tensor_copy(
                    vself[:, FC * i:FC * i + FC, :, 0:DH],
                    bank[:, 6 + i, :].rearrange("p (t h c) -> p t h c", t=FC, h=H)).then_inc(sig("B3_v_placed"), 1)
            attend(B3)
            nc.vector.drain().then_inc(sig("B3_heads_done"), 2)

            def b3_update(h):
                dve.wait_ge(sig("B3_projected"), h + 1)
                nc.vector.tensor_tensor(flat(z[:], h), flat(z[:], h), bank[:, 2 + h, :], ALU.add)
                fence()

            normalise("F3", z, xn, b3_update)
            take_transposed("F3", col("F3g2"), col("F3b2"))

            def add_stream():
                for h in range(2):
                    add_gated(tanh_g[:, 7:8], flat(z[:], h), h)

            final = mixed(experts(F3, add_stream), tanh_g[:, 7:8])
            for h in range(2):
                final(h)
                nc.vector.drain().then_inc(sig("x_final"), 1)
        @block.tensor
        def _(pe):
            mm = nc.tensor.matmul

            def turn(name):
                for t in range(T):
                    if t % FC == 0:
                        pe.wait_ge(sig("normed"), 2 * TURNED.index(name) + t // FC + 1)
                    ins = nc.tensor.transpose(bank[:, t // FC, (t % FC) * P:(t % FC + 1) * P], xn[:, t, :], ident)
                    if t % FC == FC - 1:
                        ins.then_inc(sig("turned"), 1)

            def turned_half(name, i):
                pe.wait_ge(sig(f"xnT{i}_ready"), TURNED.index(name) + 1)

            def project_T(name, weight, first_bank, what="q", rows_=P):
                for i in range(2):
                    turned_half(name, i)
                    mm(bank[0:rows_, first_bank + i, :], W(weight), xnT[:, i * HALF:(i + 1) * HALF], start=True,
                       stop=True).then_inc(sig(f"{name}_{what}_projected"), 1)

            def attend(a, keys, values):
                def scores(b, j):
                    late, j = divmod(j, a.units)
                    s = j // a.per_slot
                    if j % a.per_slot == 0:
                        pe.wait_ge(sig(f"{a.name}_slot_filled"), b * a.slots + (late * a.slots + s + 1))
                    if a is B3 and late and j == 0:
                        pe.wait_ge(sig("B3_keys_spread"), b + 1)
                    for c in range(2):
                        at = a.key_at(b + late, j) + c * BANK
                        dst = bank[:, 2 * (j % 2) + c, :]
                        ins = mm(dst, qslot[:, s, :], kblock[:, bass.ds(at, BANK)], start=True, stop=a is not A3)
                        if a is A3:
                            ins = mm(dst.rearrange("p (h k) -> p h k", k=SK), ident_bf[:],
                                     spread(mask_add[:, a.tile(j) % TPB, :], [P, BANK // SK, SK], 1), start=False, stop=True)
                    ins.then_inc(sig(f"{a.name}_scores_ready"), 1)

                def turn_probs(b, j):
                    pe.wait_ge(sig(f"{a.name}_exp_ready"), b * a.units + (j + 1))
                    for c in range(UNIT // P):
                        ins = nc.tensor.transpose(bank[:, 4 + c // FC, (c % FC) * P:(c % FC + 1) * P],
                                                  prob[:, j % 2, c * P:(c + 1) * P], ident)
                    ins.then_inc(sig(f"{a.name}_probs_turned"), 1)

                def weigh(b, j):
                    pe.wait_ge(sig(f"{a.name}_probT_ready"), b * a.units + (j + 1))
                    pe.wait_ge(sig(f"{a.name}_out_free"), b * a.units + (j + 1))
                    if a is B3:
                        per = S // P
                        for h in range(a.hpu):
                            for k in range(per):
                                o = (h + a.group(j) * a.hpu) * VW
                                v = vself[:].rearrange("p t h c -> p (t h c)")[
                                    :, bass.ds(b * (per * H * VW) + (k * H * VW + o), VW)]
                                c = h * per + k
                                ins = mm(bank[:, 6 + j % 2, h * VW:(h + 1) * VW], probT[:, j % 2, c * P:(c + 1) * P], v,
                                         start=k == 0, stop=k == per - 1)
                    else:
                        flat = a.values[:].rearrange("p b h c -> p (b h c)")
                        for c in range(H // 2):
                            at = (a.tile(j) // TPB * (H // 2) + c) * 2 * VW
                            v = flat[:, bass.ds(b * (a.span * H * VW) + at, 2 * VW)]
                            ins = mm(bank[:, 6 + j % 2, c * 2 * VW:(c + 1) * 2 * VW], probT[:, j % 2, c * P:(c + 1) * P], v,
                                     start=True, stop=True)
                    ins.then_inc(sig(f"{a.name}_out_ready"), 1)

                def round_(b, more):
                    for j in range(a.units):
                        weigh(b, j)
                        if more or j + 1 < a.units:
                            turn_probs(b, j + 1)
                        if more or j + 3 < a.units:
                            scores(b, j + 3)

                keys(0)
                scores(0, 0)
                keys(1)
                scores(0, 1)
                values()
                turn_probs(0, 0)
                keys(2)
                scores(0, 2)
                with pe.Fori(0, a.rounds - 1) as b:
                    round_(b, True)
                round_(a.rounds - 1, False)

            def out_project(a, weight, bias):
                name = a.name
                pe.wait_ge(sig(f"{name}_shifted"), a.rounds * a.units)
                for i in range(2):
                    mm(bank[:, 2 + i, :].rearrange("p (t c) -> p t c", t=FC), ones_row,
                       spread(row(bias), [1, FC, P], 1), start=True, stop=False)
                for t in range(T):
                    if t % FC == 0:
                        pe.wait_ge(sig(f"{name}_heads_done"), t // FC + 1)
                    ins = nc.tensor.transpose(bank[:, t // FC, (t % FC) * P:(t % FC + 1) * P], heads[:, 0, t, :], ident)
                    if t % FC == FC - 1:
                        ins.then_inc(sig(f"{name}_heads_turned"), 1)
                for i in range(2):
                    dst = bank[:, 2 + i, :]
                    pe.wait_ge(sig(f"{name}_headsT_ready"), i + 1)
                    for j in range(FC):
                        t = i * FC + j
                        ins = mm(dst[:, j * P:(j + 1) * P], headsT[:, t * P:(t + 1) * P], W(weight), start=False,
                                 stop=j == FC - 1)
                    ins.then_inc(sig(f"{name}_projected"), 1)

            def single_head(name, weight, key, width, values, rows_):
                turn(name)
                project_T(name, weight, 2, rows_=rows_)
                for t in range(T):
                    if t % FC == 0:
                        pe.wait_ge(sig(f"{name}_q_copied"), t // FC + 1)
                    b = t // TPB
                    ins = mm(bank[:, 0, t * SK:(t + 1) * SK], qT[0:rows_, 0, t * P:(t + 1) * P],
                             keyT[0:rows_, key, b * SK:(b + 1) * SK], start=True, stop=True)
                ins.then_inc(sig(f"{name}_scores_ready"), 1)
                pe.wait_ge(sig(f"{name}_exp_ready"), 1)
                for c in range(T // 2):
                    ins = nc.tensor.transpose(bank[:, 1, c * P:(c + 1) * P], prob[:, 0, c * P:(c + 1) * P], ident)
                ins.then_inc(sig(f"{name}_probs_turned"), 1)
                pe.wait_ge(sig(f"{name}_probT_ready"), 1)
                for t in range(T):
                    lo = SK * (t % 2)
                    at = t // 2 * width
                    ins = mm(bank[:, 6 + t % 2, at:at + width], probT[lo:lo + SK, 0, (t // 2) * P:(t // 2 + 1) * P],
                             values[lo:lo + SK, t // TPB, :], start=True, stop=True)
                ins.then_inc(sig(f"{name}_out_ready"), 1)

            def experts(m, gate, gate_bias):
                for t in range(T):
                    if t % FC == 0:
                        turned_half(m.name, t // FC)
                    dst = bank[:, 6, t * E:(t + 1) * E]
                    if gate_bias is not None:
                        mm(dst, ones_row, row(gate_bias), start=True, stop=False)
                    ins = mm(dst, xnT[:, t * P:(t + 1) * P], W(gate), start=gate_bias is None, stop=True)
                ins.then_inc(sig(f"{m.name}_logits_ready"), 1)
                splits = 2 * ("F0", "F2", "F3").index(m.name)
                pe.wait_ge(sig("x_split"), splits + 1)
                freed = "mult_ready" if m.gated else "act_ready"

                def product(dst, a_hi, a_lo, b_hi, b_lo):
                    mm(dst, a_hi, b_hi, start=True, stop=False)
                    mm(dst, a_hi, b_lo, start=False, stop=False)
                    return mm(dst, a_lo, b_hi, start=False, stop=True)

                def up(i, u, free=True):
                    g, f = divmod(u, FC)
                    late, g = divmod(g, ROUND)
                    slot = g // 2
                    if f == 0 and g % 2 == 0:
                        pe.wait_ge(sig(f"{m.name}_split"), i * RING + (late * RING + slot + 1))
                    if free:
                        pe.wait_ge(sig(f"{m.name}_{freed}"), i * (ROUND * FC) + max(u + 1 - m.banks, 1))
                    half = slice((g % 2) * HALF, (g % 2 + 1) * HALF)
                    at = [slice(k * FF + f * P, k * FF + (f + 1) * P) for k in range(2)]
                    if m.gated:
                        product(bank[:, 2 + f % 2, :], whi[:, slot, at[1]], wlo[:, slot, at[1]], xhi[:, half], xlo[:, half])
                    product(bank[:, f % m.banks, :], whi[:, slot, at[0]], wlo[:, slot, at[0]], xhi[:, half],
                            xlo[:, half]).then_inc(sig(f"{m.name}_up_ready"), 1)

                def down(i, g):
                    slot = g // 2
                    pe.wait_ge(sig(f"{m.name}_down{slot}_landed"), i * 16 + 16)
                    pe.wait_ge(sig(f"{m.name}_{freed}"), i * (ROUND * FC) + (g + 1) * FC)
                    pe.wait_ge(sig(f"{m.name}_acc_free"), i * ROUND + (g + 1))
                    for j in range(FC):
                        for f in range(FC):
                            tile = slice(j * P, (j + 1) * P)
                            ins = mm(bank[:, 4 + g % 2, tile], hid[:, g % 2, f, tile],
                                     wdown[:, slot, f * P:(f + 1) * P], start=f == 0, stop=f == FC - 1)
                    ins.then_inc(sig(f"{m.name}_down_ready"), 1)

                def round_(i, groups, more, after_first=lambda: None):
                    for g in range(groups):
                        for u in range(g * FC + 2, g * FC + 2 + FC):
                            if u < (groups + more) * FC:
                                up(i, u)
                        down(i, g)
                        if g == 0:
                            after_first()

                up(0, 0, free=False)
                up(0, 1, free=False)
                pe.wait_ge(sig("x_split"), splits + 2)
                with pe.Fori(0, m.rounds) as i:
                    round_(i, ROUND, 1)
                if not m.gated:
                    pe.wait_ge(sig(f"{m.name}_gates_set"), 1)
                    for t in range(T):
                        ins = mm(bank[0:E, 6 + t // FC, (t % FC) * P:(t % FC + 1) * P], gates[:, t, 0:E], ident,
                                 start=True, stop=True)
                    ins.then_inc(sig(f"{m.name}_gates_turned"), 1)

                def output_biases():
                    pe.wait_ge(sig(f"{m.name}_gatesT_ready"), 1)
                    pe.wait_ge(sig("down_bias_landed"), 16)
                    for t in range(T):
                        ins = mm(bank[:, 6 + t // FC, (t % FC) * P:(t % FC + 1) * P], gatesT[:, t * P:(t + 1) * P],
                                 down_bias[:, ("F2", "F3").index(m.name), :], start=True, stop=True)
                    ins.then_inc(sig(f"{m.name}_gated_bias_ready"), 1)

                round_(m.rounds, m.tail, 0, (lambda: None) if m.gated else output_biases)

            pe.wait_ge(sig("const_landed"), 16)
            pe.wait_ge(sig("ctx_landed"), 16)
            pe.wait_ge(sig("w_landed"), 16)
            pe.wait_ge(sig("rows_landed"), 16)
            ctx_keys = ctxT[:, :, 0, :]
            for name, bk, off, r in (("A0k1", 0, 0, P), ("A0k2", 0, 256, P), ("A3k", 1, 0, P), ("A2k", 1, 256, P),
                                     ("A1q", 2, 0, 64)):
                mm(bank[0:r, bk, off:off + B * SK].rearrange("p (b k) -> p b k", b=B), W(name), ctx_keys,
                   start=True, stop=True).then_inc(sig("keys_projected"), 1)
            for name, bk, bias, width in (("A0v", 3, None, P), ("A3v", 4, "A3bv", P), ("A2v", 5, "A2bv", P),
                                          ("A1q", 6, "A1bv", 64)):
                if bias is not None:
                    mm(bank[:, bk, 0:B * width].rearrange("p (b c) -> p b c", b=B), ones_row,
                       spread(row(bias), [1, B, width], 1), start=True, stop=False)
                for b in range(B):
                    ins = mm(bank[:, bk, b * width:(b + 1) * width], ctxT[:, b, :, :].rearrange("p r k -> p (r k)"),
                             W(name), start=bias is None, stop=bias is None or b == B - 1)
                ins.then_inc(sig("values_projected"), 1)
            at = ROWS["gx"][0]
            mm(bank[:, 7, 0:SCALARS], ones_row, rows[0:1, at:at + SCALARS], start=True, stop=True).then_inc(
                sig("scalars_spread"), 1)

            pe.wait_ge(sig("keys_copied"), 5)
            turn("A0")
            pe.wait_ge(sig("values_placed"), 1)
            project_T("A0", "A0q1", 2)
            project_T("A0", "A0q2", 4)

            def a0_keys(j):
                if j == 0:
                    pe.wait_ge(sig("A0m0_keys_spread"), B)
                if j == 1:
                    pe.wait_ge(sig("A0m1_keys_spread"), B)

            def b3_keys(j):
                if j < 2:
                    pe.wait_ge(sig("B3_first_keys_dve"), j + 1)
                else:
                    pe.wait_ge(sig("B3_first_keys_pool"), 2)

            attend(A0, a0_keys, lambda: None)
            out_project(A0, "A0o", "A0bo")
            pe.wait_ge(sig("magnitudes_ready"), 1)
            mm(bank[:, 7, 0:2], ones_sq, thr[:, 0:2], start=True, stop=True).then_inc(sig("magnitudes_summed"), 1)
            turn("F0")
            experts(F0, "F0g", None)
            single_head("A1", "A1q", 4, 64, v1, 64)
            for odd in range(2):
                mm(bank[:, 2 + odd, :].rearrange("p (t c) -> p t c", t=FC), ones_row,
                   spread(row("A1bo"), [1, FC, P], 1), start=True, stop=False)
            pe.wait_ge(sig("A1_heads_done"), 1)
            flat = heads[:, 0, :, :].rearrange("p t c -> p (t c)")
            for c in range(T // 2):
                ins = nc.tensor.transpose(bank[:, c // 2, (c % 2) * P:(c % 2 + 1) * P], flat[:, c * P:(c + 1) * P],
                                          ident)
                if c % 2:
                    ins.then_inc(sig("A1_heads_turned"), 1)
            pe.wait_ge(sig("A1_headsT_ready"), 2)
            for odd in range(2):
                dst = bank[:, 2 + odd, :]
                lo, o = 64 * odd, W_COLS["A1o"][0]
                for c in range(T // 2):
                    ins = mm(dst[:, c * P:(c + 1) * P], headsT[lo:lo + 64, c * P:(c + 1) * P],
                             w[lo:lo + 64, o:o + P], start=False, stop=c == T // 2 - 1)
                ins.then_inc(sig("A1_projected"), 1)
            turn("F1")
            pe.wait_ge(sig("f1_ternary"), 1)
            for t in range(T):
                if t % FC == 0:
                    turned_half("F1", t // FC)
                if t >= 2:
                    pe.wait_ge(sig("F1_act_ready"), t - 1)
                mm(bank[:, 2 + t % 2, :], xnT[:, t * P:(t + 1) * P], f1q[:, 0, :], start=True, stop=True).then_inc(
                    sig("F1_up_ready"), 1)

            def turn_hidden(t):
                pe.wait_ge(sig("F1_hid_normed"), t + 1)
                for f in range(FC):
                    ins = nc.tensor.transpose(bank[:, t % 2, f * P:(f + 1) * P],
                                              f1hid[:, t, f * P:(f + 1) * P], ident)
                ins.then_inc(sig("F1_hid_turned"), 1)

            turn_hidden(0)
            for t in range(T):
                if t + 1 < T:
                    turn_hidden(t + 1)
                pe.wait_ge(sig("F1_hidT_ready"), t + 1)
                for f in range(FC):
                    ins = mm(bank[:, 4 + t // FC, (t % FC) * P:(t % FC + 1) * P], prob[:, t % 2, f * P:(f + 1) * P],
                             f1q[:, 1, f * P:(f + 1) * P], start=f == 0, stop=f == FC - 1)
                ins.then_inc(sig("F1_down_ready"), 1)
            single_head("A2", "A2q", 3, P, v2, P)
            turn("F2")
            experts(F2, "F2g", "F2gb")
            turn("A3")
            project_T("A3", "A3q", 2)
            pe.wait_ge(sig("mask_ready"), 1)
            attend(A3, lambda j: pe.wait_ge(sig("A3_keys_spread"), B), lambda: None)
            out_project(A3, "A3o", "A3bo")
            turn("B3")
            project_T("B3", "F3k", 4, what="k")
            project_T("B3", "F3q", 2)
            for i in range(2):
                dst = bank[:, 6 + i, :]
                mm(dst.rearrange("p (t c) -> p t c", t=FC), ones_row, spread(row("F3bv"), [1, FC, P], 1),
                   start=True, stop=False)
                for j in range(FC):
                    t = i * FC + j
                    ins = mm(dst[:, j * P:(j + 1) * P], xnT[:, t * P:(t + 1) * P], W("F3v"), start=False,
                             stop=j == FC - 1)
            ins.then_inc(sig("B3_v_projected"), 1)
            attend(B3, b3_keys, lambda: pe.wait_ge(sig("B3_v_placed"), 2))
            out_project(B3, "F3o", "F3bo")
            turn("F3")
            experts(F3, "F3g", "F3gb")


def kernel(**inputs):
    import concourse.bacc as bacc
    from concourse.bass_utils import run_bass_kernel_spmd

    a = {k: np.asarray(v) for k, v in inputs.items()}
    f32 = np.float32

    square = {"A0q1": a["L0_xattn_q1_w"].T, "A0q2": a["L0_xattn_q2_w"].T, "A0k1": a["L0_xattn_kv1_w"][:P].T,
              "A0k2": a["L0_xattn_kv2_w"][:P].T, "A0v": a["L0_xattn_kv1_w"][P:].T, "A0o": a["L0_xattn_proj_w"].T,
              "A3k": a["L3_xattn_wk_w"].T, "A2k": a["L2_xattn_Wk"].T, "A3v": a["L3_xattn_wv_w"].T,
              "A2v": a["L2_xattn_Wv"].T, "A3q": a["L3_xattn_wq_w"].T, "A3o": a["L3_xattn_wo_w"].T,
              "A2q": a["L2_xattn_Wq"].T, "F3q": a["L3_ffn_wq"], "F3k": a["L3_ffn_wk"], "F3v": a["L3_ffn_wv"],
              "F3o": a["L3_ffn_wo"], "A1o": np.concatenate([a["L1_xattn_Wo"]] * 2, 0), "A1q": a["L1_xattn_Wq"],
              "F0g": a["L0_ffn_gate_W"].T, "F2g": a["L2_ffn_gate_w"], "F3g": a["L3_ffn_gate_w"]}
    w_pack = np.zeros((P, W_WIDTH), f32)
    for n, (o, c) in W_COLS.items():
        w_pack[:, o:o + c] = square[n]
    columns = {"A0norm": a["L0_xattn_norm_w"], "A2bq": a["L2_xattn_bq"], "A2bk": a["L2_xattn_bk"],
               "A3bq": a["L3_xattn_wq_b"], "A3bk": a["L3_xattn_wk_b"], "F3bq": a["L3_ffn_bq"], "F3bk": a["L3_ffn_bk"],
               "F3g1": a["L3_ffn_ln1_g"], "F3b1": a["L3_ffn_ln1_b"], "F3g2": a["L3_ffn_ln2_g"],
               "F3b2": a["L3_ffn_ln2_b"], "F1w": a["L1_ffn_ln_w"], "F1b": a["L1_ffn_ln_b"],
               "A1bq": np.concatenate([a["L1_xattn_bq"]] * 2)}
    cols_pack = np.zeros((P, COLS_WIDTH), f32)
    for n, (o, c) in COLS.items():
        cols_pack[:, o:o + c] = columns[n].reshape(c, P).T
    in_rows = {"A0bo": a["L0_xattn_proj_b"], "A1bo": a["L1_xattn_bo"], "A2bv": a["L2_xattn_bv"],
               "A3bv": a["L3_xattn_wv_b"], "A3bo": a["L3_xattn_wo_b"], "F3bv": a["L3_ffn_bv"], "F3bo": a["L3_ffn_bo"],
               "A1bv": a["L1_xattn_bq"], "F2gb": a["L2_ffn_gate_b"], "F3gb": a["L3_ffn_gate_b"], "gx": a["g_xattn"],
               "gf": a["g_ffn"], "lam1": a["L0_xattn_lambda_1"].reshape(-1), "lam2": a["L0_xattn_lambda_2"].reshape(-1)}
    rows_pack = np.zeros((1, ROWS_WIDTH), f32)
    for n, (o, c) in ROWS.items():
        rows_pack[0, o:o + c] = in_rows[n]

    def down_layout(m):
        return m.reshape(-1, FC, P, P).transpose(0, 2, 1, 3).reshape(-1, P, FF)

    shared = [a[f"L0_ffn_{n}_s"].transpose(1, 0, 2).reshape(1, P, FF) for n in ("w1", "w3")]
    moe0 = np.concatenate([
        np.concatenate([a["L0_ffn_w1_e"], a["L0_ffn_w3_e"], down_layout(a["L0_ffn_w2_e"])], 2),
        np.concatenate(shared + [down_layout(a["L0_ffn_w2_s"].reshape(1, FF, P))], 2)], 0)
    moe2, moe3 = (np.concatenate([a[f"{n}_w1"], a[f"{n}_b1"].reshape(E, FC, P).transpose(0, 2, 1),
                                  down_layout(a[f"{n}_w2"])], 2) for n in ("L2_ffn", "L3_ffn"))
    f1 = np.stack([a["L1_ffn_W_fc"].T, a["L1_ffn_W_proj"].T.reshape(FC, P, P).transpose(1, 0, 2).reshape(P, FF)], 1)

    const = np.zeros((P, C_WIDTH), f32)
    const[:, C_ID:C_ID + P] = np.eye(P, dtype=f32)
    const[:, C_ONES:C_ONES + P] = 1.0
    const[:, C_HEAD:C_HEAD + H] = np.repeat(np.eye(H, dtype=f32), DH, 0)
    const[:, C_IOTA:C_IOTA + E] = np.arange(E, dtype=f32)

    ctx_t = a["ctx_1024"].transpose(2, 0, 1)
    arrays = {
        "x": a["x"].reshape(T, P, P).transpose(1, 0, 2),
        "ctx": np.stack([ctx_t, ctx_t], 2),
        "w": w_pack, "cols": cols_pack, "rows": rows_pack, "const": const,
        "mask": a["mask_1x1xSxS2_bf1"].reshape(TPB, P, SK).transpose(1, 0, 2).view(np.uint8),
        "f1": f1, "moe0": moe0, "moe2": moe2, "moe3": moe3,
        "down_bias": np.stack([a["L2_ffn_b2"], a["L3_ffn_b2"]], 1),
    }
    nc = bacc.Bacc("TRN2", target_bir_lowering=False, num_devices=1)
    feed, args = {}, []
    for name, arr in arrays.items():
        arr = np.ascontiguousarray(arr)
        feed[f"in_{name}"] = arr
        args.append(nc.dram_tensor(f"in_{name}", arr.shape, mybir.dt.from_np(arr.dtype), kind="ExternalInput").ap())
    args.append(nc.dram_tensor("out", (P, T, P), F32, kind="ExternalOutput").ap())
    build(nc, *args)
    r = run_bass_kernel_spmd(nc, [feed], core_ids=[0])
    return r.results[0]["out"].transpose(1, 0, 2).reshape(B, S, P)
```

```python
from contextlib import ExitStack

import numpy as np

import concourse.bass as bass
from concourse import mybir

ALU = mybir.AluOpType
ACT = mybir.ActivationFunctionType
AX = mybir.AxisListType
F32 = mybir.dt.float32
F32R = mybir.dt.float32r
BF16 = mybir.dt.bfloat16
U32 = mybir.dt.uint32
U8 = mybir.dt.uint8

P = 128
B, S, SK = 4, 256, 64
T = B * S // P
TPB = S // P
N = B * S
HALF = N // 2
H, DH = 16, 8
VW = DH + 1
E = 8
FF = 512
FC = FF // P
UNIT = 1024
BANK = 512
RING = 2
ROUND = 2 * RING
LN_EPS = 1e-5
RMS_EPS = 1e-6
ABSMEAN_EPS = 1e-6
MASKED = -1e30

SQUARE = ["A0q1", "A0q2", "A0k1", "A0k2", "A0v", "A0o", "A3k", "A2k", "A3v", "A2v", "A3q", "A3o", "A2q",
          "F3q", "F3k", "F3v", "F3o"]
W_COLS = {n: (P * i, P) for i, n in enumerate(SQUARE)}
_at = P * len(SQUARE)
for _n, _w in (("A1o", P), ("A1q", 64), ("F0g", E), ("F2g", E), ("F3g", E)):
    W_COLS[_n] = (_at, _w)
    _at += _w
W_WIDTH = _at
W_FIRST = 6 * P
LATER = {"A3": ("A3k", 2, "A3bk", "A3v", "A3bv", P, P, 4), "A1": ("A1q", 4, "A1bq", "A1q", "A1bv", 64, 64, 6),
         "A2": ("A2k", 3, "A2bk", "A2v", "A2bv", P, P, 6)}
COLS = {}
_at = 0
for _n, _w in (("A0norm", 1), ("A1bq", 1), ("A2bq", 1), ("A2bk", 1), ("A3bq", 1), ("A3bk", 1), ("F3bq", 1),
               ("F3bk", 1), ("F3g1", 1), ("F3b1", 1), ("F3g2", 1), ("F3b2", 1), ("F1w", FC), ("F1b", FC)):
    COLS[_n] = (_at, _w)
    _at += _w
COLS_WIDTH = _at
ROWS = {}
_at = 0
for _n, _w in (("A0bo", P), ("A1bo", P), ("A2bv", P), ("A3bv", P), ("A3bo", P), ("F3bv", P), ("F3bo", P),
               ("A1bv", 64), ("F2gb", E), ("F3gb", E), ("gx", 4), ("gf", 4), ("lam1", H), ("lam2", H)):
    ROWS[_n] = (_at, _w)
    _at += _w
ROWS_WIDTH = _at
SCALARS = 8 + 2 * H
C_ID, C_ONES, C_HEAD, C_IOTA = 0, P, 2 * P, 2 * P + H
C_WIDTH = 2 * P + H + E
POWERS = ["A0", "A0rms", "F0", "A1", "F1", "F1h", "A2", "F2", "A3", "F3in", "B3", "F3"]
TURNED = ["A0", "F0", "A1", "F1", "A2", "F2", "A3", "B3", "F3"]
SINGLE = ["A1", "A2"]
LATE = 3 * 16


def build(nc, x_in, ctx_in, w_in, cols_in, rows_in, const_in, mask_in, f1_in, moe0_in, moe2_in, moe3_in, down_bias_in, out):
    with ExitStack() as ctx:
        def sb(name, shape, dt=F32):
            return ctx.enter_context(nc.sbuf_tensor(name, shape, dt))

        x = sb("x", [P, T, P])
        z = sb("z", [P, T, P])
        f1t = z[:].rearrange("p t c -> p (t c)").rearrange("p (i f) -> p i f", i=2)
        ctxT = sb("ctxT", [P, B, 2, SK])
        w = sb("w", [P, W_WIDTH])
        cols = sb("cols", [P, COLS_WIDTH])
        rows = sb("rows", [1, ROWS_WIDTH])
        const = sb("const", [P, C_WIDTH])
        ident_bf = sb("ident_bf", [P, P], BF16)
        mask_raw = sb("mask_raw", [P, TPB, SK], U8)
        mask_add = sb("mask_add", [P, TPB, SK], BF16)
        down_bias = sb("down_bias", [E, 2, P])
        wraw = sb("wraw", [P, RING, 2 * FF])
        whi = sb("whi", [P, RING, 2 * FF], F32R)
        wlo = sb("wlo", [P, RING, 2 * FF], F32R)
        wdown = sb("wdown", [P, RING, FF])
        up_bias = sb("up_bias", [P, RING, FC])
        xhi = sb("xhi", [P, N], F32R)
        xlo = sb("xlo", [P, N], F32R)
        keyT = sb("keyT", [P, 5, B * SK])
        with ExitStack() as outside:
            kblock, f1w, f1q, qT, xn, xnT = (outside.enter_context(nc.sbuf_tensor(name, shape, F32)) for name, shape in (
                ("kblock", [P, 8 * UNIT]),
                ("f1w", [P, 2, FF]),
                ("f1q", [P, 2, FF]),
                ("qT", [P, 2, N]),
                ("xn", [P, T, P]),
                ("xnT", [P, N])))
        kself = [sb(f"kself_{part}", [P, 8 * UNIT], F32R) for part in ("high", "low")]
        qself = sb("qself", [P, TPB, 2, P], F32R)
        kparts = sb("kparts", [P, 2, N], F32R)
        f1hid = kblock[:, 4 * UNIT:8 * UNIT].rearrange("p (t f) -> p t f", t=T)
        v0 = sb("v0", [P, B, H // 2, 2 * VW])
        v3 = sb("v3", [P, B, H // 2, 2 * VW])
        vself = sb("vself", [P, T, H, VW])
        v2 = sb("v2", [P, B, P])
        v1 = sb("v1", [P, B, 64])
        qslot = sb("qslot", [P, 4, P])
        prob = sb("prob", [P, 2, UNIT])
        probT = sb("probT", [P, 2, UNIT])
        heads = sb("heads", [P, 2, T, P])
        headsT = heads[:, 1, :, :].rearrange("p t c -> p (t c)")
        hid = kblock[:, 4 * UNIT:8 * UNIT].rearrange("p (g f k) -> p g f k", g=2, f=FC)
        silu = heads[:, 0, :, :].rearrange("p t c -> p (t c)").rearrange("p (f k) -> p f k", f=2)
        acc = prob[:, 0, :].rearrange("p (t c) -> p t c", t=T)
        stats = sb("stats", [P, T, 6])
        meanvar = sb("meanvar", [P, T, 2])
        var_eps = sb("var_eps", [P, T])
        rstd = sb("rstd", [P, T])
        minus_half = sb("minus_half", [P, T])
        rowmax = sb("rowmax", [P, 2, H])
        rsum = sb("rsum", [P, 2, H])
        scal = sb("scal", [P, SCALARS])
        tanh_g = sb("tanh_g", [P, 9])
        lam = sb("lam", [P, H])
        thr = sb("thr", [P, 6])
        logit = sb("logit", [P, T, E])
        gprob = sb("gprob", [P, T, E])
        top = sb("top", [P, T, 8])
        topi = sb("topi", [P, T, 8], U32)
        topf = sb("topf", [P, T, 8])
        pick = sb("pick", [P, 2, T, E])
        small = sb("small", [P, 4, T])
        gates = sb("gates", [P, T, E + 1])
        gatesT = probT[0:E, 0, :]
        bank = ctx.enter_context(nc.psum_tensor("bank", [P, 8, BANK], F32))

        ident = const[:, C_ID:C_ID + P]
        ones_row = const[0:1, C_ONES:C_ONES + P]
        ones_sq = const[:, C_ONES:C_ONES + P]
        head_of = const[:, C_HEAD:C_HEAD + H]
        iota = const[:, C_IOTA:C_IOTA + E]

        def W(name):
            o, n = W_COLS[name]
            return w[:, o:o + n]

        def col(name, i=0):
            o = COLS[name][0] + i
            return cols[:, o:o + 1]

        def row(name):
            o, n = ROWS[name]
            return rows[0:1, o:o + n]

        def banks(i, n=2):
            return bank[:, i:i + n, :].rearrange("p b c -> p (b c)")

        def spread(ap, shape, axis):
            return ap.unsqueeze(axis).broadcast_to(shape)

        made = {}

        def sig(name):
            if name not in made:
                made[name] = ctx.enter_context(nc.semaphore(name))
            return made[name]

        class Attn:
            def __init__(self, name, span, units, slots, maps, heads_per_unit, scale, ones_values):
                self.name, self.units, self.slots, self.maps = name, units, slots, maps
                self.span, self.rounds, self.tiles = span, B // span, span * TPB
                self.hpu, self.kpu = heads_per_unit, UNIT // heads_per_unit
                self.scale, self.values = scale, ones_values
                self.per_slot = units // slots

            def tile(self, j):
                return j * self.tiles // self.units

            def map(self, j):
                return j % self.maps

            def group(self, j):
                return j % (H // self.hpu)

            def key_at(self, r, j):
                if self.name == "A0":
                    return r * (self.span * UNIT) + self.map(j) * B * UNIT
                if self.name == "A3":
                    return r * (self.span * UNIT) + self.tile(j) // TPB * UNIT
                return (r & 1) * (4 * UNIT) + self.group(j) * UNIT

        A0 = Attn("A0", 1, 2 * TPB, 2 * TPB, 2, H, DH ** -0.5, v0)
        A3 = Attn("A3", 2, 2 * TPB, 2 * TPB, 1, H, DH ** -0.5, v3)
        B3 = Attn("B3", 1, 4 * TPB, TPB, 1, 4, DH ** -0.5, vself)

        class Moe:
            def __init__(self, name, experts, func, gated, before):
                self.name, self.experts, self.func, self.gated, self.before = name, experts, func, gated, before
                self.index = ("F0", "F2", "F3").index(name)
                self.width = 2 * FF if gated else FF
                self.raw = self.width + (0 if gated else FC)
                self.banks = 2 if gated else FC
                self.rounds = (experts - 1) // RING
                self.tail = 2 * (experts - self.rounds * RING)

        F0 = Moe("F0", E + 1, ACT.Silu, True, None)
        F2 = Moe("F2", E, ACT.Gelu, False, F0)
        F3 = Moe("F3", E, ACT.Relu, False, F2)

        def spread_group(engine, part, g, dst, token):
            shape = [P, B3.hpu, S]
            keys = kparts[:].rearrange("p i n -> p (i n)").bitcast(F32)[:, bass.ds(token + part * N, S)]
            return engine.tensor_tensor(
                kself[part][:, bass.ds(dst + g * UNIT, UNIT)].rearrange("p (h k) -> p h k", h=B3.hpu),
                spread(keys, shape, 1), spread(head_of[:, g * B3.hpu:(g + 1) * B3.hpu], shape, 2), ALU.mult)

        moe_dram = {"F0": moe0_in, "F2": moe2_in, "F3": moe3_in}

        block = ctx.enter_context(nc.Block())

        @block.sync
        def _(sp):
            sp.dma_start(const[:], const_in).then_inc(sig("const_landed"), 16)
            sp.dma_start(x[:], x_in).then_inc(sig("x_landed"), 16)
            sp.dma_start(f1w[:], f1_in).then_inc(sig("late_landed"), 16)
            sp.dma_start(mask_raw[:], mask_in).then_inc(sig("late_landed"), 16)
            sp.dma_start(down_bias[:], down_bias_in).then_inc(sig("late_landed"), 16)

            def load_expert(m, e, slot):
                sp.dma_start(wraw[:, slot, 0:m.raw], moe_dram[m.name][e, :, 0:m.raw]).then_inc(
                    sig(f"{m.name}_w{slot}_landed"), 16)

            def load_down(m, e, slot):
                sp.dma_start(wdown[:, slot, :], moe_dram[m.name][e, :, m.raw:m.raw + FF]).then_inc(
                    sig(f"{m.name}_down{slot}_landed"), 16)

            def stream_experts(m):
                if m.before is not None:
                    sp.wait_ge(sig(f"{m.before.name}_split"), m.before.experts)
                for r in range(RING):
                    load_expert(m, r, r)
                if m.before is not None:
                    sp.wait_ge(sig(f"{m.before.name}_down_ready"), 2 * m.before.experts)
                for r in range(RING):
                    load_down(m, r, r)
                with sp.Fori(1, m.rounds) as i:
                    for r in range(RING):
                        sp.wait_ge(sig(f"{m.name}_split"), (i - 1) * RING + (r + 1))
                        load_expert(m, bass.ds(i * RING + r, 1), r)
                        sp.wait_ge(sig(f"{m.name}_down_ready"), (i - 1) * ROUND + 2 * (r + 1))
                        load_down(m, bass.ds(i * RING + r, 1), r)
                for r in range(m.tail // 2):
                    sp.wait_ge(sig(f"{m.name}_split"), (m.rounds - 1) * RING + r + 1)
                    load_expert(m, m.rounds * RING + r, r)
                    sp.wait_ge(sig(f"{m.name}_down_ready"), (m.rounds - 1) * ROUND + 2 * (r + 1))
                    load_down(m, m.rounds * RING + r, r)

            stream_experts(F0)
            stream_experts(F2)
            stream_experts(F3)
            for h in range(2):
                tiles = slice(FC * h, FC * (h + 1))
                sp.wait_ge(sig("x_final"), h + 1)
                sp.dma_start(out[:, tiles, :], x[:, tiles, :]).then_inc(sig("out_written"), 16)
            sp.wait_ge(sig("out_written"), 32)

        @block.gpsimd
        def _(pool):
            def power(name):
                for h in range(2):
                    half = slice(FC * h, FC * (h + 1))
                    pool.wait_ge(sig("var_ready"), 2 * POWERS.index(name) + h + 1)
                    nc.gpsimd.tensor_tensor(rstd[:, half], var_eps[:, half], minus_half[:, half], ALU.pow).then_inc(
                        sig("rstd_ready"), 1)

            def block_keys(name, dst, src, width):
                nc.gpsimd.tensor_tensor(
                    kblock[:, bass.ds(dst, H * width)].rearrange("p (h k) -> p h k", h=H),
                    spread(src, [P, H, width], 1), spread(head_of, [P, H, width], 2), ALU.mult,
                ).then_inc(sig(f"{name}_keys_spread"), 1)

            def fill_slots(a, between):
                def fill(b, s):
                    j = s * a.per_slot
                    at = b * (a.tiles * P) + a.tile(j) * P
                    nc.gpsimd.tensor_copy(qslot[:, s, :], qT[:, a.map(j), bass.ds(at, P)]).then_inc(
                        sig(f"{a.name}_slot_filled"), 1)

                for s in range(a.slots):
                    pool.wait_ge(sig(f"{a.name}_q_copied"), a.map(s * a.per_slot) + 1)
                    fill(0, s)
                between()
                pool.wait_ge(sig(f"{a.name}_q_copied"), 2 * a.maps)
                with pool.Fori(1, a.rounds) as b:
                    for s in range(a.slots):
                        pool.wait_ge(sig(f"{a.name}_scores_ready"), (b - 1) * a.units + (s + 1) * a.per_slot)
                        fill(b, s)

            def split_expert(m, i, r):
                raw, hi = wraw[:, r, 0:m.width], whi[:, r, 0:m.width]
                pool.wait_ge(sig(f"{m.name}_w{r}_landed"), i * 16 + 16)
                ones = const[:, C_ONES:C_ONES + 1].broadcast_to([P, m.width])
                nc.gpsimd.tensor_tensor(hi, raw, ones, ALU.mult).then_inc(sig(f"{m.name}_hi"), 1)
                if not m.gated:
                    nc.gpsimd.tensor_copy(up_bias[:, r, :], wraw[:, r, m.width:m.width + FC])
                pool.wait_ge(sig(f"{m.name}_hi"), i * RING + (r + 1))
                nc.gpsimd.tensor_tensor(wlo[:, r, 0:m.width], raw, hi.bitcast(F32), ALU.subtract).then_inc(
                    sig(f"{m.name}_split"), 1)

            def split_first(m):
                if m.before is not None:
                    pool.wait_ge(sig(f"{m.before.name}_act_ready"), 2 * FC * m.before.experts)
                for r in range(RING):
                    split_expert(m, 0, r)

            def split_rest(m):
                with pool.Fori(1, m.rounds) as i:
                    for r in range(RING):
                        pool.wait_ge(sig(f"{m.name}_act_ready"), (i - 1) * (ROUND * FC) + 2 * FC * (r + 1))
                        split_expert(m, i, r)
                for r in range(m.tail // 2):
                    pool.wait_ge(sig(f"{m.name}_act_ready"), (m.rounds - 1) * (ROUND * FC) + 2 * FC * (r + 1))
                    split_expert(m, m.rounds, r)

            nc.gpsimd.memset(minus_half[:], -0.5).then_inc(sig("minus_half_set"), 1)
            pool.wait_ge(sig("minus_half_set"), 1)
            power("A0")
            pool.wait_ge(sig("const_landed"), 16)
            pool.wait_ge(sig("keys_copied"), 2)
            for b in range(B):
                block_keys("A0m1", (B + b) * UNIT, keyT[:, 1, b * SK:(b + 1) * SK], SK)
            fill_slots(A0, lambda: split_first(F0))
            power("A0rms")
            power("F0")
            pool.wait_ge(sig("thresholds_ready"), 1)
            for i in range(2):
                nc.gpsimd.tensor_scalar(f1t[:, i, :], f1w[:, i, :], thr[:, 4 + i:5 + i], None, ALU.is_lt)
                nc.gpsimd.tensor_scalar(f1q[:, i, :], f1w[:, i, :], thr[:, 2 + i:3 + i], None, ALU.is_gt).then_inc(
                    sig("f1_compared"), 1)
            pool.wait_ge(sig("f1_compared"), 2)
            nc.gpsimd.tensor_tensor(f1q[:], f1q[:], f1t, ALU.subtract).then_inc(sig("f1_ternary"), 1)
            split_rest(F0)
            power("A1")
            pool.wait_ge(sig("later_copied"), 1)
            pool.wait_ge(sig("A0_scores_ready"), A0.units * A0.rounds)
            for b in range(B):
                block_keys("A3", b * UNIT, keyT[:, 2, b * SK:(b + 1) * SK], SK)
            split_first(F2)
            power("F1")
            power("F1h")
            power("A2")
            power("F2")
            split_rest(F2)
            power("A3")
            fill_slots(A3, lambda: split_first(F3))
            power("F3in")
            power("B3")
            pool.wait_ge(sig("B3_high_ready"), 1)
            spread_group(nc.gpsimd, 0, 0, 0, 0)
            pool.wait_ge(sig("B3_low_ready"), 1)
            spread_group(nc.gpsimd, 1, 0, 0, 0).then_inc(sig("B3_first_keys_pool"), 1)
            pool.wait_ge(sig("B3_low_ready"), 2)

            def fill(b, s):
                for part, src in enumerate((xhi, xlo)):
                    ins = nc.gpsimd.tensor_copy(qself[:, s, part, :], src[:, bass.ds(b * S + s * P, P)])
                ins.then_inc(sig("B3_slot_filled"), 1)

            def spread_batch(dst, token):
                for g in range(4):
                    for part in range(2):
                        ins = spread_group(nc.gpsimd, part, g, dst, token)
                ins.then_inc(sig("B3_keys_spread"), 1)

            fill(0, 0)
            fill(0, 1)
            for g in range(2, 4):
                spread_group(nc.gpsimd, 0, g, 0, 0)
                spread_group(nc.gpsimd, 1, g, 0, 0).then_inc(sig("B3_first_keys_pool"), 1)
            pool.wait_ge(sig("B3_v_projected"), 1)
            spread_batch(H * S, S)
            pool.wait_ge(sig("B3_low_ready"), 4)
            with pool.Fori(1, B - 1) as b:
                pool.wait_ge(sig("B3_scores_ready"), (b - 1) * B3.units + B3.per_slot)
                fill(b, 0)
                pool.wait_ge(sig("B3_scores_ready"), b * B3.units)
                fill(b, 1)
                spread_batch(((b + 1) & 1) * (H * S), (b + 1) * S)
            pool.wait_ge(sig("B3_scores_ready"), (B - 2) * B3.units + B3.per_slot)
            fill(B - 1, 0)
            pool.wait_ge(sig("B3_scores_ready"), (B - 1) * B3.units)
            fill(B - 1, 1)
            power("F3")
            split_rest(F3)

        @block.scalar
        def _(act):
            act.dma_start(ctxT[:], ctx_in).then_inc(sig("ctx_landed"), 16)
            act.dma_start(w[:, 0:W_FIRST], w_in[:, 0:W_FIRST]).then_inc(sig("A0_w_landed"), 16)
            act.dma_start(rows[:], rows_in).then_inc(sig("rows_landed"), 16)
            act.dma_start(cols[:], cols_in).then_inc(sig("cols_landed"), 16)
            act.dma_start(w[:, W_FIRST:W_WIDTH], w_in[:, W_FIRST:W_WIDTH]).then_inc(sig("w_landed"), 16)

            def copy(dst, src, bias=None, scale=None):
                if bias is None and scale is None:
                    return nc.scalar.copy(dst, src)
                return nc.scalar.activation(dst, src, ACT.Identity, bias=0.0 if bias is None else bias,
                                            scale=1.0 if scale is None else scale)

            def take_transposed(name, gain=None, bias=None):
                act.wait_ge(sig("turned"), 2 * TURNED.index(name) + 1)
                copy(xnT[:, 0:HALF], bank[:, 0, :], bias, gain).then_inc(sig("xnT0_ready"), 1)
                if name in ("F0", "F2", "F3"):
                    copy(xhi[:, 0:HALF], bank[:, 0, :], bias, gain).then_inc(sig("xhi_ready"), 1)

            def take_queries(name, bias, rows_=P):
                for i in range(2):
                    act.wait_ge(sig(f"{name}_q_projected"), i + 1)
                    copy(qT[0:rows_, 0, i * HALF:(i + 1) * HALF], bank[0:rows_, 2 + i, :], bias).then_inc(
                        sig(f"{name}_q_copied"), 1)

            def attend(a):
                def exps(b, j):
                    act.wait_ge(sig(f"{a.name}_shifted"), b * a.units + (j + 1))
                    nc.scalar.activation(prob[:, j % 2, :], prob[:, j % 2, :], ACT.Exp, scale=a.scale).then_inc(
                        sig(f"{a.name}_exp_ready"), 1)

                def take(b, j):
                    act.wait_ge(sig(f"{a.name}_probs_turned"), b * a.units + (j + 1))
                    nc.scalar.copy(probT[:, j % 2, :], banks(4)).then_inc(sig(f"{a.name}_probT_ready"), 1)

                def round_(b, more):
                    for j in range(a.units):
                        take(b, j)
                        if more or j + 1 < a.units:
                            exps(b, j + 1)

                exps(0, 0)
                with act.Fori(0, a.rounds - 1) as b:
                    round_(b, True)
                round_(a.rounds - 1, False)

            def take_heads(name, scale=None):
                for i in range(2):
                    act.wait_ge(sig(f"{name}_heads_turned"), i + 1)
                    copy(headsT[:, i * HALF:(i + 1) * HALF], bank[:, i, :], None, scale).then_inc(
                        sig(f"{name}_headsT_ready"), 1)

            def single_head(name, m_rows, bias, scale):
                take_transposed(name)
                take_queries(name, bias[0:m_rows], rows_=m_rows)
                for h in range(2):
                    act.wait_ge(sig("single_shifted"), 2 * SINGLE.index(name) + h + 1)
                    pr = prob[:, 0, h * FC * SK:(h + 1) * FC * SK]
                    nc.scalar.activation(pr, pr, ACT.Exp, scale=scale).then_inc(sig("single_exp_ready"), 1)
                for h in range(2):
                    act.wait_ge(sig("single_probs_turned"), 2 * SINGLE.index(name) + h + 1)
                    nc.scalar.copy(probT[:, 0, h * 2 * P:(h + 1) * 2 * P], bank[:, 4 + h, 0:2 * P]).then_inc(
                        sig("single_probT_ready"), 1)

            def experts(m):
                if m.name != "F3":
                    act.wait_ge(sig("router_shifted"), m.index + 1)
                    nc.scalar.activation(gprob[:], gprob[:], ACT.Exp).then_inc(sig("router_exp_ready"), 1)

                def unit(i, u):
                    g, f = divmod(u, FC)
                    act.wait_ge(sig(f"{m.name}_up_ready"), i * (ROUND * FC) + (u + 1))
                    dst = silu[:, f % 2, :] if m.gated else hid[:, g % 2, f, :]
                    bias = {} if m.gated else {"bias": up_bias[:, g // 2 % RING, f:f + 1]}
                    nc.scalar.activation(dst, bank[:, f % m.banks, :], m.func, **bias).then_inc(
                        sig(f"{m.name}_act_ready"), 1)

                with act.Fori(0, m.rounds) as i:
                    for u in range(ROUND * FC):
                        unit(i, u)
                unit(m.rounds, 0)
                unit(m.rounds, 1)
                if not m.gated:
                    act.wait_ge(sig(f"{m.name}_gates_turned"), 1)
                    nc.scalar.copy(gatesT, banks(6)[0:E, :]).then_inc(sig(f"{m.name}_gatesT_ready"), 1)
                for u in range(2, m.tail * FC):
                    unit(m.rounds, u)

            def copy_later(name):
                _, i, bias, _, _, width, r, bk = LATER[name]
                act.wait_ge(sig("later_projected"), list(LATER).index(name) + 1)
                copy(keyT[0:r, i, :], bank[0:r, bk, 0:B * SK], col(bias)[0:r])
                if name == "A3":
                    for half in range(2):
                        for b in range(B):
                            at = slice(64 * half, 64 * half + 64)
                            src = bank[at, bk + 1, b * P:(b + 1) * P].rearrange("p (h c) -> p h c", h=H)
                            ins = nc.scalar.copy(v3[at, b, :, half * VW:half * VW + DH], src[:, half::2, :])
                else:
                    ins = nc.scalar.copy({"A1": v1, "A2": v2}[name][:].rearrange("p b c -> p (b c)"),
                                         bank[:, bk + 1, 0:B * width])
                ins.then_inc(sig("later_copied"), 1)

            for i in range(2):
                act.wait_ge(sig("keys_projected"), 2)
                nc.scalar.copy(keyT[:, i, :], bank[:, 7, i * B * SK:(i + 1) * B * SK]).then_inc(sig("keys_copied"), 1)
            act.wait_ge(sig("cols_landed"), 16)
            act.wait_ge(sig("scalars_copied"), 1)
            nc.scalar.activation(tanh_g[:, 0:8], scal[:, 0:8], ACT.Tanh).then_inc(sig("gates_ready"), 1)

            take_transposed("A0")
            for i in range(2):
                for m in range(2):
                    act.wait_ge(sig("A0_q_projected"), 2 * i + m + 1)
                    nc.scalar.copy(qT[:, m, i * HALF:(i + 1) * HALF], bank[:, 2 + 2 * m + i, :]).then_inc(
                        sig("A0_q_copied"), 1)
            attend(A0)
            take_heads("A0", col("A0norm"))
            act.wait_ge(sig("mask_ready"), 1)
            copy_later("A3")
            take_transposed("F0")
            experts(F0)
            copy_later("A1")
            single_head("A1", 64, col("A1bq"), float(np.float32(1.0) / np.sqrt(np.float32(P))))
            for i in range(2):
                act.wait_ge(sig("A1_heads_turned"), i + 1)
                nc.scalar.copy(headsT[:, i * 256:(i + 1) * 256], bank[:, i, 0:256]).then_inc(
                    sig("A1_headsT_ready"), 1)
            take_transposed("F1")
            for t in range(T):
                act.wait_ge(sig("F1_up_ready"), t + 1)
                nc.scalar.activation(f1hid[:, t, :], bank[:, 2 + t % 2, :], ACT.Gelu).then_inc(
                    sig("F1_act_ready"), 1)
            for t in range(T):
                act.wait_ge(sig("F1_hid_turned"), t + 1)
                for f in range(FC):
                    at = slice(f * P, (f + 1) * P)
                    ins = copy(prob[:, t % 2, at], bank[:, t % 2, at], col("F1b", f), col("F1w", f))
                ins.then_inc(sig("F1_hidT_ready"), 1)
            copy_later("A2")
            single_head("A2", P, col("A2bq"), 1.0)
            take_transposed("F2")
            experts(F2)
            take_transposed("A3")
            take_queries("A3", col("A3bq"))
            attend(A3)
            take_heads("A3")
            take_transposed("B3", col("F3g1"), col("F3b1"))
            for half in range(2):
                at = slice(half * HALF, (half + 1) * HALF)
                act.wait_ge(sig("B3_k_projected"), half + 1)
                copy(kparts[:, 0, at], bank[:, 4 + half, :], col("F3bk")).then_inc(sig("B3_high_ready"), 1)
                act.wait_ge(sig("B3_q_projected"), half + 1)
                copy(xhi[:, at], bank[:, 2 + half, :], col("F3bq")).then_inc(sig("B3_high_ready"), 1)
            act.wait_ge(sig("B3_v_projected"), 1)
            for i in range(2):
                nc.scalar.copy(
                    vself[:, FC * i:FC * i + FC, :, 0:DH],
                    bank[:, 6 + i, :].rearrange("p (t h c) -> p t h c", t=FC, h=H)).then_inc(sig("B3_v_placed"), 1)
            attend(B3)
            take_heads("B3")
            take_transposed("F3", col("F3g2"), col("F3b2"))
            experts(F3)

        @block.vector
        def _(dve):
            fence = nc.vector.drain

            def variances(h):
                tiles = slice(FC * h, FC * (h + 1))
                nc.vector.tensor_scalar_add(var_eps[:, tiles], meanvar[:, tiles, 1], LN_EPS).then_inc(sig("var_ready"), 1)

            def normalise(name, src, dst, update=lambda h: None):
                for h in range(2):
                    update(h)
                    for t in range(FC * h, FC * (h + 1)):
                        nc.vector.bn_stats(stats[:, t, :], src[:, t, :])
                    fence()
                    for t in range(FC * h, FC * (h + 1)):
                        nc.vector.bn_aggr(meanvar[:, t, :], stats[:, t, :])
                    fence()
                    variances(h)
                for h in range(2):
                    dve.wait_ge(sig("rstd_ready"), 2 * POWERS.index(name) + h + 1)
                    for t in range(FC * h, FC * (h + 1)):
                        ins = nc.vector.tensor_scalar(dst[:, t, :], src[:, t, :], meanvar[:, t, 0:1], rstd[:, t:t + 1],
                                                      ALU.subtract, ALU.mult)
                    if name in TURNED:
                        ins.then_inc(sig("normed"), 1)

            def take_transposed(name, gain=None, bias=None):
                dve.wait_ge(sig("turned"), 2 * TURNED.index(name) + 2)
                if gain is None:
                    ins = nc.vector.tensor_copy(xnT[:, HALF:N], bank[:, 1, :])
                else:
                    ins = nc.vector.tensor_scalar(xnT[:, HALF:N], bank[:, 1, :], gain, bias, ALU.mult, ALU.add)
                ins.then_inc(sig("xnT1_ready"), 1)
                if name in ("F0", "F2", "F3"):
                    dve.wait_ge(sig("xhi_ready"), ("F0", "F2", "F3").index(name) + 1)
                    nc.vector.tensor_tensor(xlo[:, 0:HALF], xnT[:, 0:HALF], xhi[:, 0:HALF].bitcast(F32),
                                            ALU.subtract).then_inc(sig("x_split"), 1)
                    fence()
                    nc.vector.tensor_copy(xhi[:, HALF:N], xnT[:, HALF:N])
                    fence()
                    nc.vector.tensor_tensor(xlo[:, HALF:N], xnT[:, HALF:N], xhi[:, HALF:N].bitcast(F32),
                                            ALU.subtract).then_inc(sig("x_split"), 1)

            def attend(a):
                nc.vector.sem_inc(sig(f"{a.name}_out_free"), 2)

                def shift(b, j):
                    sc = banks(2 * (j % 2)).rearrange("p (h k) -> p h k", h=a.hpu)
                    dve.wait_ge(sig(f"{a.name}_scores_ready"), b * a.units + (j + 1))
                    nc.vector.reduce_max(rowmax[:, j % 2, 0:a.hpu], sc, AX.X)
                    fence()
                    nc.vector.tensor_tensor(prob[:, j % 2, :].rearrange("p (h k) -> p h k", h=a.hpu), sc,
                                            spread(rowmax[:, j % 2, 0:a.hpu], [P, a.hpu, a.kpu], 2),
                                            ALU.subtract).then_inc(sig(f"{a.name}_shifted"), 1)

                def take(b, j):
                    o = bank[:, 6 + j % 2, 0:a.hpu * VW].rearrange("p (h c) -> p h c", h=a.hpu)
                    dve.wait_ge(sig(f"{a.name}_out_ready"), b * a.units + (j + 1))
                    nc.vector.reciprocal(rsum[:, j % 2, 0:a.hpu], o[:, :, DH])
                    fence()
                    if a.map(j) == 1:
                        nc.vector.tensor_tensor(rsum[:, 1, :], rsum[:, 1, :], lam[:], ALU.mult)
                        fence()
                    width = a.hpu * DH
                    dst = heads[:, a.map(j), :, :].rearrange("p t c -> p (t c)")[
                        :, bass.ds(b * (a.tiles * P) + (a.tile(j) * P + a.group(j) % (P // width) * width), width)]
                    nc.vector.tensor_tensor(dst.rearrange("p (h c) -> p h c", h=a.hpu), o[:, :, 0:DH],
                                            spread(rsum[:, j % 2, 0:a.hpu], [P, a.hpu, DH], 2),
                                            ALU.mult).then_inc(sig(f"{a.name}_out_free"), 1)
                    if a.map(j) == 1:
                        fence()
                        at = bass.ds(b * (a.tiles * P) + a.tile(j) * P, P)
                        first, second = (heads[:, m, :, :].rearrange("p t c -> p (t c)")[:, at] for m in range(2))
                        nc.vector.tensor_tensor(first, first, second, ALU.subtract)
                        fence()
                        nc.vector.bn_stats(stats[:].rearrange("p t s -> p (t s)")[
                            :, bass.ds(b * (a.tiles * 6) + a.tile(j) * 6, 6)], first)

                def round_(b, more):
                    for j in range(a.units):
                        if more or j + 2 < a.units:
                            shift(b, j + 2)
                        take(b, j)

                shift(0, 0)
                shift(0, 1)
                with dve.Fori(0, a.rounds - 1) as b:
                    round_(b, True)
                round_(a.rounds - 1, False)

            def flat(a, h=None):
                a = a.rearrange("p t c -> p (t c)")
                return a if h is None else a[:, h * HALF:(h + 1) * HALF]

            def add_gated(gate, src, h, dst=x):
                nc.vector.scalar_tensor_tensor(flat(dst[:], h), src, gate, flat(dst[:], h), ALU.mult, ALU.add)
                fence()

            def single_head(name, width, values_dup):
                take_transposed(name)
                for h in range(2):
                    tiles = slice(FC * h, FC * (h + 1))
                    sc = bank[:, h, 0:FC * SK].rearrange("p (t k) -> p t k", t=FC)
                    pr = prob[:, 0, h * FC * SK:(h + 1) * FC * SK].rearrange("p (t k) -> p t k", t=FC)
                    dve.wait_ge(sig("single_scores_ready"), 2 * SINGLE.index(name) + h + 1)
                    nc.vector.reduce_max(rowmax[:, 0, tiles], sc, AX.X)
                    fence()
                    nc.vector.tensor_tensor(pr, sc, spread(rowmax[:, 0, tiles], [P, FC, SK], 2), ALU.subtract).then_inc(
                        sig("single_shifted"), 1)
                for h in range(2):
                    tiles = slice(FC * h, FC * (h + 1))
                    pr = prob[:, 0, h * FC * SK:(h + 1) * FC * SK].rearrange("p (t k) -> p t k", t=FC)
                    dve.wait_ge(sig("single_exp_ready"), 2 * SINGLE.index(name) + h + 1)
                    nc.vector.reduce_sum(rsum[:, 0, tiles], pr, AX.X)
                fence()
                nc.vector.reciprocal(rsum[:, 1, 0:T], rsum[:, 0, 0:T])
                fence()

            def single_output(name, h, width):
                dve.wait_ge(sig("single_out_ready"), 2 * SINGLE.index(name) + h + 1)
                dst = heads[:].rearrange("p m t c -> p (m t c)")[:, 0:T * width].rearrange("p (t c) -> p t c", t=T)
                for odd in range(2):
                    o = bank[:, (6, 2)[h] + odd, 0:2 * width].rearrange("p (t c) -> p t c", t=2)
                    tiles = slice(FC * h + odd, FC * (h + 1), 2)
                    ins = nc.vector.tensor_tensor(dst[:, tiles, :], o, spread(rsum[:, 1, tiles], [P, 2, width], 2), ALU.mult)
                return ins

            def route(m):
                lg = bank[:, 6, 0:T * E].rearrange("p (t e) -> p t e", t=T)
                wide = [P, T, E]
                dve.wait_ge(sig("router_logits_ready"), m.index + 1)
                if m.name == "F3":
                    nc.vector.tensor_copy(gprob[:], lg)
                    fence()
                else:
                    nc.vector.reduce_max(small[:, 0, :], lg, AX.X)
                    fence()
                    nc.vector.tensor_tensor(gprob[:], lg, spread(small[:, 0, :], wide, 2), ALU.subtract).then_inc(
                        sig("router_shifted"), 1)
                    dve.wait_ge(sig("router_exp_ready"), m.index + 1)
                    nc.vector.reduce_sum(small[:, 1, :], gprob[:], AX.X)
                    fence()
                    nc.vector.reciprocal(small[:, 2, :], small[:, 1, :])
                    fence()
                    nc.vector.tensor_tensor(gprob[:], gprob[:], spread(small[:, 2, :], wide, 2), ALU.mult)
                    fence()
                for t in range(T):
                    nc.vector.max(top[:, t, :], gprob[:, t, :])
                fence()
                for t in range(T):
                    nc.vector.max_index(topi[:, t, :], top[:, t, :], gprob[:, t, :])
                fence()
                nc.vector.tensor_copy(topf[:], topi[:])
                fence()
                iotas = spread(iota, wide, 1)
                if m.name == "F3":
                    nc.vector.tensor_tensor(gates[:, :, 0:E], iotas, topf[:, :, 0:1].broadcast_to(wide), ALU.is_equal)
                    fence()
                    return
                for k in range(2):
                    nc.vector.tensor_tensor(pick[:, k, :, :], iotas, topf[:, :, k:k + 1].broadcast_to(wide), ALU.is_equal)
                fence()
                nc.vector.tensor_tensor(pick[:, 0, :, :], pick[:, 0, :, :], pick[:, 1, :, :], ALU.add)
                fence()
                if m.name == "F2":
                    nc.vector.tensor_tensor(small[:, 0, :], top[:, :, 0], top[:, :, 1], ALU.add)
                    fence()
                    nc.vector.tensor_scalar_add(small[:, 1, :], small[:, 0, :], 1e-9)
                    fence()
                    nc.vector.reciprocal(small[:, 2, :], small[:, 1, :])
                    fence()
                    nc.vector.tensor_tensor(gprob[:], gprob[:], spread(small[:, 2, :], wide, 2), ALU.mult)
                    fence()
                nc.vector.tensor_tensor(gates[:, :, 0:E], gprob[:], pick[:, 0, :, :], ALU.mult)
                fence()

            def experts(m, between=lambda: None):
                nc.vector.memset(acc, 0.0)
                route(m)
                if not m.gated:
                    nc.vector.sem_inc(sig(f"{m.name}_gates_set"), 1)
                between()
                nc.vector.sem_inc(sig(f"{m.name}_acc_free"), 2)

                def mult(i, u):
                    g, f = divmod(u, FC)
                    dve.wait_ge(sig(f"{m.name}_act_ready"), i * (ROUND * FC) + (u + 1))
                    nc.vector.tensor_tensor(hid[:, g % 2, f, :], silu[:, f % 2, :], bank[:, 2 + f % 2, :],
                                            ALU.mult).then_inc(sig(f"{m.name}_mult_ready"), 1)

                def gather(i, g):
                    dve.wait_ge(sig(f"{m.name}_down_ready"), i * ROUND + (g + 1))
                    for j in range(FC):
                        t = g % 2 * FC + j
                        ins = nc.vector.scalar_tensor_tensor(
                            acc[:, t, :], bank[:, 4 + g % 2, j * P:(j + 1) * P],
                            gates[:, t, bass.ds(i * RING + g // 2, 1)], acc[:, t, :], ALU.mult, ALU.add)
                    ins.then_inc(sig(f"{m.name}_acc_free"), 1)
                    fence()

                def round_(i, groups, more, last=True):
                    for g in range(groups):
                        if m.gated:
                            for u in range(g * FC + 2, g * FC + 2 + FC):
                                if u < (groups + more) * FC:
                                    mult(i, u)
                        if last or g + 1 < groups:
                            gather(i, g)
                        if not last and g == 1 and not m.gated:
                            dve.wait_ge(sig(f"{m.name}_gated_bias_ready"), 1)
                            nc.vector.tensor_tensor(flat(acc), flat(acc), banks(6), ALU.add)
                            fence()

                if m.gated:
                    mult(0, 0)
                    mult(0, 1)
                with dve.Fori(0, m.rounds) as i:
                    round_(i, ROUND, 1)
                round_(m.rounds, m.tail, 0, last=False)

                def finish():
                    gather(m.rounds, m.tail - 1)

                return finish

            dve.wait_ge(sig("x_landed"), 16)
            normalise("A0", x, xn)
            nc.vector.memset(gates[:, :, E], 1.0 / E)
            nc.vector.memset(v0[:], 0.0)
            fence()
            for i in range(2):
                nc.vector.memset(v0[64 * i:64 * i + 64, :, :, i * VW + DH], 1.0)
            dve.wait_ge(sig("values_projected"), 1)
            for i in range(2):
                for b in range(B):
                    src = bank[64 * i:64 * i + 64, 6, b * P:(b + 1) * P].rearrange("p (h c) -> p h c", h=H)
                    nc.vector.tensor_copy(v0[64 * i:64 * i + 64, b, :, i * VW:i * VW + DH], src[:, i::2, :])
            fence()
            dve.wait_ge(sig("scalars_spread"), 1)
            nc.vector.tensor_copy(scal[:], bank[:, 5, 0:SCALARS]).then_inc(sig("scalars_copied"), 1)
            dve.wait_ge(sig("scalars_copied"), 1)
            nc.vector.tensor_tensor(lam[:], scal[:, 8:8 + H], scal[:, 8 + H:8 + 2 * H], ALU.subtract)
            fence()
            nc.vector.tensor_scalar_add(lam[:], lam[:], 0.1).then_inc(sig("values_placed"), 1)
            take_transposed("A0")
            dve.wait_ge(sig("keys_copied"), 1)
            for b in range(B):
                nc.vector.tensor_tensor(
                    kblock[:, b * UNIT:(b + 1) * UNIT].rearrange("p (h k) -> p h k", h=H),
                    spread(keyT[:, 0, b * SK:(b + 1) * SK], [P, H, SK], 1), spread(head_of, [P, H, SK], 2),
                    ALU.mult).then_inc(sig("A0m0_keys_spread"), 1)
            dve.wait_ge(sig("late_landed"), LATE)
            nc.vector.memset(vself[:, :, :, DH], 1.0)
            nc.vector.memset(v3[:], 0.0)
            fence()
            for i in range(2):
                nc.vector.memset(v3[64 * i:64 * i + 64, :, :, i * VW + DH], 1.0)
            fence()
            nc.vector.tensor_scalar(mask_add[:], mask_raw[:], 1.0, -MASKED, ALU.subtract, ALU.mult)
            nc.vector.tensor_copy(ident_bf[:], ident).then_inc(sig("mask_ready"), 1)
            attend(A0)
            fence()
            for h in range(2):
                for t in range(FC * h, FC * (h + 1)):
                    nc.vector.bn_aggr(meanvar[:, t, :], stats[:, t, :])
                fence()
                tiles = slice(FC * h, FC * (h + 1))
                nc.vector.tensor_tensor(small[:, 0, tiles], meanvar[:, tiles, 0], meanvar[:, tiles, 0], ALU.mult)
                fence()
                nc.vector.scalar_tensor_tensor(var_eps[:, tiles], small[:, 0, tiles], RMS_EPS, meanvar[:, tiles, 1], ALU.add,
                                               ALU.add).then_inc(sig("var_ready"), 1)
            for h in range(2):
                tiles = slice(FC * h, FC * (h + 1))
                dve.wait_ge(sig("rstd_ready"), 2 * POWERS.index("A0rms") + h + 1)
                nc.vector.tensor_tensor(heads[:, 0, tiles, :], heads[:, 0, tiles, :], spread(rstd[:, tiles], [P, FC, P], 2),
                                        ALU.mult).then_inc(sig("A0_heads_done"), 1)
            dve.wait_ge(sig("late_landed"), LATE)
            nc.vector.tensor_reduce(thr[:, 0:2], f1w[:], AX.X, ALU.add, apply_absolute_value=True).then_inc(
                sig("magnitudes_ready"), 1)
            dve.wait_ge(sig("gates_ready"), 1)
            nc.vector.tensor_scalar_mul(tanh_g[:, 8:9], tanh_g[:, 4:5], 0.5)

            def attended(name, gate):
                def update(h):
                    dve.wait_ge(sig(f"{name}_projected"), h + 1)
                    add_gated(gate, bank[:, 2 + h, :], h)
                return update

            def mixed(finish, gate):
                def update(h):
                    if h == 1:
                        finish()
                    add_gated(gate, flat(acc, h), h)
                return update

            normalise("F0", x, xn, attended("A0", tanh_g[:, 0:1]))
            dve.wait_ge(sig("magnitudes_summed"), 1)
            nc.vector.tensor_scalar(thr[:, 0:2], bank[:, 7, 0:2], 1.0 / (FF * P), ABSMEAN_EPS, ALU.mult, ALU.add)
            fence()
            nc.vector.tensor_scalar_mul(thr[:, 2:4], thr[:, 0:2], 0.5)
            nc.vector.tensor_scalar_mul(thr[:, 4:6], thr[:, 0:2], -0.5).then_inc(sig("thresholds_ready"), 1)
            take_transposed("F0")
            finish = experts(F0)
            normalise("A1", x, xn, mixed(finish, tanh_g[:, 8:9]))
            single_head("A1", 64, v1)
            for h in range(2):
                single_output("A1", h, 64).then_inc(sig("A1_heads_done"), 1)

            def a1_update(h):
                if h == 0:
                    dve.wait_ge(sig("A1_projected"), 2)
                for odd in range(2):
                    xs = x[:, FC * h + odd:FC * (h + 1):2, :]
                    src = bank[:, 4 + odd, h * 2 * P:(h + 1) * 2 * P].rearrange("p (t c) -> p t c", t=2)
                    nc.vector.scalar_tensor_tensor(xs, src, tanh_g[:, 1:2], xs, ALU.mult, ALU.add)
                fence()
            normalise("F1", x, xn, a1_update)
            take_transposed("F1")
            for h in range(2):
                for t in range(FC * h, FC * (h + 1)):
                    dve.wait_ge(sig("F1_act_ready"), t + 1)
                    nc.vector.bn_stats(stats[:, t, :], f1hid[:, t, :])
                fence()
                for t in range(FC * h, FC * (h + 1)):
                    nc.vector.bn_aggr(meanvar[:, t, :], stats[:, t, :])
                fence()
                variances(h)
            for t in range(T):
                if t % FC == 0:
                    dve.wait_ge(sig("rstd_ready"), 2 * POWERS.index("F1h") + t // FC + 1)
                hidden = f1hid[:, t, :]
                nc.vector.tensor_scalar(hidden, hidden, meanvar[:, t, 0:1], rstd[:, t:t + 1], ALU.subtract,
                                        ALU.mult).then_inc(sig("F1_hid_normed"), 1)

            def f1_update(h):
                dve.wait_ge(sig("F1_down_ready"), FC * (h + 1))
                add_gated(tanh_g[:, 5:6], bank[:, 4 + h, :], h)
            normalise("A2", x, xn, f1_update)
            single_head("A2", P, v2)

            def a2_update(h):
                single_output("A2", h, P)
                fence()
                add_gated(tanh_g[:, 2:3], flat(heads[:, 0, :, :], h), h)
            normalise("F2", x, xn, a2_update)
            take_transposed("F2")
            finish = experts(F2)
            normalise("A3", x, xn, mixed(finish, tanh_g[:, 6:7]))
            take_transposed("A3")
            attend(A3)
            nc.vector.drain().then_inc(sig("A3_heads_done"), 2)
            normalise("F3in", x, z, attended("A3", tanh_g[:, 3:4]))
            fence()
            normalise("B3", z, xn)
            take_transposed("B3", col("F3g1"), col("F3b1"))
            for half in range(2):
                at = slice(half * HALF, (half + 1) * HALF)
                for i, (low, high, src, bias) in enumerate((
                        (kparts[:, 1, at], kparts[:, 0, at], bank[:, 4 + half, :], "F3bk"),
                        (xlo[:, at], xhi[:, at], bank[:, 2 + half, :], "F3bq"))):
                    dve.wait_ge(sig("B3_high_ready"), 2 * half + i + 1)
                    nc.vector.scalar_tensor_tensor(low, src, col(bias), high.bitcast(F32), ALU.add,
                                                   ALU.subtract).then_inc(sig("B3_low_ready"), 1)
            fence()
            spread_group(nc.vector, 0, 1, 0, 0)
            spread_group(nc.vector, 1, 1, 0, 0).then_inc(sig("B3_first_keys_dve"), 1)
            attend(B3)
            nc.vector.drain().then_inc(sig("B3_heads_done"), 2)

            def b3_update(h):
                dve.wait_ge(sig("B3_projected"), h + 1)
                nc.vector.tensor_tensor(flat(z[:], h), flat(z[:], h), bank[:, 2 + h, :], ALU.add)
                fence()

            normalise("F3", z, xn, b3_update)
            take_transposed("F3", col("F3g2"), col("F3b2"))

            def add_stream():
                for h in range(2):
                    add_gated(tanh_g[:, 7:8], flat(z[:], h), h)

            final = mixed(experts(F3, add_stream), tanh_g[:, 7:8])
            for h in range(2):
                final(h)
                nc.vector.drain().then_inc(sig("x_final"), 1)
        @block.tensor
        def _(pe):
            mm = nc.tensor.matmul

            def product(dst, a_hi, a_lo, b_hi, b_lo):
                mm(dst, a_hi, b_hi, start=True, stop=False)
                mm(dst, a_hi, b_lo, start=False, stop=False)
                return mm(dst, a_lo, b_hi, start=False, stop=True)

            def turn(name):
                for t in range(T):
                    if t % FC == 0:
                        pe.wait_ge(sig("normed"), 2 * TURNED.index(name) + t // FC + 1)
                    ins = nc.tensor.transpose(bank[:, t // FC, (t % FC) * P:(t % FC + 1) * P], xn[:, t, :], ident)
                    if t % FC == FC - 1:
                        ins.then_inc(sig("turned"), 1)

            def turned_half(name, i):
                pe.wait_ge(sig(f"xnT{i}_ready"), TURNED.index(name) + 1)

            def project_queries(name, weight, rows_=P):
                for i in range(2):
                    turned_half(name, i)
                    mm(bank[0:rows_, 2 + i, :], W(weight), xnT[:, i * HALF:(i + 1) * HALF], start=True,
                       stop=True).then_inc(sig(f"{name}_q_projected"), 1)

            def attend(a, keys, values):
                def scores(b, j):
                    late, j = divmod(j, a.units)
                    if a is B3:
                        if late and j == 0:
                            pe.wait_ge(sig("B3_keys_spread"), b + 1)
                        if j % a.per_slot == 0:
                            pe.wait_ge(sig("B3_slot_filled"), (b + late) * a.slots + a.tile(j) + 1)
                        if not late and j == 3:
                            pe.wait_ge(sig("B3_first_keys_pool"), 3)
                        for c in range(2):
                            at = bass.ds(a.key_at(b + late, j) + c * BANK, BANK)
                            high, low = (qself[:, a.tile(j), part, :] for part in range(2))
                            ins = product(bank[:, 2 * (j % 2) + c, :], high, low, kself[0][:, at], kself[1][:, at])
                        ins.then_inc(sig("B3_scores_ready"), 1)
                        return
                    s = j // a.per_slot
                    if j % a.per_slot == 0:
                        pe.wait_ge(sig(f"{a.name}_slot_filled"), b * a.slots + (late * a.slots + s + 1))
                    for c in range(2):
                        at = a.key_at(b + late, j) + c * BANK
                        dst = bank[:, 2 * (j % 2) + c, :]
                        ins = mm(dst, qslot[:, s, :], kblock[:, bass.ds(at, BANK)], start=True, stop=a is not A3)
                        if a is A3:
                            ins = mm(dst.rearrange("p (h k) -> p h k", k=SK), ident_bf[:],
                                     spread(mask_add[:, a.tile(j) % TPB, :], [P, BANK // SK, SK], 1), start=False, stop=True)
                    ins.then_inc(sig(f"{a.name}_scores_ready"), 1)

                def turn_probs(b, j):
                    pe.wait_ge(sig(f"{a.name}_exp_ready"), b * a.units + (j + 1))
                    for c in range(UNIT // P):
                        ins = nc.tensor.transpose(bank[:, 4 + c // FC, (c % FC) * P:(c % FC + 1) * P],
                                                  prob[:, j % 2, c * P:(c + 1) * P], ident)
                    ins.then_inc(sig(f"{a.name}_probs_turned"), 1)

                def weigh(b, j):
                    pe.wait_ge(sig(f"{a.name}_probT_ready"), b * a.units + (j + 1))
                    pe.wait_ge(sig(f"{a.name}_out_free"), b * a.units + (j + 1))
                    if a is B3:
                        per = S // P
                        for h in range(a.hpu):
                            for k in range(per):
                                o = (h + a.group(j) * a.hpu) * VW
                                v = vself[:].rearrange("p t h c -> p (t h c)")[
                                    :, bass.ds(b * (per * H * VW) + (k * H * VW + o), VW)]
                                c = h * per + k
                                ins = mm(bank[:, 6 + j % 2, h * VW:(h + 1) * VW], probT[:, j % 2, c * P:(c + 1) * P], v,
                                         start=k == 0, stop=k == per - 1)
                    else:
                        flat = a.values[:].rearrange("p b h c -> p (b h c)")
                        for c in range(H // 2):
                            at = (a.tile(j) // TPB * (H // 2) + c) * 2 * VW
                            v = flat[:, bass.ds(b * (a.span * H * VW) + at, 2 * VW)]
                            ins = mm(bank[:, 6 + j % 2, c * 2 * VW:(c + 1) * 2 * VW], probT[:, j % 2, c * P:(c + 1) * P], v,
                                     start=True, stop=True)
                    ins.then_inc(sig(f"{a.name}_out_ready"), 1)

                def round_(b, more):
                    for j in range(a.units):
                        weigh(b, j)
                        if more or j + 1 < a.units:
                            turn_probs(b, j + 1)
                        if more or j + 3 < a.units:
                            scores(b, j + 3)

                keys(0)
                scores(0, 0)
                keys(1)
                if a is not B3:
                    pe.wait_ge(sig(f"{a.name}_q_copied"), 2 * a.maps)
                scores(0, 1)
                values()
                turn_probs(0, 0)
                keys(2)
                scores(0, 2)
                with pe.Fori(0, a.rounds - 1) as b:
                    round_(b, True)
                round_(a.rounds - 1, False)

            def out_project(a, weight, bias):
                name = a.name
                pe.wait_ge(sig(f"{name}_shifted"), a.rounds * a.units)
                for i in range(2):
                    mm(bank[:, 2 + i, :].rearrange("p (t c) -> p t c", t=FC), ones_row,
                       spread(row(bias), [1, FC, P], 1), start=True, stop=False)
                for t in range(T):
                    if t % FC == 0:
                        pe.wait_ge(sig(f"{name}_heads_done"), t // FC + 1)
                    ins = nc.tensor.transpose(bank[:, t // FC, (t % FC) * P:(t % FC + 1) * P], heads[:, 0, t, :], ident)
                    if t % FC == FC - 1:
                        ins.then_inc(sig(f"{name}_heads_turned"), 1)
                for i in range(2):
                    dst = bank[:, 2 + i, :]
                    pe.wait_ge(sig(f"{name}_headsT_ready"), i + 1)
                    for j in range(FC):
                        t = i * FC + j
                        ins = mm(dst[:, j * P:(j + 1) * P], headsT[:, t * P:(t + 1) * P], W(weight), start=False,
                                 stop=j == FC - 1)
                    ins.then_inc(sig(f"{name}_projected"), 1)

            def single_head(name, weight, key, width, values, rows_):
                turn(name)
                project_queries(name, weight, rows_)
                pe.wait_ge(sig("later_copied"), list(LATER).index(name) + 1)
                for t in range(T):
                    h, b = t // FC, t // TPB
                    if t % FC == 0:
                        pe.wait_ge(sig(f"{name}_q_copied"), h + 1)
                    ins = mm(bank[:, h, (t % FC) * SK:(t % FC + 1) * SK], qT[0:rows_, 0, t * P:(t + 1) * P],
                             keyT[0:rows_, key, b * SK:(b + 1) * SK], start=True, stop=True)
                    if t % FC == FC - 1:
                        ins.then_inc(sig("single_scores_ready"), 1)
                for h in range(2):
                    pe.wait_ge(sig("single_exp_ready"), 2 * SINGLE.index(name) + h + 1)
                    for c in range(2):
                        at = (2 * h + c) * P
                        ins = nc.tensor.transpose(bank[:, 4 + h, c * P:(c + 1) * P], prob[:, 0, at:at + P], ident)
                    ins.then_inc(sig("single_probs_turned"), 1)
                for t in range(T):
                    h = t // FC
                    if t % FC == 0:
                        pe.wait_ge(sig("single_probT_ready"), 2 * SINGLE.index(name) + h + 1)
                    lo = SK * (t % 2)
                    at = t // 2 % 2 * width
                    ins = mm(bank[:, (6, 2)[h] + t % 2, at:at + width], probT[lo:lo + SK, 0, (t // 2) * P:(t // 2 + 1) * P],
                             values[lo:lo + SK, t // TPB, :], start=True, stop=True)
                    if t % FC == FC - 1:
                        ins.then_inc(sig("single_out_ready"), 1)

            def experts(m, gate, gate_bias):
                if gate_bias is not None:
                    mm(bank[:, 6, 0:T * E].rearrange("p (t e) -> p t e", t=T), ones_row,
                       spread(row(gate_bias), [1, T, E], 1), start=True, stop=False)
                for t in range(T):
                    if t % FC == 0:
                        turned_half(m.name, t // FC)
                    dst = bank[:, 6, t * E:(t + 1) * E]
                    ins = mm(dst, xnT[:, t * P:(t + 1) * P], W(gate), start=gate_bias is None,
                             stop=gate_bias is None or t == T - 1)
                ins.then_inc(sig("router_logits_ready"), 1)
                splits = 2 * m.index
                pe.wait_ge(sig("x_split"), splits + 1)
                freed = "mult_ready" if m.gated else "act_ready"

                def up(i, u, free=True):
                    g, f = divmod(u, FC)
                    late, g = divmod(g, ROUND)
                    slot = g // 2
                    if f == 0 and g % 2 == 0:
                        pe.wait_ge(sig(f"{m.name}_split"), i * RING + (late * RING + slot + 1))
                    if free:
                        pe.wait_ge(sig(f"{m.name}_{freed}"), i * (ROUND * FC) + max(u + 1 - m.banks, 1))
                    half = slice((g % 2) * HALF, (g % 2 + 1) * HALF)
                    at = [slice(k * FF + f * P, k * FF + (f + 1) * P) for k in range(2)]
                    if m.gated:
                        product(bank[:, 2 + f % 2, :], whi[:, slot, at[1]], wlo[:, slot, at[1]], xhi[:, half], xlo[:, half])
                    product(bank[:, f % m.banks, :], whi[:, slot, at[0]], wlo[:, slot, at[0]], xhi[:, half],
                            xlo[:, half]).then_inc(sig(f"{m.name}_up_ready"), 1)

                def down(i, g):
                    slot = g // 2
                    pe.wait_ge(sig(f"{m.name}_down{slot}_landed"), i * 16 + 16)
                    pe.wait_ge(sig(f"{m.name}_{freed}"), i * (ROUND * FC) + (g + 1) * FC)
                    pe.wait_ge(sig(f"{m.name}_acc_free"), i * ROUND + (g + 1))
                    for j in range(FC):
                        for f in range(FC):
                            tile = slice(j * P, (j + 1) * P)
                            ins = mm(bank[:, 4 + g % 2, tile], hid[:, g % 2, f, tile],
                                     wdown[:, slot, f * P:(f + 1) * P], start=f == 0, stop=f == FC - 1)
                    ins.then_inc(sig(f"{m.name}_down_ready"), 1)

                def round_(i, groups, more, after_first=lambda: None):
                    for g in range(groups):
                        for u in range(g * FC + 2, g * FC + 2 + FC):
                            if u < (groups + more) * FC:
                                up(i, u)
                        down(i, g)
                        if g == 0:
                            after_first()

                up(0, 0, free=False)
                up(0, 1, free=False)
                pe.wait_ge(sig("x_split"), splits + 2)
                with pe.Fori(0, m.rounds) as i:
                    round_(i, ROUND, 1)
                if not m.gated:
                    pe.wait_ge(sig(f"{m.name}_gates_set"), 1)
                    for t in range(T):
                        ins = mm(bank[0:E, 6 + t // FC, (t % FC) * P:(t % FC + 1) * P], gates[:, t, 0:E], ident,
                                 start=True, stop=True)
                    ins.then_inc(sig(f"{m.name}_gates_turned"), 1)

                def output_biases():
                    pe.wait_ge(sig(f"{m.name}_gatesT_ready"), 1)
                    pe.wait_ge(sig("late_landed"), LATE)
                    for t in range(T):
                        ins = mm(bank[:, 6 + t // FC, (t % FC) * P:(t % FC + 1) * P], gatesT[:, t * P:(t + 1) * P],
                                 down_bias[:, ("F2", "F3").index(m.name), :], start=True, stop=True)
                    ins.then_inc(sig(f"{m.name}_gated_bias_ready"), 1)

                round_(m.rounds, m.tail, 0, (lambda: None) if m.gated else output_biases)

            pe.wait_ge(sig("const_landed"), 16)
            pe.wait_ge(sig("ctx_landed"), 16)
            pe.wait_ge(sig("A0_w_landed"), 16)
            ctx_keys = ctxT[:, :, 0, :]

            def context_keys(dst, weight):
                return mm(dst.rearrange("p (b k) -> p b k", b=B), W(weight), ctx_keys, start=True, stop=True)

            def context_values(bk, weight, bias, width):
                if bias is not None:
                    mm(bank[:, bk, 0:B * width].rearrange("p (b c) -> p b c", b=B), ones_row,
                       spread(row(bias), [1, B, width], 1), start=True, stop=False)
                for b in range(B):
                    ins = mm(bank[:, bk, b * width:(b + 1) * width], ctxT[:, b, :, :].rearrange("p r k -> p (r k)"),
                             W(weight), start=bias is None, stop=bias is None or b == B - 1)
                return ins

            def project_later(name):
                key_weight, _, _, value_weight, value_bias, width, r, bk = LATER[name]
                context_keys(bank[0:r, bk, 0:B * SK], key_weight)
                context_values(bk + 1, value_weight, value_bias, width).then_inc(sig("later_projected"), 1)

            for i in range(2):
                context_keys(bank[:, 7, i * B * SK:(i + 1) * B * SK], ("A0k1", "A0k2")[i]).then_inc(sig("keys_projected"), 1)
            context_values(6, "A0v", None, P).then_inc(sig("values_projected"), 1)
            pe.wait_ge(sig("rows_landed"), 16)
            at = ROWS["gx"][0]
            mm(bank[:, 5, 0:SCALARS], ones_row, rows[0:1, at:at + SCALARS], start=True, stop=True).then_inc(
                sig("scalars_spread"), 1)

            turn("A0")
            for i in range(2):
                turned_half("A0", i)
                for m in range(2):
                    if i == 1 and m == 1:
                        pe.wait_ge(sig("scalars_copied"), 1)
                    mm(bank[:, 2 + 2 * m + i, :], W(("A0q1", "A0q2")[m]), xnT[:, i * HALF:(i + 1) * HALF], start=True,
                       stop=True).then_inc(sig("A0_q_projected"), 1)

            def a0_keys(j):
                if j == 0:
                    pe.wait_ge(sig("A0m0_keys_spread"), B)
                if j == 1:
                    pe.wait_ge(sig("A0m1_keys_spread"), B)

            def b3_keys(j):
                if j == 1:
                    pe.wait_ge(sig("B3_first_keys_dve"), 1)
                else:
                    pe.wait_ge(sig("B3_first_keys_pool"), j // 2 + 1)

            attend(A0, a0_keys, lambda: pe.wait_ge(sig("values_placed"), 1))
            out_project(A0, "A0o", "A0bo")
            pe.wait_ge(sig("magnitudes_ready"), 1)
            mm(bank[:, 7, 0:2], ones_sq, thr[:, 0:2], start=True, stop=True).then_inc(sig("magnitudes_summed"), 1)
            pe.wait_ge(sig("w_landed"), 16)
            project_later("A3")
            turn("F0")
            pe.wait_ge(sig("later_copied"), 1)
            experts(F0, "F0g", None)
            project_later("A1")
            single_head("A1", "A1q", 4, 64, v1, 64)
            for odd in range(2):
                mm(bank[:, 4 + odd, :].rearrange("p (t c) -> p t c", t=FC), ones_row,
                   spread(row("A1bo"), [1, FC, P], 1), start=True, stop=False)
            flat = heads[:, 0, :, :].rearrange("p t c -> p (t c)")
            for c in range(T // 2):
                if c % 2 == 0:
                    pe.wait_ge(sig("A1_heads_done"), c // 2 + 1)
                ins = nc.tensor.transpose(bank[:, c // 2, (c % 2) * P:(c % 2 + 1) * P], flat[:, c * P:(c + 1) * P],
                                          ident)
                if c % 2:
                    ins.then_inc(sig("A1_heads_turned"), 1)
            pe.wait_ge(sig("A1_headsT_ready"), 2)
            for odd in range(2):
                dst = bank[:, 4 + odd, :]
                lo, o = 64 * odd, W_COLS["A1o"][0]
                for c in range(T // 2):
                    ins = mm(dst[:, c * P:(c + 1) * P], headsT[lo:lo + 64, c * P:(c + 1) * P],
                             w[lo:lo + 64, o:o + P], start=False, stop=c == T // 2 - 1)
                ins.then_inc(sig("A1_projected"), 1)
            turn("F1")
            pe.wait_ge(sig("f1_ternary"), 1)
            for t in range(T):
                if t % FC == 0:
                    turned_half("F1", t // FC)
                if t >= 2:
                    pe.wait_ge(sig("F1_act_ready"), t - 1)
                mm(bank[:, 2 + t % 2, :], xnT[:, t * P:(t + 1) * P], f1q[:, 0, :], start=True, stop=True).then_inc(
                    sig("F1_up_ready"), 1)

            def turn_hidden(t):
                pe.wait_ge(sig("F1_hid_normed"), t + 1)
                for f in range(FC):
                    ins = nc.tensor.transpose(bank[:, t % 2, f * P:(f + 1) * P],
                                              f1hid[:, t, f * P:(f + 1) * P], ident)
                ins.then_inc(sig("F1_hid_turned"), 1)

            turn_hidden(0)
            for t in range(T):
                if t + 1 < T:
                    turn_hidden(t + 1)
                pe.wait_ge(sig("F1_hidT_ready"), t + 1)
                for f in range(FC):
                    ins = mm(bank[:, 4 + t // FC, (t % FC) * P:(t % FC + 1) * P], prob[:, t % 2, f * P:(f + 1) * P],
                             f1q[:, 1, f * P:(f + 1) * P], start=f == 0, stop=f == FC - 1)
                ins.then_inc(sig("F1_down_ready"), 1)
            project_later("A2")
            single_head("A2", "A2q", 3, P, v2, P)
            turn("F2")
            experts(F2, "F2g", "F2gb")
            turn("A3")
            project_queries("A3", "A3q")
            pe.wait_ge(sig("mask_ready"), 1)
            attend(A3, lambda j: pe.wait_ge(sig("A3_keys_spread"), B), lambda: None)
            out_project(A3, "A3o", "A3bo")
            for i in range(2):
                mm(bank[:, 6 + i, :].rearrange("p (t c) -> p t c", t=FC), ones_row,
                   spread(row("F3bv"), [1, FC, P], 1), start=True, stop=False)
            turn("B3")
            for half in range(2):
                turned_half("B3", half)
                for what, first_bank in (("k", 4), ("q", 2)):
                    mm(bank[:, first_bank + half, :], W("F3" + what), xnT[:, half * HALF:(half + 1) * HALF],
                       start=True, stop=True).then_inc(sig(f"B3_{what}_projected"), 1)
            for i in range(2):
                dst = bank[:, 6 + i, :]
                for j in range(FC):
                    t = i * FC + j
                    ins = mm(dst[:, j * P:(j + 1) * P], xnT[:, t * P:(t + 1) * P], W("F3v"), start=False,
                             stop=j == FC - 1)
            ins.then_inc(sig("B3_v_projected"), 1)
            attend(B3, b3_keys, lambda: pe.wait_ge(sig("B3_v_placed"), 2))
            out_project(B3, "F3o", "F3bo")
            turn("F3")
            experts(F3, "F3g", "F3gb")


def kernel(**inputs):
    import concourse.bacc as bacc
    from concourse.bass_utils import run_bass_kernel_spmd

    a = {k: np.asarray(v) for k, v in inputs.items()}
    f32 = np.float32

    square = {"A0q1": a["L0_xattn_q1_w"].T, "A0q2": a["L0_xattn_q2_w"].T, "A0k1": a["L0_xattn_kv1_w"][:P].T,
              "A0k2": a["L0_xattn_kv2_w"][:P].T, "A0v": a["L0_xattn_kv1_w"][P:].T, "A0o": a["L0_xattn_proj_w"].T,
              "A3k": a["L3_xattn_wk_w"].T, "A2k": a["L2_xattn_Wk"].T, "A3v": a["L3_xattn_wv_w"].T,
              "A2v": a["L2_xattn_Wv"].T, "A3q": a["L3_xattn_wq_w"].T, "A3o": a["L3_xattn_wo_w"].T,
              "A2q": a["L2_xattn_Wq"].T, "F3q": a["L3_ffn_wq"], "F3k": a["L3_ffn_wk"], "F3v": a["L3_ffn_wv"],
              "F3o": a["L3_ffn_wo"], "A1o": np.concatenate([a["L1_xattn_Wo"]] * 2, 0), "A1q": a["L1_xattn_Wq"],
              "F0g": a["L0_ffn_gate_W"].T, "F2g": a["L2_ffn_gate_w"], "F3g": a["L3_ffn_gate_w"]}
    w_pack = np.zeros((P, W_WIDTH), f32)
    for n, (o, c) in W_COLS.items():
        w_pack[:, o:o + c] = square[n]
    columns = {"A0norm": a["L0_xattn_norm_w"], "A2bq": a["L2_xattn_bq"], "A2bk": a["L2_xattn_bk"],
               "A3bq": a["L3_xattn_wq_b"], "A3bk": a["L3_xattn_wk_b"], "F3bq": a["L3_ffn_bq"], "F3bk": a["L3_ffn_bk"],
               "F3g1": a["L3_ffn_ln1_g"], "F3b1": a["L3_ffn_ln1_b"], "F3g2": a["L3_ffn_ln2_g"],
               "F3b2": a["L3_ffn_ln2_b"], "F1w": a["L1_ffn_ln_w"], "F1b": a["L1_ffn_ln_b"],
               "A1bq": np.concatenate([a["L1_xattn_bq"]] * 2)}
    cols_pack = np.zeros((P, COLS_WIDTH), f32)
    for n, (o, c) in COLS.items():
        cols_pack[:, o:o + c] = columns[n].reshape(c, P).T
    in_rows = {"A0bo": a["L0_xattn_proj_b"], "A1bo": a["L1_xattn_bo"], "A2bv": a["L2_xattn_bv"],
               "A3bv": a["L3_xattn_wv_b"], "A3bo": a["L3_xattn_wo_b"], "F3bv": a["L3_ffn_bv"], "F3bo": a["L3_ffn_bo"],
               "A1bv": a["L1_xattn_bq"], "F2gb": a["L2_ffn_gate_b"], "F3gb": a["L3_ffn_gate_b"], "gx": a["g_xattn"],
               "gf": a["g_ffn"], "lam1": a["L0_xattn_lambda_1"].reshape(-1), "lam2": a["L0_xattn_lambda_2"].reshape(-1)}
    rows_pack = np.zeros((1, ROWS_WIDTH), f32)
    for n, (o, c) in ROWS.items():
        rows_pack[0, o:o + c] = in_rows[n]

    def down_layout(m):
        return m.reshape(-1, FC, P, P).transpose(0, 2, 1, 3).reshape(-1, P, FF)

    shared = [a[f"L0_ffn_{n}_s"].transpose(1, 0, 2).reshape(1, P, FF) for n in ("w1", "w3")]
    moe0 = np.concatenate([
        np.concatenate([a["L0_ffn_w1_e"], a["L0_ffn_w3_e"], down_layout(a["L0_ffn_w2_e"])], 2),
        np.concatenate(shared + [down_layout(a["L0_ffn_w2_s"].reshape(1, FF, P))], 2)], 0)
    moe2, moe3 = (np.concatenate([a[f"{n}_w1"], a[f"{n}_b1"].reshape(E, FC, P).transpose(0, 2, 1),
                                  down_layout(a[f"{n}_w2"])], 2) for n in ("L2_ffn", "L3_ffn"))
    f1 = np.stack([a["L1_ffn_W_fc"].T, a["L1_ffn_W_proj"].T.reshape(FC, P, P).transpose(1, 0, 2).reshape(P, FF)], 1)

    const = np.zeros((P, C_WIDTH), f32)
    const[:, C_ID:C_ID + P] = np.eye(P, dtype=f32)
    const[:, C_ONES:C_ONES + P] = 1.0
    const[:, C_HEAD:C_HEAD + H] = np.repeat(np.eye(H, dtype=f32), DH, 0)
    const[:, C_IOTA:C_IOTA + E] = np.arange(E, dtype=f32)

    ctx_t = a["ctx_1024"].transpose(2, 0, 1)
    arrays = {
        "x": a["x"].reshape(T, P, P).transpose(1, 0, 2),
        "ctx": np.stack([ctx_t, ctx_t], 2),
        "w": w_pack, "cols": cols_pack, "rows": rows_pack, "const": const,
        "mask": a["mask_1x1xSxS2_bf1"].reshape(TPB, P, SK).transpose(1, 0, 2).view(np.uint8),
        "f1": f1, "moe0": moe0, "moe2": moe2, "moe3": moe3,
        "down_bias": np.stack([a["L2_ffn_b2"], a["L3_ffn_b2"]], 1),
    }
    nc = bacc.Bacc("TRN2", target_bir_lowering=False, num_devices=1)
    feed, args = {}, []
    for name, arr in arrays.items():
        arr = np.ascontiguousarray(arr)
        feed[f"in_{name}"] = arr
        args.append(nc.dram_tensor(f"in_{name}", arr.shape, mybir.dt.from_np(arr.dtype), kind="ExternalInput").ap())
    args.append(nc.dram_tensor("out", (P, T, P), F32, kind="ExternalOutput").ap())
    build(nc, *args)
    r = run_bass_kernel_spmd(nc, [feed], core_ids=[0])
    return r.results[0]["out"].transpose(1, 0, 2).reshape(B, S, P)
```
